# Optimizing a Trainium2 kernel written in Bass

```python
import numpy as np
import jax
import jax.numpy as jnp

def _softmax(x, axis=-1):
    return jax.nn.softmax(x, axis=axis)

def _gelu(x):
    return jax.nn.gelu(x, approximate=True)

def _silu(x):
    return jax.nn.silu(x)

def _sigmoid(x):
    return jax.nn.sigmoid(x)

def _layernorm(x, axis=-1, eps=1e-05):
    m = jnp.mean(x, axis=axis, keepdims=True)
    v = jnp.var(x, axis=axis, keepdims=True)
    return (x - m) / jnp.sqrt(v + eps)

def _scatter_add(tgt, idx, src, axis=0):
    return tgt.at[idx].add(src)

def _segment_sum(src, seg, n):
    return jax.ops.segment_sum(src, seg, n)
kernel_name = 'mk_prb_d4_jaxref_r8_74c107'

def setup_inputs(seed: int=0):
    np.random.seed(seed)
    _w = jnp.asarray

    def _L0_attn_setup():
        import jax, jax.numpy as jnp
        import numpy as np
        import math
        B, T, E, H = (2, 256, 128, 16)
        D = E // H
        THETA = 10000.0

        def _rope(x):
            d = x.shape[-1]
            t = x.shape[1]
            freqs = 1.0 / THETA ** (jnp.arange(0, d, 2, dtype=jnp.float32) / d)
            ang = jnp.arange(t, dtype=jnp.float32)[:, None] * freqs[None, :]
            cos = jnp.cos(ang)[None, :, None, :]
            sin = jnp.sin(ang)[None, :, None, :]
            xr = x[..., 0::2]
            xi = x[..., 1::2]
            o = jnp.stack([xr * cos - xi * sin, xr * sin + xi * cos], axis=-1)
            return o.reshape(x.shape)
        key = jax.random.key(seed)
        k1, k2, k3 = jax.random.split(key, 3)
        x = jax.random.normal(k1, (B, T, E), dtype=jnp.float32)
        W_qkv = jax.random.normal(k2, (3 * E, E), dtype=jnp.float32) * 0.02
        b_qkv = jax.random.normal(k3, (3 * E,), dtype=jnp.float32) * 0.02
        return {'x': x, 'W_qkv': W_qkv, 'b_qkv': b_qkv}
    _L0_attn_in = _L0_attn_setup()

    def _L0_ffn_setup():
        import jax, jax.numpy as jnp
        import numpy as np
        import math
        EMBED_DIM = 128
        FFN_DIM = 512
        N_EXPERTS = 8
        TOP_K = 2
        CAP_FACTOR = 1.25
        key = jax.random.key(seed)
        k0, k1, k2, k3 = jax.random.split(key, 4)
        B, S = (4, 256)
        x = jax.random.normal(k0, (B, S, EMBED_DIM), dtype=jnp.float32)
        Wr = jax.random.normal(k1, (EMBED_DIM, N_EXPERTS), dtype=jnp.float32) * 0.02
        W1 = jax.random.normal(k2, (N_EXPERTS, EMBED_DIM, FFN_DIM), dtype=jnp.float32) * 0.02
        W2 = jax.random.normal(k3, (N_EXPERTS, FFN_DIM, EMBED_DIM), dtype=jnp.float32) * 0.02
        return {'x': x, 'Wr': Wr, 'W1': W1, 'W2': W2}
    _L0_ffn_in = _L0_ffn_setup()

    def _L1_attn_setup():
        import jax, jax.numpy as jnp
        import numpy as np
        EPS_LAM = 1e-08
        LN_EPS = 1e-05

        def _linear_recurrence(lam, values):
            B, T, D = values.shape
            a = jnp.broadcast_to(lam[None, None, :], (B, T, D))

            def combine(e1, e2):
                a1, b1 = e1
                a2, b2 = e2
                return (a1 * a2, a2 * b1 + b2)
            _, h = jax.lax.associative_scan(combine, (a, values), axis=1)
            return h
        key = jax.random.key(seed)
        ks = jax.random.split(key, 8)
        B, T, D = (8, 1024, 128)
        x = jax.random.normal(ks[0], (B, T, D), dtype=jnp.float32)
        log_lambda_raw = jax.random.normal(ks[1], (D,), dtype=jnp.float32) * 0.5 - 1.0
        Wb = jax.random.normal(ks[2], (D, D), dtype=jnp.float32) / np.sqrt(D)
        bb = jnp.zeros((D,), dtype=jnp.float32)
        Wc = jax.random.normal(ks[3], (D, D), dtype=jnp.float32) / np.sqrt(D)
        bc = jnp.zeros((D,), dtype=jnp.float32)
        gamma = jnp.ones((D,), dtype=jnp.float32)
        beta = jnp.zeros((D,), dtype=jnp.float32)
        return {'x': x, 'log_lambda_raw': log_lambda_raw, 'Wb': Wb, 'bb': bb, 'Wc': Wc, 'bc': bc, 'gamma': gamma, 'beta': beta}
    _L1_attn_in = _L1_attn_setup()

    def _L1_ffn_setup():
        import jax, jax.numpy as jnp
        import numpy as np
        B, L, D = (2, 256, 128)
        E = 15
        H = D * 1
        K = 3
        T = 1.0
        key = jax.random.key(seed)
        ks = jax.random.split(key, 12)
        s = 0.02
        return {'x': jax.random.normal(ks[0], (B, L, D), dtype=jnp.float32), 'router_W': jax.random.normal(ks[1], (D, E), dtype=jnp.float32) * s, 'router_b': jnp.zeros((E,), dtype=jnp.float32), 'sW1': jax.random.normal(ks[2], (D, H), dtype=jnp.float32) * s, 'sb1': jnp.zeros((H,), dtype=jnp.float32), 'sW2': jax.random.normal(ks[3], (H, D), dtype=jnp.float32) * s, 'sb2': jnp.zeros((D,), dtype=jnp.float32), 'eW1': jax.random.normal(ks[4], (E, D, H), dtype=jnp.float32) * s, 'eb1': jnp.zeros((E, H), dtype=jnp.float32), 'eW2': jax.random.normal(ks[5], (E, H, D), dtype=jnp.float32) * s, 'eb2': jnp.zeros((E, D), dtype=jnp.float32)}
    _L1_ffn_in = _L1_ffn_setup()

    def _L2_attn_setup():
        import jax, jax.numpy as jnp
        import numpy as np
        D_MODEL = 128
        N_HEADS = 16
        HEAD_DIM = D_MODEL // N_HEADS

        def _rope(x):
            B = x.shape[0]
            half = HEAD_DIM // 2
            theta = 1.0 / 10000.0 ** (jnp.arange(0, HEAD_DIM, 2, dtype=jnp.float32) / HEAD_DIM)
            pos = jnp.arange(B, dtype=jnp.float32)
            ang = pos[:, None] * theta[None, :]
            ang2 = jnp.concatenate([ang, ang], axis=-1)
            cos = jnp.cos(ang2)[:, None, None, :]
            sin = jnp.sin(ang2)[:, None, None, :]
            neg_half = jnp.concatenate([x[..., :half], -x[..., half:]], axis=-1)
            return x * cos + neg_half * sin
        key = jax.random.key(seed)
        k_x, k_q, k_k, k_v = jax.random.split(key, 4)
        B, S = (4, 256)
        scale = 1.0 / np.sqrt(D_MODEL)
        x = jax.random.normal(k_x, (B, S, D_MODEL), dtype=jnp.float32)
        Wq = jax.random.normal(k_q, (D_MODEL, D_MODEL), dtype=jnp.float32) * scale
        Wk = jax.random.normal(k_k, (D_MODEL, D_MODEL), dtype=jnp.float32) * scale
        Wv = jax.random.normal(k_v, (D_MODEL, D_MODEL), dtype=jnp.float32) * scale
        return {'x': x, 'Wq': Wq, 'Wk': Wk, 'Wv': Wv}
    _L2_attn_in = _L2_attn_setup()

    def _L2_ffn_setup():
        import jax, jax.numpy as jnp
        import numpy as np
        H, E, DFF = (128, 8, 512)
        key = jax.random.key(seed)
        ks = jax.random.split(key, 7)
        s = lambda *shape: 1.0 / np.sqrt(shape[-2] if len(shape) > 1 else shape[-1])
        x = jax.random.normal(ks[0], (2, 256, H), dtype=jnp.float32)
        Wr = jax.random.normal(ks[1], (H, E), dtype=jnp.float32) * (1.0 / np.sqrt(H))
        br = jnp.zeros((E,), dtype=jnp.float32)
        W1 = jax.random.normal(ks[2], (E, H, DFF), dtype=jnp.float32) * (1.0 / np.sqrt(H))
        b1 = jnp.zeros((E, DFF), dtype=jnp.float32)
        W2 = jax.random.normal(ks[3], (E, DFF, H), dtype=jnp.float32) * (1.0 / np.sqrt(DFF))
        b2 = jnp.zeros((E, H), dtype=jnp.float32)
        return {'x': x, 'Wr': Wr, 'br': br, 'W1': W1, 'b1': b1, 'W2': W2, 'b2': b2}
    _L2_ffn_in = _L2_ffn_setup()

    def _L3_attn_setup():
        import jax, jax.numpy as jnp
        import numpy as np
        N_HEADS = 16

        def _alibi_causal_mask(T, n_heads, dtype):
            slopes = (1.0 / jnp.power(2.0, jnp.arange(1, n_heads + 1, dtype=dtype)))[:, None, None]
            idx = jnp.arange(T)
            rel = (idx[None, :] - idx[:, None]).astype(dtype)
            alibi = jnp.tril(rel)
            causal = jnp.where(idx[None, :] > idx[:, None], -jnp.inf, 0.0).astype(dtype)
            return (alibi + causal)[None, :, :] * slopes
        key = jax.random.key(seed)
        ks = jax.random.split(key, 5)
        B, T, C = (2, 256, 128)
        scale = 0.02
        return {'x': jax.random.normal(ks[0], (B, T, C), dtype=jnp.float32), 'W_attn': jax.random.normal(ks[1], (C, 3 * C), dtype=jnp.float32) * scale, 'b_attn': jax.random.normal(ks[2], (3 * C,), dtype=jnp.float32) * scale, 'W_proj': jax.random.normal(ks[3], (C, C), dtype=jnp.float32) * scale, 'b_proj': jax.random.normal(ks[4], (C,), dtype=jnp.float32) * scale}
    _L3_attn_in = _L3_attn_setup()

    def _L3_ffn_setup():
        import jax, jax.numpy as jnp
        import numpy as np
        DIM = 128
        HIDDEN = 384
        SCALE = 1.0 / 127.0

        def _dequant(w_int, dtype):
            return w_int.astype(dtype) * jnp.asarray(SCALE, dtype)
        key = jax.random.key(seed)
        k_x, k_g, k_u, k_d = jax.random.split(key, 4)
        x = jax.random.normal(k_x, (4, 256, DIM), dtype=jnp.float32)
        w_gate = jax.random.randint(k_g, (HIDDEN, DIM), -127, 128, dtype=jnp.int32)
        w_up = jax.random.randint(k_u, (HIDDEN, DIM), -127, 128, dtype=jnp.int32)
        w_down = jax.random.randint(k_d, (DIM, HIDDEN), -127, 128, dtype=jnp.int32)
        return {'x': x, 'w_gate': w_gate, 'w_up': w_up, 'w_down': w_down}
    _L3_ffn_in = _L3_ffn_setup()
    _d = {'L0_attn_x': _L0_attn_in['x'], 'L0_attn_W_qkv': _L0_attn_in['W_qkv'], 'L0_attn_b_qkv': _L0_attn_in['b_qkv'], 'L0_ffn_Wr': _L0_ffn_in['Wr'], 'L0_ffn_W1': _L0_ffn_in['W1'], 'L0_ffn_W2': _L0_ffn_in['W2'], 'L1_attn_log_lambda_raw': _L1_attn_in['log_lambda_raw'], 'L1_attn_Wb': _L1_attn_in['Wb'], 'L1_attn_bb': _L1_attn_in['bb'], 'L1_attn_Wc': _L1_attn_in['Wc'], 'L1_attn_bc': _L1_attn_in['bc'], 'L1_attn_gamma': _L1_attn_in['gamma'], 'L1_attn_beta': _L1_attn_in['beta'], 'L1_ffn_router_W': _L1_ffn_in['router_W'], 'L1_ffn_router_b': _L1_ffn_in['router_b'], 'L1_ffn_sW1': _L1_ffn_in['sW1'], 'L1_ffn_sb1': _L1_ffn_in['sb1'], 'L1_ffn_sW2': _L1_ffn_in['sW2'], 'L1_ffn_sb2': _L1_ffn_in['sb2'], 'L1_ffn_eW1': _L1_ffn_in['eW1'], 'L1_ffn_eb1': _L1_ffn_in['eb1'], 'L1_ffn_eW2': _L1_ffn_in['eW2'], 'L1_ffn_eb2': _L1_ffn_in['eb2'], 'L2_attn_Wq': _L2_attn_in['Wq'], 'L2_attn_Wk': _L2_attn_in['Wk'], 'L2_attn_Wv': _L2_attn_in['Wv'], 'L2_ffn_Wr': _L2_ffn_in['Wr'], 'L2_ffn_br': _L2_ffn_in['br'], 'L2_ffn_W1': _L2_ffn_in['W1'], 'L2_ffn_b1': _L2_ffn_in['b1'], 'L2_ffn_W2': _L2_ffn_in['W2'], 'L2_ffn_b2': _L2_ffn_in['b2'], 'L3_attn_W_attn': _L3_attn_in['W_attn'], 'L3_attn_b_attn': _L3_attn_in['b_attn'], 'L3_attn_W_proj': _L3_attn_in['W_proj'], 'L3_attn_b_proj': _L3_attn_in['b_proj'], 'L3_ffn_w_gate': _L3_ffn_in['w_gate'], 'L3_ffn_w_up': _L3_ffn_in['w_up'], 'L3_ffn_w_down': _L3_ffn_in['w_down']}
    _x0 = _d['L0_attn_x']
    _d['L0_attn_x'] = jax.random.normal(jax.random.fold_in(jax.random.key(seed), 1), (16, 256, 128), dtype=_x0.dtype)
    del _x0
    return _d

def reference(L0_attn_x, L0_attn_W_qkv, L0_attn_b_qkv, L0_ffn_Wr, L0_ffn_W1, L0_ffn_W2, L1_attn_log_lambda_raw, L1_attn_Wb, L1_attn_bb, L1_attn_Wc, L1_attn_bc, L1_attn_gamma, L1_attn_beta, L1_ffn_router_W, L1_ffn_router_b, L1_ffn_sW1, L1_ffn_sb1, L1_ffn_sW2, L1_ffn_sb2, L1_ffn_eW1, L1_ffn_eb1, L1_ffn_eW2, L1_ffn_eb2, L2_attn_Wq, L2_attn_Wk, L2_attn_Wv, L2_ffn_Wr, L2_ffn_br, L2_ffn_W1, L2_ffn_b1, L2_ffn_W2, L2_ffn_b2, L3_attn_W_attn, L3_attn_b_attn, L3_attn_W_proj, L3_attn_b_proj, L3_ffn_w_gate, L3_ffn_w_up, L3_ffn_w_down):

    def _L0_attn_ref(x, W_qkv, b_qkv):
        import jax, jax.numpy as jnp
        import numpy as np
        import math
        B, T, E, H = (2, 256, 128, 16)
        D = E // H
        THETA = 10000.0

        def _rope(x):
            d = x.shape[-1]
            t = x.shape[1]
            freqs = 1.0 / THETA ** (jnp.arange(0, d, 2, dtype=jnp.float32) / d)
            ang = jnp.arange(t, dtype=jnp.float32)[:, None] * freqs[None, :]
            cos = jnp.cos(ang)[None, :, None, :]
            sin = jnp.sin(ang)[None, :, None, :]
            xr = x[..., 0::2]
            xi = x[..., 1::2]
            o = jnp.stack([xr * cos - xi * sin, xr * sin + xi * cos], axis=-1)
            return o.reshape(x.shape)
        b, t, _ = x.shape
        qkv = x @ W_qkv.T + b_qkv
        qkv = qkv.reshape(b, t, 3, H, D)
        q, k, v = (qkv[:, :, 0], qkv[:, :, 1], qkv[:, :, 2])
        q = _rope(q)
        k = _rope(k)
        q = q.transpose(0, 2, 1, 3)
        k = k.transpose(0, 2, 1, 3)
        v = v.transpose(0, 2, 1, 3)
        scores = jnp.einsum('bhqd,bhkd->bhqk', q, k) / math.sqrt(D)
        w = jax.nn.softmax(scores, axis=-1)
        out = jnp.einsum('bhqk,bhkd->bhqd', w, v)
        return out.transpose(0, 2, 1, 3).reshape(b, t, E)

    def _L0_ffn_ref(x, Wr, W1, W2):
        import jax, jax.numpy as jnp
        import numpy as np
        import math
        EMBED_DIM = 128
        FFN_DIM = 512
        N_EXPERTS = 8
        TOP_K = 2
        CAP_FACTOR = 1.25
        B, S, D = x.shape
        t = B * S
        xf = x.reshape(t, D)
        probs = jax.nn.softmax(xf.astype(jnp.float32) @ Wr, axis=-1)
        topk_probs, topk_experts = jax.lax.top_k(probs, TOP_K)
        cap = max(math.ceil(t * TOP_K * CAP_FACTOR / N_EXPERTS), 1)
        y = jnp.zeros_like(xf)
        for e in range(N_EXPERTS):
            mask = topk_experts == e
            gate = jnp.sum(jnp.where(mask, topk_probs, 0.0), axis=-1)
            has = jnp.any(mask, axis=-1)
            g_masked = jnp.where(has, gate, -jnp.inf)
            vals, idx = jax.lax.top_k(g_masked, cap)
            g = jnp.where(jnp.isfinite(vals), vals, 0.0)
            xe = xf[idx]
            h = jax.nn.relu(xe @ W1[e]) @ W2[e]
            y = y.at[idx].add(g[:, None] * h)
        return y.reshape(B, S, D)

    def _L1_attn_ref(x, log_lambda_raw, Wb, bb, Wc, bc, gamma, beta):
        import jax, jax.numpy as jnp
        import numpy as np
        EPS_LAM = 1e-08
        LN_EPS = 1e-05

        def _linear_recurrence(lam, values):
            B, T, D = values.shape
            a = jnp.broadcast_to(lam[None, None, :], (B, T, D))

            def combine(e1, e2):
                a1, b1 = e1
                a2, b2 = e2
                return (a1 * a2, a2 * b1 + b2)
            _, h = jax.lax.associative_scan(combine, (a, values), axis=1)
            return h
        lam = jax.nn.sigmoid(log_lambda_raw)
        x_b = jnp.einsum('btd,ed->bte', x, Wb) + bb
        values = (1.0 - lam) * x_b
        h_all = _linear_recurrence(lam, values)
        out = jnp.einsum('btd,ed->bte', h_all, Wc) + bc
        z = out + x
        mu = jnp.mean(z, axis=-1, keepdims=True)
        var = jnp.var(z, axis=-1, keepdims=True)
        z = (z - mu) / jnp.sqrt(var + LN_EPS) * gamma + beta
        return z

    def _L1_ffn_ref(x, router_W, router_b, sW1, sb1, sW2, sb2, eW1, eb1, eW2, eb2):
        import jax, jax.numpy as jnp
        import numpy as np
        B, L, D = (2, 256, 128)
        E = 15
        H = D * 1
        K = 3
        T = 1.0
        b, l, d = x.shape
        n = b * l
        xt = x.reshape(n, d)
        shared = jax.nn.relu(xt @ sW1 + sb1) @ sW2 + sb2
        logits = xt @ router_W + router_b
        probs = jax.nn.softmax(logits / T, axis=-1)
        top_p, top_i = jax.lax.top_k(probs, K)
        cw = jnp.zeros((n, E), dtype=probs.dtype)
        cw = cw.at[jnp.arange(n)[:, None], top_i].set(top_p)
        h = jax.nn.relu(jnp.einsum('nd,edh->neh', xt, eW1) + eb1)
        ye = jnp.einsum('neh,ehd->ned', h, eW2) + eb2
        routed = jnp.einsum('ned,ne->nd', ye, cw)
        return (shared + routed).reshape(b, l, d)

    def _L2_attn_ref(x, Wq, Wk, Wv):
        import jax, jax.numpy as jnp
        import numpy as np
        D_MODEL = 128
        N_HEADS = 16
        HEAD_DIM = D_MODEL // N_HEADS

        def _rope(x):
            B = x.shape[0]
            half = HEAD_DIM // 2
            theta = 1.0 / 10000.0 ** (jnp.arange(0, HEAD_DIM, 2, dtype=jnp.float32) / HEAD_DIM)
            pos = jnp.arange(B, dtype=jnp.float32)
            ang = pos[:, None] * theta[None, :]
            ang2 = jnp.concatenate([ang, ang], axis=-1)
            cos = jnp.cos(ang2)[:, None, None, :]
            sin = jnp.sin(ang2)[:, None, None, :]
            neg_half = jnp.concatenate([x[..., :half], -x[..., half:]], axis=-1)
            return x * cos + neg_half * sin
        B, S, D = x.shape
        q = (x @ Wq.T).reshape(B, S, N_HEADS, HEAD_DIM)
        k = (x @ Wk.T).reshape(B, S, N_HEADS, HEAD_DIM)
        v = (x @ Wv.T).reshape(B, S, N_HEADS, HEAD_DIM)
        q = _rope(q)
        k = _rope(k)
        q = q.transpose(0, 2, 1, 3)
        k = k.transpose(0, 2, 1, 3)
        v = v.transpose(0, 2, 1, 3)
        scores = jnp.einsum('bhqd,bhkd->bhqk', q, k) / np.sqrt(HEAD_DIM)
        weights = jax.nn.softmax(scores, axis=-1)
        out = jnp.einsum('bhqk,bhkd->bhqd', weights, v)
        return out.transpose(0, 2, 1, 3).reshape(B, S, D)

    def _L2_ffn_ref(x, Wr, br, W1, b1, W2, b2):
        import jax, jax.numpy as jnp
        import numpy as np
        H, E, DFF = (128, 8, 512)
        B, S, Hd = x.shape
        n_exp = W1.shape[0]
        xt = x.reshape(-1, Hd)
        logits = xt @ Wr + br
        probs = jax.nn.softmax(logits, axis=-1)
        gate = jnp.max(probs, axis=-1)
        idx = jnp.argmax(probs, axis=-1)
        h1 = jnp.maximum(jnp.einsum('th,ehf->etf', xt, W1) + b1[:, None, :], 0.0)
        ye = jnp.einsum('etf,efh->eth', h1, W2) + b2[:, None, :]
        onehot = jax.nn.one_hot(idx, n_exp, dtype=xt.dtype)
        y = jnp.einsum('te,eth->th', onehot, ye) * gate[:, None]
        return y.reshape(B, S, Hd)

    def _L3_attn_ref(x, W_attn, b_attn, W_proj, b_proj):
        import jax, jax.numpy as jnp
        import numpy as np
        N_HEADS = 16

        def _alibi_causal_mask(T, n_heads, dtype):
            slopes = (1.0 / jnp.power(2.0, jnp.arange(1, n_heads + 1, dtype=dtype)))[:, None, None]
            idx = jnp.arange(T)
            rel = (idx[None, :] - idx[:, None]).astype(dtype)
            alibi = jnp.tril(rel)
            causal = jnp.where(idx[None, :] > idx[:, None], -jnp.inf, 0.0).astype(dtype)
            return (alibi + causal)[None, :, :] * slopes
        B, T, C = x.shape
        H = N_HEADS
        D = C // H
        qkv = x @ W_attn + b_attn
        q, k, v = jnp.split(qkv, 3, axis=-1)
        q = q.reshape(B, T, H, D).transpose(0, 2, 1, 3)
        k = k.reshape(B, T, H, D).transpose(0, 2, 1, 3)
        v = v.reshape(B, T, H, D).transpose(0, 2, 1, 3)
        att = jnp.einsum('bhtd,bhsd->bhts', q, k) / jnp.sqrt(jnp.asarray(D, x.dtype))
        att = att + _alibi_causal_mask(T, H, x.dtype)[None]
        att = jax.nn.softmax(att, axis=-1)
        y = jnp.einsum('bhts,bhsd->bhtd', att, v)
        y = y.transpose(0, 2, 1, 3).reshape(B, T, C)
        return y @ W_proj + b_proj

    def _L3_ffn_ref(x, w_gate, w_up, w_down):
        import jax, jax.numpy as jnp
        import numpy as np
        DIM = 128
        HIDDEN = 384
        SCALE = 1.0 / 127.0

        def _dequant(w_int, dtype):
            return w_int.astype(dtype) * jnp.asarray(SCALE, dtype)
        wg = _dequant(w_gate, x.dtype)
        wu = _dequant(w_up, x.dtype)
        wd = _dequant(w_down, x.dtype)
        gate = jnp.einsum('bsd,hd->bsh', x, wg)
        up = jnp.einsum('bsd,hd->bsh', x, wu)
        h = jax.nn.silu(gate) * up
        return jnp.einsum('bsh,dh->bsd', h, wd)
    x = L0_attn_x
    xn = _layernorm(x, axis=-1)
    x = x + _L0_attn_ref(xn, L0_attn_W_qkv, L0_attn_b_qkv) + _L0_ffn_ref(xn, L0_ffn_Wr, L0_ffn_W1, L0_ffn_W2)
    xn = _layernorm(x, axis=-1)
    x = x + _L1_attn_ref(xn, L1_attn_log_lambda_raw, L1_attn_Wb, L1_attn_bb, L1_attn_Wc, L1_attn_bc, L1_attn_gamma, L1_attn_beta) + _L1_ffn_ref(xn, L1_ffn_router_W, L1_ffn_router_b, L1_ffn_sW1, L1_ffn_sb1, L1_ffn_sW2, L1_ffn_sb2, L1_ffn_eW1, L1_ffn_eb1, L1_ffn_eW2, L1_ffn_eb2)
    xn = _layernorm(x, axis=-1)
    x = x + _L2_attn_ref(xn, L2_attn_Wq, L2_attn_Wk, L2_attn_Wv) + _L2_ffn_ref(xn, L2_ffn_Wr, L2_ffn_br, L2_ffn_W1, L2_ffn_b1, L2_ffn_W2, L2_ffn_b2)
    xn = _layernorm(x, axis=-1)
    x = x + _L3_attn_ref(xn, L3_attn_W_attn, L3_attn_b_attn, L3_attn_W_proj, L3_attn_b_proj) + _L3_ffn_ref(xn, L3_ffn_w_gate, L3_ffn_w_up, L3_ffn_w_down)
    return x

_drawn_inputs = setup_inputs


def setup_inputs(seed=0):
    import zlib

    import numpy as np

    out = dict(_drawn_inputs(seed))
    spreads = {'L1_attn_bb': (0.0, 0.1),
     'L1_attn_bc': (0.0, 0.1),
     'L1_attn_gamma': (1.0, 0.2),
     'L1_attn_beta': (0.0, 0.1),
     'L1_ffn_router_b': (0.0, 0.52),
     'L1_ffn_sb1': (0.0, 0.417),
     'L1_ffn_sb2': (0.0, 0.1),
     'L1_ffn_eb1': (0.0, 0.8),
     'L1_ffn_eb2': (0.0, 0.446),
     'L2_ffn_br': (0.0, 0.1),
     'L2_ffn_b1': (0.0, 0.404),
     'L2_ffn_b2': (0.0, 0.277)}
    factors = {'L1_ffn_router_W': 3.914,
     'L1_ffn_eW1': 7.474,
     'L1_ffn_eW2': 6.903,
     'L3_attn_W_attn': 64.0,
     'L3_attn_b_attn': 64.0,
     'L3_attn_W_proj': 64.0,
     'L3_attn_b_proj': 64.0}
    for name, (base, spread) in spreads.items():
        noise = np.random.default_rng([zlib.crc32(name.encode()), seed]).standard_normal(out[name].shape)
        drawn = base * np.exp(spread * noise) if base else spread * noise
        out[name] = jnp.asarray(drawn.astype(out[name].dtype))
    for name, factor in factors.items():
        out[name] = (out[name] * factor).astype(out[name].dtype)
    return out
```

```python
from contextlib import ExitStack

import numpy as np

import concourse.bass as bass
from concourse import mybir

F32 = mybir.dt.float32
F16 = mybir.dt.float16
BF16 = mybir.dt.bfloat16
I32 = mybir.dt.int32
ALU = mybir.AluOpType
ACT = mybir.ActivationFunctionType
AX = mybir.AxisListType

P = 128
B = 16
T = 256
NT = B * T // P
H = 16
DH = P // H
NG = 4
NJ = H // NG
NPAIR = H // 2
CAP = 1280
EPS = 1e-5
PRIMED = 1
QSCALE = float(DH) ** -0.5
SEARCH_BITS = 30

SHARED_SIGNALS = ("bn", "aggr", "stats_kept", "stats", "rstd", "xn_ready", "turned", "xts_ready", "xt_copied",
                  "logits", "logits_copied", "shifted", "exp_logits", "gates", "counted", "summed")

EXPERTS = {0: 8, 1: 15, 2: 8}
TOPK = {0: 2, 1: 3, 2: 1}
FF = 512
NF = FF // P
HID = 384
NHC = HID // P


def feed_forward_plan(layer):
    if layer in (0, 2):
        nh, ny = 2 * EXPERTS[layer], EXPERTS[layer]
        need = [2 * m + 1 for m in range(ny)]
    elif layer == 1:
        nh = ny = 8
        need = list(range(ny))
    else:
        nh, ny = NHC, 1
        need = [NHC - 1]
    pieces, m = [], 0
    for k in range(nh):
        pieces.append(("H", k))
        if m < ny and k >= need[m] + 1:
            pieces.append(("Y", m))
            m += 1
    pieces += [("Y", mm) for mm in range(m, ny)]
    return pieces, nh, ny, need


def batch_steps(layer):
    if layer == 1:
        frame = [("G", 0), ("B", 0), ("R", 0), "F", "F", "F", ("Z", 0)] + ["F"] * 13 + [("N", 0)]
    else:
        frame = ([("G", 0), ("B", 0)] if layer == 2 else []) + [("P", 0), ("V", 0), "F", "F", "F"]
        frame += [("K", 0), ("K", 1), "F", ("K", 2), ("K", 3), "F"]
        for p in range(NPAIR):
            frame += [("S", p), "F"]
        frame += ["F", ("M", 0), "F"]
        for p in range(NPAIR):
            frame += [("T", p)] + (["F"] if p else []) + ([("O", p - 1)] if p else [])
        frame += ["F", ("O", NPAIR - 1), ("N", 0)]
    pieces = feed_forward_plan(layer)[0]
    steps, n = [], 0
    for s in frame:
        if s == "F":
            if n < len(pieces):
                steps.append(pieces[n])
                n += 1
        elif s[0] == "N":
            steps += pieces[n:] + [s]
        else:
            steps.append(s)
    return steps


def settle(eng, sem):
    eng.sem_inc(sem, 1)


class Chain:

    def __init__(self, eng, sem):
        self.eng, self.sem, self.base, self.n = eng, sem, 0, 0

    def enter(self, b):
        self.n, self.row = 0, b

    def mark(self, ins):
        ins.then_inc(self.sem, 1)
        self.n += 1
        return self.base + self.n

    def wait(self, mark):
        self.eng.wait_ge(self.sem, mark)

    def link(self, ins):
        self.wait(self.mark(ins))


class RowChain(Chain):

    def __init__(self, eng, sem, per):
        super().__init__(eng, sem)
        self.per = per

    def enter(self, row):
        self.base, self.n = row * self.per, 0

    def leave(self):
        assert self.n == self.per, f"per row {self.n}, not {self.per}"


def build(nc, d, out):
    ctx = ExitStack()
    with ctx:
        def sb(name, shape, dt=F32):
            return ctx.enter_context(nc.sbuf_tensor(name, shape, dt))

        def psum(name, shape):
            return ctx.enter_context(nc.psum_tensor(name, shape, F32))

        sems = {}

        def sem(name):
            if name not in sems:
                sems[name] = ctx.enter_context(nc.semaphore(name))
            return sems[name]

        X = sb("X", [P, NT, P])
        XT = sb("XT", [P, B * T])
        w1 = {0: sb("w1_02", [P, 8, FF]), 1: sb("w1_1", [P, 16, P])}
        w2 = {0: sb("w2_02", [P, 8, NF, P]), 1: sb("w2_1", [P, 16, P])}
        w1[2], w2[2] = w1[0], w2[0]
        b1 = {2: sb("b1_2", [P, 8, NF]), 1: sb("b1_1", [P, 16])}
        b2 = {2: sb("b2_2", [16, P]), 1: sb("b2_1", [16, P])}
        wr = {l: sb(f"wr_{l}", [P, EXPERTS[l]]) for l in EXPERTS}
        br = {1: sb("br_1", [P, 15]), 2: sb("br_2", [P, 8])}
        wq0 = sb("wq0", [P, 5, P])
        bq0 = sb("bq0", [P, 4])
        bv0 = sb("bv0", [P, P])
        rope0 = sb("rope0", [P, 4, T])
        wq2 = sb("wq2", [P, 3, P])
        rope2 = sb("rope2", [P, 2, B])
        wq3 = sb("wq3", [P, 3, P])
        bq3 = sb("bq3", [P, 2])
        bv3 = sb("bv3", [P, P])
        wp3 = sb("wp3", [P, P])
        bp3 = sb("bp3", [P, P])
        wi3 = sb("wi3", [P, 3, HID], I32)
        wf3 = sb("wf3", [P, 3, HID])
        wb1, wc1 = sb("wb1", [P, P]), sb("wc1", [P, P])
        bb1 = sb("bb1", [P, 1])
        bc1 = sb("bc1", [1, P])
        gam1, bet1 = sb("gam1", [P, P]), sb("bet1", [P, P])
        llr1 = sb("llr1", [P, 1])
        lamt = sb("lamt", [P, 1])
        oml = sb("oml", [P, 1])
        lam1 = sb("lam1", [P, 1])
        lamrow = sb("lamrow", [P, T])
        ident = sb("ident", [P, P])
        onesr = sb("onesr", [1, P])
        onesm = sb("onesm", [P, P])
        selq = sb("selq", [P, 4, NJ, P], F16)
        selm = sb("selm", [P, NJ, P], BF16)
        alcol = sb("alcol", [2, 2, NJ, P], F16)
        alrow = sb("alrow", [2, T], F16)
        maskb = sb("maskb", [P, 2, P], BF16)
        identb = sb("identb", [P, P], BF16)
        rank = sb("rank", [P, NT, 16])
        neghalf = sb("neghalf", [P, NT])
        tri = sb("tri", [P, P])

        st6 = sb("st6", [P, 4, 6])
        mv4 = sb("mv4", [P, 4, 2])
        MV = sb("MV", [P, NT, 2])
        vare = sb("vare", [P, NT])
        rstd = sb("rstd", [P, NT])
        xn = sb("xn", [P, 2, 4, P])
        xts = sb("xts", [P, 2, 4 * P])
        LG = sb("LG", [P, NT, 16])
        pr = sb("pr", [P, NT, 16])
        GA = sb("GA", [P, NT, 16])
        ra, rb, rc = (sb(n, [P, NT, 16]) for n in ("ra", "rb", "rc"))
        r1, r2 = sb("r1", [P, NT]), sb("r2", [P, NT])
        thr = sb("thr", [P, 8], I32)
        cand = sb("cand", [P, 8], I32)
        bitf = sb("bitf", [P, 8])
        biti = sb("biti", [P, 8], I32)
        addb = sb("addb", [P, 8], I32)
        cmp_ = sb("cmp_", [P, 8, NT])
        key = sb("key", [P, 8, NT])
        cnt = sb("cnt", [P, 8])
        left = sb("left", [P, 8])
        scan = sb("scan", [P, 8, NT])

        xtb = sb("xtb", [P, 2, T])
        gst = sb("gst", [P, 2, 2, 16])
        qkf = sb("qkf", [P, 2, 2 * T])
        qk16 = sb("qk16", [P, 2, 2 * T], F16)
        stk = sb("stk", [P, NJ, 2 * T], F16)
        mx = sb("mx", [P, 2, P])
        mt = sb("mt", [P, T], BF16)
        pT = sb("pT", [P, 2, 2, 2, T])
        va = sb("va", [P, 2, H, DH + 1])
        hb = sb("hb", [P, 4, 2 * T])
        gt = sb("gt", [16, T])
        rden = sb("rden", [P, 2, H])
        ob = sb("ob", [P, 2, P])
        oT = sb("oT", [P, T])
        th = sb("th", [P, 2, T])
        hg = sb("hg", [P, 2, T])
        vals = sb("vals", [P, T])
        hT = sb("hT", [P, T])
        zs = sb("zs", [P, 2, 6])
        zmv = sb("zmv", [P, 2, 2])
        zve, zr = sb("zve", [P, 2]), sb("zr", [P, 2])
        zn, zg = sb("zn", [P, 2, P]), sb("zg", [P, 2, P])

        pS = psum("pS", [P, 2, 512])
        pT_ = psum("pT_", [P, 2, 512])
        pH = psum("pH", [P, 2, 512])
        pY = psum("pY", [P, 512])
        pO = psum("pO", [P, 512])
        po = pO[:, 0:2 * H * (DH + 1)].rearrange("p (c h e) -> p c h e", c=2, h=H)

        xin = d["x"].rearrange("(t p) e -> p t e", p=P)
        xout = out.rearrange("b (c p) e -> p (b c) e", p=P)

        loads = {
            "ld_x": [(X[:, 0:16, :], xin[:, 0:16, :]), (X[:, 16:32, :], xin[:, 16:32, :])],
            "ld_cst": [(ident[:, :], d["c_ident"]), (onesr[:, :], d["c_ones"][0:1, :]), (onesm[:, :], d["c_ones"]),
                       (selq[:, :, :, :], d["c_selq"]), (selm[:, :, :], d["c_selm"]),
                       (alcol[:, :, :, :], d["c_alcol"]), (alrow[:, :], d["c_alrow"]),
                       (maskb[:, :, :], d["c_mask"]), (identb[:, :], d["c_identb"]), (rank[:, :, :], d["c_rank"]),
                       (neghalf[:, :], d["c_neghalf"]), (tri[:, :], d["c_tri"]), (rope0[:, :, :], d["c_rope0"]),
                       (rope2[:, :, :], d["c_rope2"]), (bitf[:, :], d["c_bitf"])],
            "ld_0": [(wr[0][:, :], d["wr0"]), (wq0[:, :, :], d["wq0"]), (bq0[:, :], d["bq0"]),
                     (bv0[:, :], d["bv0"].partition_broadcast(P)),
                     (w1[0][:, :, :], d["w1_0"]), (w2[0][:, :, :, :], d["w2_0"])],
            "ld_1": [(wr[1][:, :], d["wr1"]), (br[1][:, :], d["br1"].partition_broadcast(P)),
                     (w1[1][:, :, :], d["w1_1"]), (w2[1][:, :, :], d["w2_1"]), (b1[1][:, :], d["b1_1"]),
                     (b2[1][:, :], d["b2_1"]), (wb1[:, :], d["wb1"]), (wc1[:, :], d["wc1"]), (bb1[:, :], d["bb1"]),
                     (bc1[:, :], d["bc1"]), (gam1[:, :], d["gam1"].partition_broadcast(P)),
                     (bet1[:, :], d["bet1"].partition_broadcast(P)), (llr1[:, :], d["llr1"])],
            "ld_3": [(wq3[:, :, :], d["wq3"]), (bq3[:, :], d["bq3"]), (bv3[:, :], d["bv3"].partition_broadcast(P)),
                     (wp3[:, :], d["wp3"]), (bp3[:, :], d["bp3"].partition_broadcast(P)), (wi3[:, :, :], d["wi3"])],
            "ld_2": [(wr[2][:, :], d["wr2"]), (br[2][:, :], d["br2"].partition_broadcast(P)),
                     (wq2[:, :, :], d["wq2"]), (w1[2][:, :, :], d["w1_2"]), (w2[2][:, :, :, :], d["w2_2"]),
                     (b1[2][:, :, :], d["b1_2"]), (b2[2][0:8, :], d["b2_2"])],
        }
        full = {k: 16 * len(v) for k, v in loads.items()}

        plans = {l: feed_forward_plan(l) for l in range(4)}
        steps = {l: batch_steps(l) for l in range(4)}
        EXTRA_Y = {0: 0, 1: 2, 2: 2, 3: 0}

        def y_use(layer, m):
            return EXTRA_Y[layer] + m

        def y_uses(layer):
            return EXTRA_Y[layer] + plans[layer][2]

        def attn(layer):
            return layer != 1

        block = ctx.enter_context(nc.Block())

        @block.tensor
        def _(pe):
            pe.wait_ge(sem("ld_cst"), full["ld_cst"])

            def phase_a(l):
                s = lambda n: sem(f"L{l}_{n}")
                with pe.Fori(0, NT // 4 // 2) as turn:
                    i = turn * 2
                    for par in range(2):
                        pe.wait_ge(sem("xn_ready"), PRIMED + l * (NT // 4) + i + par + 1)
                        pe.wait_ge(sem("xts_ready"), PRIMED + l * (NT // 4) + i)
                        for u in range(4):
                            ins = pe.transpose(pS[:, par, u * P:(u + 1) * P], xn[:, par, u, :], ident[:, :])
                        ins.then_inc(sem("turned"), 1)
                    if l < 3:
                        for par in range(2):
                            pe.wait_ge(sem("xts_ready"), PRIMED + l * (NT // 4) + i + par + 1)
                            pe.wait_ge(sem("logits_copied"), PRIMED + l * (NT // 4) + i)
                            for u in range(4):
                                ins = pe.matmul(pT_[:, par, u * 16:u * 16 + EXPERTS[l]],
                                                xts[:, par, u * P:(u + 1) * P], wr[l][:, :], start=True, stop=True)
                            ins.then_inc(sem("logits"), 1)

            def search():
                with pe.Fori(0, SEARCH_BITS) as i:
                    pe.wait_ge(sem("counted"), PRIMED + i + 1)
                    pe.matmul(pT_[:, 0, 0:8], onesm[:, :], cnt[:, :], start=True, stop=True).then_inc(sem("summed"), 1)
                pe.wait_ge(sem("counted"), PRIMED + SEARCH_BITS + 1)
                pe.matmul(pT_[:, 0, 0:8], onesm[:, :], cnt[:, :], start=True, stop=True).then_inc(sem("summed"), 1)
                pe.wait_ge(sem("counted"), PRIMED + SEARCH_BITS + 2)
                pe.matmul(pS[:, 0, 0:8 * NT], tri[:, :], cmp_[:, :, :].rearrange("p e t -> p (e t)"),
                          start=True, stop=True)
                pe.matmul(pS[:, 1, 0:8 * NT], onesm[:, :], cmp_[:, :, :].rearrange("p e t -> p (e t)"),
                          start=True, stop=True).then_inc(sem("summed"), 1)

            def hidden(l, b, par, k, s):
                nh = plans[l][1]
                pe.wait_ge(s("h_act"), PRIMED + b * nh + max(0, k - 1))
                bank = pH[:, k % 2, :]
                for half in range(2):
                    if l == 3:
                        w = wf3[:, half, k * P:(k + 1) * P]
                    elif l == 1:
                        w = w1[1][:, 2 * k + half, :]
                    else:
                        f = 2 * (k % 2) + half
                        w = w1[l][:, k // 2, f * P:(f + 1) * P]
                    ins = pe.matmul(bank[:, half * T:(half + 1) * T], w, xtb[:, par, :], start=True, stop=True)
                ins.then_inc(s("h_ready"), 1)

            def project(l, b, m, s):
                nh, need = plans[l][1], plans[l][3]
                pe.wait_ge(s("h_act"), PRIMED + b * nh + need[m] + 1)
                pe.wait_ge(s("y_free"), PRIMED + b * y_uses(l) + y_use(l, m))
                if l == 1:
                    for half in range(2):
                        for c in range(2):
                            ins = pe.matmul(pY[:, half * T + c * P:half * T + (c + 1) * P],
                                            hb[:, m % 4, half * T + c * P:half * T + (c + 1) * P],
                                            w2[1][:, 2 * m + half, :], start=True, stop=True)
                else:
                    for c in range(2):
                        if l == 3:
                            parts = [(hb[:, f, c * P:(c + 1) * P], wf3[:, 2, f * P:(f + 1) * P]) for f in range(NHC)]
                        else:
                            parts = [(hb[:, (2 * m + f // 2) % 4, (f % 2) * T + c * P:(f % 2) * T + (c + 1) * P],
                                      w2[l][:, m, f, :]) for f in range(NF)]
                        for n, (lhs, rhs) in enumerate(parts):
                            ins = pe.matmul(pY[:, c * P:(c + 1) * P], lhs, rhs, start=(n == 0),
                                            stop=(n == len(parts) - 1))
                ins.then_inc(s("y_ready"), 1)

            def row(l, b, par):
                s = lambda n: sem(f"L{l}_{n}")
                pe.wait_ge(s("row_staged"), PRIMED + b + 1)
                for kind, k in steps[l]:
                    if kind == "H":
                        hidden(l, b, par, k, s)
                    elif kind == "Y":
                        project(l, b, k, s)
                    elif kind == "G":
                        pe.wait_ge(s("y_free"), PRIMED + b * y_uses(l))
                        for c in range(2):
                            ins = pe.transpose(pY[0:16, c * P:(c + 1) * P], gst[:, par, c, :], ident[:, :])
                        ins.then_inc(s("y_ready"), 1)
                    elif kind == "B":
                        pe.wait_ge(s("y_free"), PRIMED + b * y_uses(l) + 1)
                        n = 16 if l == 1 else 8
                        for c in range(2):
                            ins = pe.matmul(pY[:, c * P:(c + 1) * P], gt[0:n, c * P:(c + 1) * P], b2[l][0:n, :],
                                            start=True, stop=True)
                        ins.then_inc(s("y_ready"), 1)
                    elif kind == "R":
                        pe.wait_ge(s("x_final"), PRIMED + b)
                        pe.matmul(pS[:, 0, 0:T], wb1[:, :], xtb[:, par, :], start=True, stop=True)\
                          .then_inc(s("xb_ready"), 1)
                    elif kind == "Z":
                        pe.wait_ge(s("scanned"), PRIMED + b + 1)
                        for c in range(2):
                            o = pS[:, 1, c * P:(c + 1) * P]
                            pe.matmul(o, hT[:, c * P:(c + 1) * P], wc1[:, :], start=True, stop=False)
                            pe.matmul(o, xtb[:, par, c * P:(c + 1) * P], ident[:, :], start=False, stop=False)
                            ins = pe.matmul(o, onesr[:, :], bc1[:, :], start=False, stop=True)
                        ins.then_inc(s("z_ready"), 1)
                    elif kind == "P":
                        pe.wait_ge(s("x_final"), PRIMED + b)
                        order = {0: [0, 2, 1, 3], 2: [0, 1], 3: [0, 1]}[l]
                        w = {0: wq0, 2: wq2, 3: wq3}[l]
                        for n, which in enumerate(order):
                            ins = pe.matmul(pS[:, n // 2, (n % 2) * T:(n % 2 + 1) * T], w[:, which, :],
                                            xtb[:, par, :], start=True, stop=True)
                        ins.then_inc(s("qk_ready"), 1)
                    elif kind == "V":
                        pe.wait_ge(s("exp_done"), PRIMED + b * NPAIR)
                        w = {0: wq0[:, 4, :], 2: wq2[:, 2, :], 3: wq3[:, 2, :]}[l]
                        for c in range(2):
                            ins = pe.matmul(pT_[:, 0, c * P:(c + 1) * P], xtb[:, par, c * P:(c + 1) * P], w,
                                            start=True, stop=True)
                        ins.then_inc(s("v_ready"), 1)
                    elif kind == "K":
                        pe.wait_ge(s("qk_split"), PRIMED + b + 1)
                        pe.wait_ge(s("v_done"), PRIMED + b + 1)
                        pe.wait_ge(s("stacked"), PRIMED + b * NJ + max(0, k - 1))
                        for side in range(2):
                            o = pT_[:, k % 2, side * T:(side + 1) * T]
                            pe.matmul(o, selq[:, 2 * side, k, :], qk16[:, 0, side * T:(side + 1) * T],
                                      start=True, stop=False)
                            ins = pe.matmul(o, selq[:, 2 * side + 1, k, :], qk16[:, 1, side * T:(side + 1) * T],
                                            start=False, stop=(l != 3))
                            if l == 3:
                                ins = pe.matmul(o, alcol[:, side, k, :], alrow[:, :], start=False, stop=True)
                        ins.then_inc(s("stack_ready"), 1)
                    elif kind == "S":
                        pe.wait_ge(s("stacked"), PRIMED + b * NJ + k // 2 + 1)
                        pe.wait_ge(s("qk_done"), PRIMED + b + 1)
                        pe.wait_ge(s("max_done"), PRIMED + b * NPAIR + k)
                        for a in range(2):
                            g, j = 2 * (k % 2) + a, k // 2
                            rows = slice(32 * g, 32 * g + 32)
                            for c in range(2):
                                n = P * (c + 1) if l == 3 else T
                                ins = pe.matmul(pS[:, a, c * T:c * T + n], stk[rows, j, c * P:(c + 1) * P],
                                          stk[rows, j, T:T + n], start=True, stop=True)
                                if l == 3:
                                    ins = pe.matmul(pS[:, a, c * T + c * P:c * T + (c + 1) * P], identb[:, :],
                                              maskb[:, 0, :], start=False, stop=True, skip_group_check=True)
                        ins.then_inc(s("raw_scores"), 1)
                    elif kind == "M":
                        pe.wait_ge(s("max_done"), PRIMED + (b + 1) * NPAIR)
                        for c in range(2):
                            ins = pe.transpose(pS[:, 0, c * P:(c + 1) * P], mx[:, c, :], ident[:, :])
                        ins.then_inc(s("max_turned"), 1)
                    elif kind == "T":
                        pe.wait_ge(s("max_rows"), PRIMED + b + 1)
                        pe.wait_ge(s("stacked"), PRIMED + (b + 1) * NJ)
                        pe.wait_ge(s("exp_done"), PRIMED + b * NPAIR + k)
                        for a in range(2):
                            g, j = 2 * (k % 2) + a, k // 2
                            rows = slice(32 * g, 32 * g + 32)
                            pe.matmul(pT_[:, a, :].rearrange("p (c q) -> p c q", c=2), selm[rows, j, :],
                                      mt[rows, None, :].to_broadcast([32, 2, T]), start=True, stop=True)
                            for c in range(2):
                                q0 = P * c if l == 3 else 0
                                ins = pe.matmul(pT_[:, a, c * T + q0:(c + 1) * T],
                                                stk[rows, j, T + c * P:T + (c + 1) * P],
                                                stk[rows, j, q0:T], start=False, stop=True,
                                                skip_group_check=True)
                                if l == 3:
                                    ins = pe.matmul(pT_[:, a, c * T + c * P:c * T + (c + 1) * P], identb[:, :],
                                                    maskb[:, 1, :], start=False, stop=True,
                                                    skip_group_check=True)
                        ins.then_inc(s("scores_ready"), 1)
                    elif kind == "O":
                        pe.wait_ge(s("exp_done"), PRIMED + b * NPAIR + k + 1)
                        pe.wait_ge(s("v_done"), PRIMED + b + 1)
                        pe.wait_ge(s("out_read"), PRIMED + b)
                        for a in range(2):
                            h = 2 * k + a
                            for c in range(2):
                                kcs = [0] if (l == 3 and c == 0) else [0, 1]
                                for kc in kcs:
                                    ins = pe.matmul(po[:, c, h, :], pT[:, k % 2, a, kc, c * P:(c + 1) * P],
                                                    va[:, kc, h, :], start=(kc == 0), stop=(kc == kcs[-1]))
                        ins.then_inc(s("pv_done"), 1)
                    elif kind == "N" and l == 3:
                        pe.wait_ge(s("out_read"), PRIMED + b + 1)
                        for c in range(2):
                            ins = pe.transpose(pS[:, 0, c * P:(c + 1) * P], ob[:, c, :], ident[:, :])
                        ins.then_inc(s("out_turned"), 1)
                        pe.wait_ge(s("oT_ready"), PRIMED + b + 1)
                        for c in range(2):
                            ins = pe.matmul(pS[:, 1, c * P:(c + 1) * P], oT[:, c * P:(c + 1) * P], wp3[:, :],
                                            start=True, stop=True)
                        ins.then_inc(s("out_proj"), 1)

            for l in range(4):
                pe.wait_ge(sem(f"ld_{l}"), full[f"ld_{l}"])
                phase_a(l)
                if l == 0:
                    search()
                if l == 3:
                    pe.wait_ge(sem("w3_ready"), 3)
                with pe.Fori(0, B // 2) as turn:
                    i = turn * 2
                    for par in range(2):
                        row(l, i + par, par)

        @block.scalar
        def _(act):
            def phase_a(l):
                s = lambda n: sem(f"L{l}_{n}")
                with act.Fori(0, NT // 4 // 2) as turn:
                    i = turn * 2
                    for par in range(2):
                        act.wait_ge(sem("turned"), PRIMED + l * (NT // 4) + i + par + 1)
                        act.wait_ge(sem("xt_copied"), PRIMED + l * (NT // 4) + i)
                        if l < 3:
                            act.wait_ge(sem("logits"), PRIMED + l * (NT // 4) + i)
                        act.activation(xts[:, par, :], pS[:, par, :], ACT.Copy).then_inc(sem("xts_ready"), 1)
                    if l < 3:
                        for par in range(2):
                            act.wait_ge(sem("logits"), PRIMED + l * (NT // 4) + i + par + 1)
                            act.activation(LG[:, bass.ds((i + par) * 4, 4), 0:EXPERTS[l]],
                                           pT_[:, par, 0:64].rearrange("p (u e) -> p u e", e=16)[:, :, 0:EXPERTS[l]],
                                           ACT.Copy).then_inc(sem("logits_copied"), 1)

            def row(l, b, par):
                s = lambda n: sem(f"L{l}_{n}")
                nh, ny = plans[l][1], y_uses(l)
                for kind, k in steps[l]:
                    if kind == "H":
                        act.wait_ge(s("h_ready"), PRIMED + b * nh + k + 1)
                        bank = pH[:, k % 2, :]
                        if l == 3:
                            act.wait_ge(s("h_act"), PRIMED + b * nh + max(0, k - 1))
                            act.activation(th[:, k % 2, :], bank[:, 0:T], ACT.Tanh, scale=0.5)\
                               .then_inc(s("tanh_done"), 1)
                            continue
                        done = max(0, k // 2 - 1) if l != 1 else max(0, k - 3)
                        act.wait_ge(s("y_ready"), PRIMED + b * ny + (EXTRA_Y[l] + done if done else 0))
                        if l == 0:
                            act.activation(hb[:, k % 4, :], bank, ACT.Relu).then_inc(s("h_act"), 1)
                        else:
                            for half in range(2):
                                bias = b1[1][:, 2 * k + half:2 * k + half + 1] if l == 1 else \
                                    b1[2][:, k // 2, 2 * (k % 2) + half:2 * (k % 2) + half + 1]
                                ins = act.activation(hb[:, k % 4, half * T:(half + 1) * T],
                                                     bank[:, half * T:(half + 1) * T], ACT.Relu, bias=bias)
                            ins.then_inc(s("h_act"), 1)
                    elif kind == "K":
                        act.wait_ge(s("stack_ready"), PRIMED + b * NJ + k + 1)
                        act.wait_ge(s("scores_ready"), PRIMED + b * NPAIR)
                        act.activation(stk[:, k, :], pT_[:, k % 2, :], ACT.Copy).then_inc(s("stacked"), 1)
                    elif kind == "T":
                        act.wait_ge(s("scores_ready"), PRIMED + b * NPAIR + k + 1)
                        act.wait_ge(s("pv_done"), PRIMED + b * NPAIR + max(0, k - 1))
                        if l == 3:
                            act.activation(pT[:, k % 2, :, 0, :], pT_[:, :, 0:T], ACT.Exp)
                            ins = act.activation(pT[:, k % 2, :, 1, P:T], pT_[:, :, T + P:2 * T], ACT.Exp)
                        else:
                            ins = act.activation(pT[:, k % 2, :, :, :].rearrange("p a c q -> p (a c q)"),
                                                 pT_[:, :, :].rearrange("p a n -> p (a n)"), ACT.Exp)
                        ins.then_inc(s("exp_done"), 1)
                    elif kind == "N" and l == 3:
                        act.wait_ge(s("out_turned"), PRIMED + b + 1)
                        act.wait_ge(s("out_proj"), PRIMED + b)
                        act.activation(oT[:, :], pS[:, 0, 0:T], ACT.Copy).then_inc(s("oT_ready"), 1)

            for l in range(4):
                if l < 3:
                    phase_a(l)
                    act.wait_ge(sem("shifted"), PRIMED + l + 1)
                    act.activation(pr[:, :, 0:EXPERTS[l]], ra[:, :, 0:EXPERTS[l]], ACT.Exp)\
                       .then_inc(sem("exp_logits"), 1)
                else:
                    phase_a(l)
                if l == 1:
                    act.wait_ge(sem("ld_1"), full["ld_1"])
                    act.activation(lamt[:, :], llr1[:, :], ACT.Tanh, scale=0.5).then_inc(sem("lam_tanh"), 1)
                with act.Fori(0, B // 2) as turn:
                    i = turn * 2
                    for par in range(2):
                        row(l, i + par, par)

        @block.gpsimd
        def _(pool):
            chain = Chain(pool, sem("pool_chain"))
            pool.wait_ge(sem("ld_cst"), full["ld_cst"])
            for l in range(4):
                s = lambda n: sem(f"L{l}_{n}")
                if l == 3:
                    pool.wait_ge(sem("ld_3"), full["ld_3"])
                    for n in range(3):
                        pool.tensor_scalar(wf3[:, n, :], wi3[:, n, :], 1.0 / 127.0, None, ALU.mult)\
                            .then_inc(sem("w3_ready"), 1)
                pool.wait_ge(sem("stats"), PRIMED + l + 1)
                chain.link(pool.tensor_scalar(vare[:, :], MV[:, :, 1], EPS, None, ALU.add))
                pool.tensor_tensor(rstd[:, :], vare[:, :], neghalf[:, :], ALU.pow).then_inc(sem("rstd"), 1)
                with pool.Fori(0, NT // 4 // 2) as turn:
                    i = turn * 2
                    for par in range(2):
                        pool.wait_ge(sem("xts_ready"), PRIMED + l * (NT // 4) + i + par + 1)
                        settle(pool, sem("pool_settled"))
                        pool.tensor_copy(XT[:, bass.ts(i + par, 4 * P)], xts[:, par, :]).then_inc(sem("xt_copied"), 1)
                pool.wait_ge(sem("xt_copied"), PRIMED + l * (NT // 4) + NT // 4)
                if l < 3:
                    pool.wait_ge(sem("gates"), PRIMED + l + 1)
                split = RowChain(pool, sem(f"L{l}_pool_chain"), 1)
                with pool.Fori(0, B // 2) as turn:
                    i = turn * 2
                    for par in range(2):
                        b = i + par
                        split.enter(b)
                        pool.wait_ge(s("row_used"), PRIMED + i)
                        settle(pool, sem("pool_settled"))
                        if l < 3:
                            pool.tensor_copy(gst[:, par, :, :], GA[:, bass.ds(b * 2, 2), :])\
                                .then_inc(s("gates_staged"), 1)
                            pool.wait_ge(s("gates_staged"), PRIMED + b + 1)
                            settle(pool, sem("pool_settled"))
                        pool.tensor_copy(xtb[:, par, :], XT[:, bass.ts(b, T)]).then_inc(s("row_staged"), 1)
                        if attn(l):
                            src = qkf[:, 0, :]
                            pool.wait_ge(s("qk_done"), PRIMED + b + 1)
                            pool.wait_ge(s("stack_ready"), PRIMED + b * NJ)
                            if l == 0:
                                pool.tensor_tensor(qkf[:, 0, :], qkf[:, 0, :], qkf[:, 1, :], ALU.add)\
                                    .then_inc(s("qk_summed"), 1)
                                pool.wait_ge(s("qk_summed"), PRIMED + b + 1)
                            settle(pool, sem("pool_settled"))
                            split.link(pool.tensor_copy(qk16[:, 0, :], src))
                            pool.tensor_tensor(qk16[:, 1, :], src, qk16[:, 0, :], ALU.subtract)\
                                .then_inc(s("qk_split"), 1)
                            split.leave()
                        else:
                            pool.wait_ge(s("z_stats"), PRIMED + b + 1)
                            settle(pool, sem("pool_settled"))
                            split.link(pool.tensor_scalar(zve[:, :], zmv[:, :, 1], EPS, None, ALU.add))
                            pool.tensor_tensor(zr[:, :], zve[:, :], neghalf[:, 0:2], ALU.pow)\
                                .then_inc(s("z_rstd"), 1)
                            split.leave()

        @block.vector
        def _(dve):
            chain = Chain(dve, sem("dve_chain"))
            dve.wait_ge(sem("ld_cst"), full["ld_cst"])
            dve.wait_ge(sem("ld_x"), full["ld_x"])
            chain.link(dve.memset(va[:, :, :, DH:DH + 1], 1.0))
            chain.link(dve.memset(mx[:, :, :], 0.0))
            chain.link(dve.memset(GA[:, :, :], 0.0))
            chain.link(dve.memset(gst[:, :, :, :], 0.0))

            def statistics(l):
                s = lambda n: sem(f"L{l}_{n}")
                with dve.Fori(0, NT // 4) as turn:
                    i = turn * 4
                    for u in range(4):
                        dve.bn_stats(st6[:, u, :], X[:, i + u, :]).then_inc(sem("bn"), 1)
                    dve.wait_ge(sem("bn"), PRIMED + l * (NT) + i + 4)
                    settle(dve, sem("dve_settled"))
                    for u in range(4):
                        ins = dve.bn_aggr(mv4[:, u, :], st6[:, u, :])
                    ins.then_inc(sem("aggr"), 1)
                    dve.wait_ge(sem("aggr"), PRIMED + l * (NT // 4) + turn + 1)
                    settle(dve, sem("dve_settled"))
                    dve.tensor_copy(MV[:, bass.ds(i, 4), :], mv4[:, :, :]).then_inc(sem("stats_kept"), 1)
                dve.wait_ge(sem("stats_kept"), PRIMED + l * (NT // 4) + NT // 4)
                dve.sem_inc(sem("stats"), 1)

            def phase_a(l):
                s = lambda n: sem(f"L{l}_{n}")
                statistics(l)
                dve.wait_ge(sem("rstd"), PRIMED + l + 1)
                with dve.Fori(0, NT // 4 // 2) as turn:
                    i = turn * 2
                    for par in range(2):
                        dve.wait_ge(sem("turned"), PRIMED + l * (NT // 4) + i)
                        for u in range(4):
                            t = (i + par) * 4 + u
                            ins = dve.tensor_scalar(xn[:, par, u, :], X[:, t, :], MV[:, t, 0:1],
                                                    rstd[:, bass.ds(t, 1)], ALU.subtract, ALU.mult)
                        ins.then_inc(sem("xn_ready"), 1)

            def routing(l):
                s = lambda n: sem(f"L{l}_{n}")
                n = EXPERTS[l]
                full_e = lambda a: a[:, :, None].to_broadcast([P, NT, n])
                lg, p_, a_, b_, c_, g_, k_ = (x[:, :, 0:n] for x in (LG, pr, ra, rb, rc, GA, rank))
                dve.wait_ge(sem(f"ld_{l}"), full[f"ld_{l}"])
                dve.wait_ge(sem("logits_copied"), PRIMED + l * (NT // 4) + NT // 4)
                if l > 0:
                    chain.link(dve.tensor_tensor(lg, lg, br[l][:, None, :].to_broadcast([P, NT, n]), ALU.add))
                chain.link(dve.tensor_reduce(r1[:, :], lg, AX.X, ALU.max))
                dve.tensor_tensor(a_, lg, full_e(r1), ALU.subtract).then_inc(sem("shifted"), 1)
                dve.wait_ge(sem("exp_logits"), PRIMED + l + 1)
                chain.link(dve.tensor_reduce(r1[:, :], p_, AX.X, ALU.add))
                chain.link(dve.reciprocal(r2[:, :], r1[:, :]))
                chain.link(dve.tensor_tensor(p_, p_, full_e(r2), ALU.mult))
                for k in range(TOPK[l]):
                    chain.link(dve.tensor_reduce(r1[:, :], p_, AX.X, ALU.max))
                    chain.link(dve.tensor_tensor(a_, p_, full_e(r1), ALU.is_ge))
                    chain.link(dve.tensor_tensor(a_, a_, k_, ALU.mult))
                    chain.link(dve.tensor_reduce(r2[:, :], a_, AX.X, ALU.max))
                    chain.link(dve.tensor_tensor(b_, k_, full_e(r2), ALU.is_equal))
                    if k == 0:
                        chain.link(dve.tensor_tensor(g_, p_, b_, ALU.mult))
                    else:
                        chain.link(dve.tensor_tensor(c_, p_, b_, ALU.mult))
                        chain.link(dve.tensor_tensor(g_, g_, c_, ALU.add))
                    if k < TOPK[l] - 1 or l == 0:
                        chain.link(dve.scalar_tensor_tensor(p_, b_, -2.0, p_, ALU.mult, ALU.add))
                if l == 1:
                    chain.link(dve.memset(GA[:, :, 15:16], 1.0))
                if l == 0:
                    capacity()
                dve.sem_inc(sem("gates"), 1)

            def capacity():
                e_t = lambda a: a[:, :, None].to_broadcast([P, 8, NT])
                flat = lambda a: a.rearrange("p e t -> p (e t)")
                g_ = GA[:, :, 0:8].rearrange("p t e -> p e t")
                p_ = pr[:, :, 0:8].rearrange("p t e -> p e t")
                chain.link(dve.tensor_scalar(key[:, :, :], p_, 0.0, None, ALU.is_ge))
                chain.link(dve.tensor_tensor(key[:, :, :], g_, key[:, :, :], ALU.subtract))
                chain.link(dve.memset(thr[:, :], 0))
                chain.link(dve.tensor_copy(biti[:, :], bitf[:, :]))
                with dve.Fori(0, SEARCH_BITS) as i:
                    rc_ = RowChain(dve, sem("search_chain"), 7)
                    rc_.enter(i)
                    rc_.link(dve.tensor_tensor(cand[:, :], thr[:, :], biti[:, :], ALU.bitwise_or))
                    rc_.link(dve.tensor_tensor(cmp_[:, :, :], key[:, :, :], e_t(cand[:, :].bitcast(F32)), ALU.is_ge))
                    dve.tensor_reduce(cnt[:, :], cmp_[:, :, :], AX.X, ALU.add).then_inc(sem("counted"), 1)
                    dve.wait_ge(sem("summed"), PRIMED + i + 1)
                    rc_.link(dve.tensor_scalar(left[:, :], pT_[:, 0, 0:8], float(CAP), None, ALU.is_ge))
                    rc_.link(dve.tensor_tensor(addb[:, :], left[:, :], bitf[:, :], ALU.mult))
                    rc_.link(dve.tensor_tensor(thr[:, :], thr[:, :], addb[:, :], ALU.bitwise_or))
                    rc_.link(dve.tensor_scalar(bitf[:, :], bitf[:, :], 0.5, None, ALU.mult))
                    rc_.link(dve.tensor_copy(biti[:, :], bitf[:, :]))
                    rc_.leave()
                thf = e_t(thr[:, :].bitcast(F32))
                chain.link(dve.tensor_tensor(cmp_[:, :, :], key[:, :, :], thf, ALU.is_gt))
                dve.tensor_reduce(cnt[:, :], cmp_[:, :, :], AX.X, ALU.add).then_inc(sem("counted"), 1)
                dve.wait_ge(sem("summed"), PRIMED + SEARCH_BITS + 1)
                chain.link(dve.tensor_scalar(left[:, :], pT_[:, 0, 0:8], -1.0, float(CAP), ALU.mult, ALU.add))
                chain.link(dve.tensor_copy(scan[:, :, :], cmp_[:, :, :]))
                dve.tensor_tensor(cmp_[:, :, :], key[:, :, :], thf, ALU.is_equal).then_inc(sem("counted"), 1)
                dve.wait_ge(sem("counted"), PRIMED + SEARCH_BITS + 2)
                dve.wait_ge(sem("summed"), PRIMED + SEARCH_BITS + 2)
                before = rb[:, :, :].rearrange("p t e -> p (t e)")[:, 0:8 * NT].rearrange("p (e t) -> p e t", e=8)
                tot = rc[:, :, :].rearrange("p t e -> p (t e)")[:, 0:8 * NT].rearrange("p (e t) -> p e t", e=8)
                chain.link(dve.tensor_copy(flat(tot), pS[:, 1, 0:8 * NT]))
                for e in range(8):
                    ins = dve.tensor_tensor_scan(before[:, e, :], onesm[:, 0:NT], tot[:, e, :], 0.0, ALU.mult, ALU.add)
                    m = chain.mark(ins)
                chain.wait(m)
                chain.link(dve.tensor_tensor(flat(before), flat(before), flat(tot), ALU.subtract))
                chain.link(dve.tensor_tensor(flat(before), flat(before), pS[:, 0, 0:8 * NT], ALU.add))
                chain.link(dve.tensor_tensor(before, before, e_t(left[:, :]), ALU.is_lt))
                chain.link(dve.tensor_tensor(before, before, cmp_[:, :, :], ALU.mult))
                chain.link(dve.tensor_tensor(before, before, scan[:, :, :], ALU.add))
                chain.link(dve.tensor_tensor(g_, g_, before, ALU.mult))

            PER = {0: 19, 1: 42, 2: 20, 3: 8}

            def row(l, b, par, rc_):
                s = lambda n: sem(f"L{l}_{n}")
                nh, ny = plans[l][1], y_uses(l)
                rc_.enter(b)
                xt = lambda c: X[:, b * 2 + c, :]
                x2 = X[:, bass.ds(b * 2, 2), :]
                state = {"x": None}

                def before_x():
                    if state["x"] is not None:
                        rc_.wait(state["x"])

                for kind, k in steps[l]:
                    if kind == "P":
                        dve.wait_ge(s("qk_ready"), PRIMED + b + 1)
                        dve.wait_ge(s("qk_split"), PRIMED + b)
                        if l == 0:
                            for half in range(2):
                                for side in range(2):
                                    ins = dve.scalar_tensor_tensor(
                                        qkf[:, half, side * T:(side + 1) * T], pS[:, half, side * T:(side + 1) * T],
                                        bq0[:, 2 * side + half:2 * side + half + 1], rope0[:, 2 * side + half, :],
                                        ALU.add, ALU.mult)
                        elif l == 2:
                            for side in range(2):
                                ins = dve.tensor_scalar(qkf[:, 0, side * T:(side + 1) * T],
                                                        pS[:, 0, side * T:(side + 1) * T],
                                                        rope2[:, side, bass.ds(b, 1)], None, ALU.mult)
                        else:
                            for side in range(2):
                                ins = dve.tensor_scalar(qkf[:, 0, side * T:(side + 1) * T],
                                                        pS[:, 0, side * T:(side + 1) * T], bq3[:, side:side + 1],
                                                        QSCALE if side == 0 else 1.0, ALU.add, ALU.mult)
                        ins.then_inc(s("qk_done"), 1)
                    elif kind == "V":
                        dve.wait_ge(s("v_ready"), PRIMED + b + 1)
                        dve.wait_ge(s("pv_done"), PRIMED + b * NPAIR)
                        src = pT_[:, 0, 0:2 * P].rearrange("p (c h e) -> p c h e", c=2, h=H)
                        for c in range(2):
                            if l == 2:
                                ins = dve.tensor_copy(va[:, c, :, 0:DH], src[:, c, :, :])
                            else:
                                bias = (bv0 if l == 0 else bv3)[:, :].rearrange("p (h e) -> p h e", h=H)
                                ins = dve.tensor_tensor(va[:, c, :, 0:DH], src[:, c, :, :], bias, ALU.add)
                        ins.then_inc(s("v_done"), 1)
                    elif kind == "S":
                        dve.wait_ge(s("raw_scores"), PRIMED + b * NPAIR + k + 1)
                        dve.wait_ge(s("max_turned"), PRIMED + b)
                        g = 2 * (k % 2)
                        mcol = mx[:, :, :].rearrange("p c (g r) -> p c g r", g=NG)[:, :, g:g + 2, k // 2]
                        if l == 3:
                            dve.tensor_reduce(mcol[:, 0, :], pS[:, :, 0:P], AX.X, ALU.max)
                            ins = dve.tensor_reduce(mcol[:, 1, :], pS[:, :, T:2 * T], AX.X, ALU.max)
                        else:
                            ins = dve.tensor_reduce(mcol.rearrange("p c a -> p a c"),
                                                    pS[:, :, :].rearrange("p a (c n) -> p a c n", c=2),
                                                    AX.X, ALU.max)
                        ins.then_inc(s("max_done"), 1)
                    elif kind == "M":
                        dve.wait_ge(s("max_turned"), PRIMED + b + 1)
                        dve.wait_ge(s("scores_ready"), PRIMED + b * NPAIR)
                        dve.tensor_scalar(mt[:, :], pS[:, 0, 0:T], -1.0, None, ALU.mult).then_inc(s("max_rows"), 1)
                    elif kind == "G":
                        dve.wait_ge(s("y_ready"), PRIMED + b * ny + 1)
                        dve.tensor_copy(gt[:, :], pY[0:16, 0:T]).then_inc(s("y_free"), 1)
                    elif kind == "B":
                        dve.wait_ge(s("y_ready"), PRIMED + b * ny + 2)
                        ins = dve.tensor_tensor(x2, x2, pY[:, 0:2 * P].rearrange("p (c e) -> p c e", c=2), ALU.add)
                        state["x"] = rc_.mark(ins)
                        rc_.wait(state["x"])
                        dve.sem_inc(s("y_free"), 1)
                    elif kind == "Y":
                        dve.wait_ge(s("y_ready"), PRIMED + b * ny + y_use(l, k) + 1)
                        if l == 3:
                            before_x()
                            state["x"] = rc_.mark(dve.tensor_tensor(
                                x2, x2, pY[:, 0:2 * P].rearrange("p (c e) -> p c e", c=2), ALU.add))
                        else:
                            for half in range(2 if l == 1 else 1):
                                before_x()
                                e = 2 * k + half if l == 1 else k
                                for c in range(2):
                                    o = half * T + c * P
                                    state["x"] = rc_.mark(dve.scalar_tensor_tensor(
                                        xt(c), pY[:, o:o + P], gst[:, par, c, e:e + 1], xt(c), ALU.mult, ALU.add))
                        rc_.wait(state["x"])
                        dve.sem_inc(s("y_free"), 1)
                    elif kind == "H" and l == 3:
                        dve.wait_ge(s("tanh_done"), PRIMED + b * nh + k + 1)
                        dve.wait_ge(s("y_ready"), PRIMED + b * ny)
                        rc_.link(dve.scalar_tensor_tensor(hg[:, k % 2, :], th[:, k % 2, :], 1.0, pH[:, k % 2, 0:T],
                                                          ALU.add, ALU.mult))
                        dve.scalar_tensor_tensor(hb[:, k, 0:T], hg[:, k % 2, :], 0.5, pH[:, k % 2, T:2 * T],
                                                 ALU.mult, ALU.mult).then_inc(s("h_act"), 1)
                    elif kind == "R":
                        dve.wait_ge(s("xb_ready"), PRIMED + b + 1)
                        rc_.link(dve.tensor_scalar(vals[:, :], pS[:, 0, 0:T], bb1[:, 0:1], oml[:, 0:1],
                                                   ALU.add, ALU.mult))
                        dve.wait_ge(s("z_ready"), PRIMED + b)
                        dve.tensor_tensor_scan(hT[:, :], lamrow[:, :], vals[:, :], 0.0, ALU.mult, ALU.add)\
                           .then_inc(s("scanned"), 1)
                    elif kind == "Z":
                        dve.wait_ge(s("z_ready"), PRIMED + b + 1)
                        for c in range(2):
                            ins = dve.bn_stats(zs[:, c, :], pS[:, 1, c * P:(c + 1) * P])
                            m = rc_.mark(ins)
                        rc_.wait(m)
                        dve.wait_ge(s("z_rstd"), PRIMED + b)
                        settle(dve, sem("dve_settled"))
                        for c in range(2):
                            m = rc_.mark(dve.bn_aggr(zmv[:, c, :], zs[:, c, :]))
                        rc_.wait(m)
                        dve.sem_inc(s("z_stats"), 1)
                    elif kind == "N" and l == 1:
                        dve.wait_ge(s("z_rstd"), PRIMED + b + 1)
                        for c in range(2):
                            m = rc_.mark(dve.tensor_scalar(zn[:, c, :], pS[:, 1, c * P:(c + 1) * P],
                                                           zmv[:, c, 0:1], zr[:, c:c + 1], ALU.subtract, ALU.mult))
                        rc_.wait(m)
                        wide = lambda a: a[:, None, :].to_broadcast([P, 2, P])
                        rc_.link(dve.tensor_tensor(zg[:, :, :], zn[:, :, :], wide(gam1), ALU.mult))
                        rc_.link(dve.tensor_tensor(zn[:, :, :], zg[:, :, :], wide(bet1), ALU.add))
                        before_x()
                        dve.tensor_tensor(x2, x2, zn[:, :, :], ALU.add).then_inc(s("x_final"), 1)
                    elif kind == "N":
                        dve.wait_ge(s("pv_done"), PRIMED + (b + 1) * NPAIR)
                        rc_.link(dve.reciprocal(rden[:, :, :], po[:, :, :, DH]))
                        for c in range(2):
                            ins = dve.tensor_tensor(ob[:, c, :].rearrange("p (h e) -> p h e", h=H), po[:, c, :, 0:DH],
                                                    rden[:, c, :, None].to_broadcast([P, H, DH]), ALU.mult)
                            m = rc_.mark(ins)
                        rc_.wait(m)
                        dve.sem_inc(s("out_read"), 1)
                        if l == 3:
                            before_x()
                            rc_.link(dve.tensor_tensor(x2, x2, bp3[:, None, :].to_broadcast([P, 2, P]), ALU.add))
                            dve.wait_ge(s("out_proj"), PRIMED + b + 1)
                            dve.tensor_tensor(x2, x2, pS[:, 1, 0:2 * P].rearrange("p (c e) -> p c e", c=2), ALU.add)\
                               .then_inc(s("x_final"), 1)
                        else:
                            before_x()
                            dve.tensor_tensor(x2, x2, ob[:, :, :], ALU.add).then_inc(s("x_final"), 1)
                dve.wait_ge(s("x_final"), PRIMED + b + 1)
                dve.sem_inc(s("row_used"), 1)
                rc_.leave()

            for l in range(4):
                phase_a(l)
                if l < 3:
                    routing(l)
                if l == 1:
                    dve.wait_ge(sem("lam_tanh"), 1)
                    chain.link(dve.tensor_scalar(lam1[:, :], lamt[:, :], 0.5, 0.5, ALU.mult, ALU.add))
                    chain.link(dve.tensor_scalar(oml[:, :], lamt[:, :], -0.5, 0.5, ALU.mult, ALU.add))
                    chain.link(dve.tensor_copy(lamrow[:, :], lam1[:, :].to_broadcast([P, T])))
                rc_ = RowChain(dve, sem(f"L{l}_dve_chain"), PER[l])
                with dve.Fori(0, B // 2) as turn:
                    i = turn * 2
                    for par in range(2):
                        row(l, i + par, par, rc_)
                dve.wait_ge(sem(f"L{l}_x_final"), PRIMED + B)

        primed = [n for n in sems if n in SHARED_SIGNALS or (n.startswith("L") and not n.endswith("_chain"))]

        @block.sync
        def _(sp):
            for name in primed:
                sp.sem_inc(sem(name), PRIMED)
            for group, moves in loads.items():
                for n, (dst, src) in enumerate(moves):
                    if group == "ld_2" and n == 0:
                        sp.wait_ge(sem("L0_x_final"), PRIMED + B)
                    sp.dma_start(dst, src).then_inc(sem(group), 16)
            for c in range(4):
                sp.wait_ge(sem("L3_x_final"), PRIMED + 4 * c + 4)
                sp.dma_start(xout[:, 8 * c:8 * c + 8, :], X[:, 8 * c:8 * c + 8, :]).then_inc(sem("stored"), 16)
            sp.wait_ge(sem("stored"), 64)


def shape_constants():
    c = {}
    f = np.float32
    c["c_ident"] = np.eye(P, dtype=f)
    c["c_ones"] = np.ones((P, P), f)
    c["c_neghalf"] = np.full((P, NT), -0.5, f)
    c["c_tri"] = np.triu(np.ones((P, P), f), 1)
    c["c_rank"] = np.broadcast_to(16.0 - np.arange(16, dtype=f), (P, NT, 16)).copy()
    c["c_bitf"] = np.full((P, 8), 2.0 ** (SEARCH_BITS - 1), f)
    sel = np.zeros((P, 4, NJ, P), np.float16)
    for j in range(NJ):
        for g in range(NG):
            for e in range(DH):
                src = (NG * j + g) * DH + e
                for which, rs in ((0, (0, 1)), (1, (2,)), (2, (0, 2)), (3, (1,))):
                    for r in rs:
                        sel[src, which, j, 32 * g + DH * r + e] = 1
    c["c_selq"] = sel
    selm = np.zeros((P, NJ, P), np.float32)
    for j in range(NJ):
        for g in range(NG):
            selm[32 * g + j, j, :] = 1
    c["c_selm"] = selm
    al = np.zeros((2, 2, NJ, P), np.float16)
    for j in range(NJ):
        for g in range(NG):
            slope = 2.0 ** -(NG * j + g + 1)
            al[0, 0, j, 32 * g + 24] = slope * 256
            al[1, 1, j, 32 * g + 24] = 1
            al[1, 0, j, 32 * g + 25] = 1
            al[0, 1, j, 32 * g + 25] = -slope * 256
    c["c_alcol"] = al
    c["c_alrow"] = np.stack([np.ones(T), np.arange(T) / 256.0]).astype(np.float16)
    m = np.where(np.arange(P)[None, :] > np.arange(P)[:, None], -1e30, 0.0).astype(f)
    c["c_mask"] = np.stack([m, m.T], axis=1)
    c["c_identb"] = np.eye(P, dtype=f)
    freqs = (f(1.0) / np.power(f(10000.0), np.arange(0, DH, 2, dtype=f) / f(DH))).astype(f)
    ang = np.arange(T, dtype=f)[:, None] * freqs[None, :]
    cos, sin = np.cos(ang).astype(f), np.sin(ang).astype(f)
    e = np.arange(P) % DH
    cs = cos[:, e // 2].T
    sn = (sin[:, e // 2] * np.where(e % 2 == 0, -1.0, 1.0).astype(f)).T
    c["c_rope0"] = np.stack([cs * f(QSCALE), sn * f(QSCALE), cs, sn], axis=1).astype(f)
    ang2 = np.arange(B, dtype=f)[:, None] * freqs[None, :]
    ang2 = np.concatenate([ang2, ang2], axis=-1)
    r2 = np.cos(ang2) + np.sin(ang2) * np.where(np.arange(DH) < DH // 2, 1.0, -1.0)
    r2 = r2[:, e].T.astype(f)
    c["c_rope2"] = np.stack([r2 * f(QSCALE), r2], axis=1).astype(f)
    return {k: np.ascontiguousarray(v) for k, v in c.items()}


def lay_out(i):
    a = {k: np.asarray(v) for k, v in i.items()}
    o = {}
    swap = np.arange(P) ^ 1
    o["x"] = a["L0_attn_x"].reshape(B * T, P)
    wt = a["L0_attn_W_qkv"].T
    q, k, v = wt[:, 0:P], wt[:, P:2 * P], wt[:, 2 * P:]
    o["wq0"] = np.stack([q, q[:, swap], k, k[:, swap], v], axis=1)
    bq, bk = a["L0_attn_b_qkv"][0:P], a["L0_attn_b_qkv"][P:2 * P]
    o["bq0"] = np.stack([bq, bq[swap], bk, bk[swap]], axis=1)
    o["bv0"] = a["L0_attn_b_qkv"][2 * P:]
    o["wr0"] = a["L0_ffn_Wr"]
    o["w1_0"] = a["L0_ffn_W1"].transpose(1, 0, 2)
    o["w2_0"] = a["L0_ffn_W2"].reshape(8, NF, P, P).transpose(2, 0, 1, 3)
    o["wr1"], o["br1"] = a["L1_ffn_router_W"], a["L1_ffn_router_b"]
    o["w1_1"] = np.concatenate([a["L1_ffn_eW1"], a["L1_ffn_sW1"][None]]).transpose(1, 0, 2)
    o["w2_1"] = np.concatenate([a["L1_ffn_eW2"], a["L1_ffn_sW2"][None]]).transpose(1, 0, 2)
    o["b1_1"] = np.concatenate([a["L1_ffn_eb1"], a["L1_ffn_sb1"][None]]).T
    o["b2_1"] = np.concatenate([a["L1_ffn_eb2"], a["L1_ffn_sb2"][None]])
    o["wb1"], o["wc1"] = a["L1_attn_Wb"].T, a["L1_attn_Wc"].T
    o["bb1"], o["bc1"] = a["L1_attn_bb"].reshape(P, 1), a["L1_attn_bc"].reshape(1, P)
    o["gam1"], o["bet1"] = a["L1_attn_gamma"], a["L1_attn_beta"]
    o["llr1"] = a["L1_attn_log_lambda_raw"].reshape(P, 1)
    o["wq2"] = np.stack([a["L2_attn_Wq"].T, a["L2_attn_Wk"].T, a["L2_attn_Wv"].T], axis=1)
    o["wr2"], o["br2"] = a["L2_ffn_Wr"], a["L2_ffn_br"]
    o["w1_2"] = a["L2_ffn_W1"].transpose(1, 0, 2)
    o["w2_2"] = a["L2_ffn_W2"].reshape(8, NF, P, P).transpose(2, 0, 1, 3)
    o["b1_2"] = a["L2_ffn_b1"].reshape(8, NF, P).transpose(2, 0, 1)
    o["b2_2"] = a["L2_ffn_b2"]
    o["wq3"] = a["L3_attn_W_attn"].reshape(P, 3, P)
    o["bq3"] = a["L3_attn_b_attn"][0:2 * P].reshape(2, P).T
    o["bv3"] = a["L3_attn_b_attn"][2 * P:]
    o["wp3"], o["bp3"] = a["L3_attn_W_proj"], a["L3_attn_b_proj"]
    down = a["L3_ffn_w_down"].T.reshape(NHC, P, P).transpose(1, 0, 2).reshape(P, HID)
    o["wi3"] = np.stack([a["L3_ffn_w_gate"].T, a["L3_ffn_w_up"].T, down], axis=1)
    return {k: np.ascontiguousarray(v) for k, v in o.items()}


def kernel(**inputs):
    import ml_dtypes as _ml
    import concourse.bacc as _bacc
    from concourse.bass_utils import run_bass_kernel_spmd as _run

    nc = _bacc.Bacc("TRN2", target_bir_lowering=False, num_devices=1)
    consts = shape_constants()
    for name in ("c_selm", "c_mask", "c_identb"):
        consts[name] = consts[name].astype(_ml.bfloat16)
    arrays = {**lay_out(inputs), **consts}
    d = {name: nc.dram_tensor("in_" + name, list(v.shape), mybir.dt.from_np(v.dtype), kind="ExternalInput").ap()
         for name, v in arrays.items()}
    out = nc.dram_tensor("out", [B, T, P], F32, kind="ExternalOutput").ap()
    build(nc, d, out)
    r = _run(nc, [{"in_" + name: v for name, v in arrays.items()}], core_ids=[0])
    return r.results[0]["out"]
```

```python
from contextlib import ExitStack

import numpy as np

import concourse.bass as bass
from concourse import mybir

F32 = mybir.dt.float32
F16 = mybir.dt.float16
BF16 = mybir.dt.bfloat16
I32 = mybir.dt.int32
ALU = mybir.AluOpType
ACT = mybir.ActivationFunctionType
AX = mybir.AxisListType

P = 128
B = 16
T = 256
NT = B * T // P
H = 16
DH = P // H
MAXROW = 26
NG = 4
NJ = H // NG
NPAIR = H // 2
CAP = 1280
EPS = 1e-5
PRIMED = 2
QSCALE = float(DH) ** -0.5
SEARCH_BITS = 30

SHARED_SIGNALS = ("bn", "aggr", "stats_kept", "stats", "rstd", "xn_ready", "turned", "xts_ready", "xt_copied",
                  "logits", "logits_copied", "shifted", "exp_logits", "gates", "counted", "summed")

EXPERTS = {0: 8, 1: 15, 2: 8}
TOPK = {0: 2, 1: 3, 2: 1}
FF = 512
NF = FF // P
HID = 384
NHC = HID // P


def feed_forward_plan(layer):
    if layer in (0, 2):
        nh, ny = 2 * EXPERTS[layer], EXPERTS[layer]
        need = [2 * m + 1 for m in range(ny)]
    elif layer == 1:
        nh = ny = 8
        need = list(range(ny))
    else:
        nh, ny = NHC, 1
        need = [NHC - 1]
    pieces, m = [], 0
    for k in range(nh):
        pieces.append(("H", k))
        if m < ny and k >= need[m] + 1:
            pieces.append(("Y", m))
            m += 1
    pieces += [("Y", mm) for mm in range(m, ny)]
    return pieces, nh, ny, need


RING = {"S": "S", "M": "S", "V": "S", "P": "S", "R": "S", "Z": "S", "K": "T", "T": "T", "Q": "T",
        "H": "H", "Y": "Y", "G": "Y", "B": "Y", "W": "Y", "O": "O"}
LAG = 3
POOL_HEADS = {h for h in range(H) if h % 3}
Y_BANKS = {0: 1, 1: 2, 2: 1, 3: 1}
LOOP_FROM, LOOP_TO = 2, 14


def turn_steps(layer, n):
    here, ahead, far, behind = (0 <= m < B for m in (n, n + 1, n + 2, n - 1))
    pieces = feed_forward_plan(layer)[0] if here else []
    if layer == 1:
        frame = ([("G", 0), ("B", 0), ("Z", 0)] if here else []) + ["F"] * 3 + ([("N", 0)] if here else [])
        frame += ([("R", 0)] if ahead else [])
    else:
        frame = [("G", 0), ("B", 0)] if layer == 2 and here else []
        for j in range(NJ):
            frame += ([("K", j)] if ahead else []) + ["F"]
            if layer == 3 and behind:
                frame += {0: [("Q", 0)], 1: [("Q", 1)], 3: [("W", 0)]}.get(j, [])
        for h in range(H):
            frame += ([("T", h)] if here else []) + ([("S", h)] if ahead else []) + ["F"]
            frame += [("D", h)] if here else []
            frame += [("O", h - LAG)] if here and h >= LAG else []
            if h == 9 and far:
                frame += [("P", 0), ("P", 1)]
        for h in range(H - LAG, H):
            frame += ["F"] + ([("O", h)] if here else []) + ([("M", h - H + LAG)] if ahead and h < H - LAG + 2 else [])
        frame += ([("V", 0), ("V", 1)] if ahead else []) + ["F"] + ([("N", 0)] if here else [])
    slots, done, placed, steps = frame.count("F"), 0, 0, []
    for step in frame:
        if step == "F":
            done += 1
            upto = -(-len(pieces) * done // slots) if layer != 1 else min(len(pieces), done)
            steps += pieces[placed:upto]
            placed = max(placed, upto)
        else:
            steps.append(step)
    steps += pieces[placed:] + ([("E", 0)] if here else [])
    used, out = {}, []
    for kind, k in steps:
        ring = RING.get(kind)
        out.append((kind, k, used.get(ring, 0)))
        used[ring] = used.get(ring, 0) + 1
    return out


def ring_uses(layer, ring, n):
    return sum(RING.get(kind) == ring for kind, _, _ in turn_steps(layer, n))


class Turn:

    def __init__(self, layer, n, loop=None):
        self.layer, self.n, self.loop = layer, n, loop
        self.steps = turn_steps(layer, n)
        self.par = n % 2

    def count(self, per, plus=0):
        if self.loop is None:
            return self.n * per + plus
        return self.loop * (2 * per) + (self.n * per + plus)

    def row(self, ahead=0):
        return self.count(1, ahead)

    def use(self, ring):
        before = sum(ring_uses(self.layer, ring, m) for m in range(-2, self.n))
        if self.loop is None:
            return before
        return self.loop * (2 * ring_uses(self.layer, ring, self.n)) + before


def run_turns(eng, layer, body):
    last = B + 1 if layer == 3 else B
    for n in range(-2, LOOP_FROM):
        body(Turn(layer, n))
    with eng.Fori(0, (LOOP_TO - LOOP_FROM) // 2) as loop:
        for par in range(2):
            body(Turn(layer, LOOP_FROM + par, loop))
    for n in range(LOOP_TO, last):
        body(Turn(layer, n))


def settle(eng, sem):
    eng.sem_inc(sem, 1)


class Chain:

    def __init__(self, eng, sem):
        self.eng, self.sem, self.base, self.n = eng, sem, 0, 0

    def enter(self, b):
        self.n, self.row = 0, b

    def mark(self, ins):
        ins.then_inc(self.sem, 1)
        self.n += 1
        return self.base + self.n

    def wait(self, mark):
        self.eng.wait_ge(self.sem, mark)

    def link(self, ins):
        self.wait(self.mark(ins))


class LoopChain(Chain):

    def __init__(self, eng, sem, per):
        super().__init__(eng, sem)
        self.per = per

    def enter(self, turn):
        self.base, self.n = turn * self.per, 0

    def leave(self):
        assert self.n == self.per, f"per pass {self.n}, not {self.per}"


class TurnChain(Chain):

    def __init__(self, eng, sem):
        super().__init__(eng, sem)
        self.total, self.counts = 0, {}

    def enter(self, turn):
        self.turn = turn
        if turn.loop is None:
            self.base = self.total
        else:
            per = self.counts[LOOP_FROM - 1]
            self.base = turn.loop * (2 * per) + self.total
        self.n = 0

    def leave(self):
        self.counts[self.turn.n] = self.n
        if self.turn.loop is not None:
            assert self.n == self.counts[LOOP_FROM - 1], (self.n, self.counts)
            if self.turn.n == LOOP_FROM + 1:
                self.total += self.n * (LOOP_TO - LOOP_FROM) - self.n
                return
        self.total += self.n


def build(nc, d, out):
    ctx = ExitStack()
    with ctx:
        def sb(name, shape, dt=F32):
            return ctx.enter_context(nc.sbuf_tensor(name, shape, dt))

        def psum(name, shape):
            return ctx.enter_context(nc.psum_tensor(name, shape, F32))

        sems = {}

        def sem(name):
            if name not in sems:
                sems[name] = ctx.enter_context(nc.semaphore(name))
            return sems[name]

        X = sb("X", [P, NT, P])
        XT = sb("XT", [P, B * T])
        w1 = {0: sb("w1_02", [P, 8, FF]), 1: sb("w1_1", [P, 16, P])}
        w2 = {0: sb("w2_02", [P, 8, NF, P]), 1: sb("w2_1", [P, 16, P])}
        w1[2], w2[2] = w1[0], w2[0]
        b1 = {2: sb("b1_2", [P, 8, NF]), 1: sb("b1_1", [P, 16])}
        b2 = {2: sb("b2_2", [16, P]), 1: sb("b2_1", [16, P])}
        wr = {l: sb(f"wr_{l}", [P, EXPERTS[l]]) for l in EXPERTS}
        br = {1: sb("br_1", [P, 15]), 2: sb("br_2", [P, 8])}
        wq0 = sb("wq0", [P, 5, P])
        bq0 = sb("bq0", [P, 4])
        bv0 = sb("bv0", [P, P])
        rope0 = sb("rope0", [P, 4, T])
        wq2 = sb("wq2", [P, 3, P])
        rope2 = sb("rope2", [P, 2, B])
        wq3 = sb("wq3", [P, 3, P])
        bq3 = sb("bq3", [P, 2])
        bv3 = sb("bv3", [P, P])
        wp3 = sb("wp3", [P, P])
        bp3 = sb("bp3", [P, P])
        wi3 = sb("wi3", [P, 3, HID], I32)
        wf3 = sb("wf3", [P, 3, HID])
        wb1, wc1 = sb("wb1", [P, P]), sb("wc1", [P, P])
        bb1 = sb("bb1", [P, 1])
        bc1 = sb("bc1", [1, P])
        gam1, bet1 = sb("gam1", [P, P]), sb("bet1", [P, P])
        llr1 = sb("llr1", [P, 1])
        lamt = sb("lamt", [P, 1])
        oml = sb("oml", [P, 1])
        lam1 = sb("lam1", [P, 1])
        lamrow = sb("lamrow", [P, T])
        ident = sb("ident", [P, P])
        onesr = sb("onesr", [1, P])
        onesm = sb("onesm", [P, P])
        selq = sb("selq", [P, 4, NJ, P], F16)
        onecol = sb("onecol", [2, P], F16)
        alcol = sb("alcol", [2, 2, NJ, P], F16)
        alrow = sb("alrow", [2, T], F16)
        maskb = sb("maskb", [P, 2, P], BF16)
        identb = sb("identb", [P, P], BF16)
        rank = sb("rank", [P, NT, 16])
        neghalf = sb("neghalf", [P, NT])
        tri = sb("tri", [P, P])

        st6 = sb("st6", [P, 4, 6])
        mv4 = sb("mv4", [P, 4, 2])
        MV = sb("MV", [P, NT, 2])
        vare = sb("vare", [P, NT])
        rstd = sb("rstd", [P, NT])
        xn = sb("xn", [P, 2, 4, P])
        xts = sb("xts", [P, 2, 4 * P])
        LG = sb("LG", [P, NT, 16])
        pr = sb("pr", [P, NT, 16])
        GA = sb("GA", [P, NT, 16])
        ra, rb, rc = (sb(n, [P, NT, 16]) for n in ("ra", "rb", "rc"))
        r1, r2 = sb("r1", [P, NT]), sb("r2", [P, NT])
        thr = sb("thr", [P, 8], I32)
        cand = sb("cand", [P, 8], I32)
        bitf = sb("bitf", [P, 8])
        biti = sb("biti", [P, 8], I32)
        addb = sb("addb", [P, 8], I32)
        cmp_ = sb("cmp_", [P, 8, NT])
        key = sb("key", [P, 8, NT])
        cnt = sb("cnt", [P, 8])
        left = sb("left", [P, 8])
        scan = sb("scan", [P, 8, NT])

        xtb = sb("xtb", [P, 2, T])
        gst = sb("gst", [P, 2, 2, 16])
        qkf = sb("qkf", [P, 2, 2 * T])
        qk16 = sb("qk16", [P, 2, 2 * T], F16)
        stk = sb("stk", [P, 2, NJ, 2 * T], F16)
        mx = sb("mx", [P, 2, NJ, P])
        pe32 = sb("pe32", [P, 4, 2 * T])
        pe16 = sb("pe16", [P, 2, 4, 2 * T], F16)
        v32 = sb("v32", [P, 2, P])
        va = sb("va", [P, 2, 2, 2, H, DH + 1], F16)
        hb = sb("hb", [P, 4, 2 * T])
        gt = sb("gt", [16, T])
        rden = sb("rden", [P, 2, H])
        ob = sb("ob", [P, 2, P])
        oT = sb("oT", [P, T])
        th = sb("th", [P, 2, T])
        hg = sb("hg", [P, 2, T])
        vals = sb("vals", [P, T])
        hT = sb("hT", [P, T])
        zs = sb("zs", [P, 2, 6])
        zmv = sb("zmv", [P, 2, 2])
        zve, zr = sb("zve", [P, 2]), sb("zr", [P, 2])
        zn, zg = sb("zn", [P, 2, P]), sb("zg", [P, 2, P])

        pS = psum("pS", [P, 2, 512])
        pT_ = psum("pT_", [P, 2, 512])
        pH = psum("pH", [P, 2, 512])
        pY = psum("pY", [P, 512])
        pO = psum("pO", [P, 512])
        po = pO[:, 0:2 * H * (DH + 1)].rearrange("p (c h e) -> p c h e", c=2, h=H)

        xin = d["x"].rearrange("(t p) e -> p t e", p=P)
        xout = out.rearrange("b (c p) e -> p (b c) e", p=P)

        loads = {
            "ld_x": [(X[:, 0:16, :], xin[:, 0:16, :]), (X[:, 16:32, :], xin[:, 16:32, :])],
            "ld_cst": [(ident[:, :], d["c_ident"]), (onesr[:, :], d["c_ones"][0:1, :]), (onesm[:, :], d["c_ones"]),
                       (selq[:, :, :, :], d["c_selq"]), (onecol[:, :], d["c_onecol"]),
                       (alcol[:, :, :, :], d["c_alcol"]), (alrow[:, :], d["c_alrow"]),
                       (maskb[:, :, :], d["c_mask"]), (identb[:, :], d["c_identb"]), (rank[:, :, :], d["c_rank"]),
                       (neghalf[:, :], d["c_neghalf"]), (tri[:, :], d["c_tri"]), (rope0[:, :, :], d["c_rope0"]),
                       (rope2[:, :, :], d["c_rope2"]), (bitf[:, :], d["c_bitf"])],
            "ld_0": [(wr[0][:, :], d["wr0"]), (wq0[:, :, :], d["wq0"]), (bq0[:, :], d["bq0"]),
                     (bv0[:, :], d["bv0"].partition_broadcast(P)),
                     (w1[0][:, :, :], d["w1_0"]), (w2[0][:, :, :, :], d["w2_0"])],
            "ld_1": [(wr[1][:, :], d["wr1"]), (br[1][:, :], d["br1"].partition_broadcast(P)),
                     (w1[1][:, :, :], d["w1_1"]), (w2[1][:, :, :], d["w2_1"]), (b1[1][:, :], d["b1_1"]),
                     (b2[1][:, :], d["b2_1"]), (wb1[:, :], d["wb1"]), (wc1[:, :], d["wc1"]), (bb1[:, :], d["bb1"]),
                     (bc1[:, :], d["bc1"]), (gam1[:, :], d["gam1"].partition_broadcast(P)),
                     (bet1[:, :], d["bet1"].partition_broadcast(P)), (llr1[:, :], d["llr1"])],
            "ld_3": [(wq3[:, :, :], d["wq3"]), (bq3[:, :], d["bq3"]), (bv3[:, :], d["bv3"].partition_broadcast(P)),
                     (wp3[:, :], d["wp3"]), (bp3[:, :], d["bp3"].partition_broadcast(P)), (wi3[:, :, :], d["wi3"])],
            "ld_2": [(wr[2][:, :], d["wr2"]), (br[2][:, :], d["br2"].partition_broadcast(P)),
                     (wq2[:, :, :], d["wq2"]), (w1[2][:, :, :], d["w1_2"]), (w2[2][:, :, :, :], d["w2_2"]),
                     (b1[2][:, :, :], d["b1_2"]), (b2[2][0:8, :], d["b2_2"])],
        }
        full = {k: 16 * len(v) for k, v in loads.items()}

        plans = {l: feed_forward_plan(l) for l in range(4)}

        SPLITTERS = {"pool": sorted(POOL_HEADS), "dve": sorted(set(range(H)) - POOL_HEADS)}

        def split_by(h):
            who = "pool" if h in POOL_HEADS else "dve"
            return who, SPLITTERS[who].index(h)

        def y_bank(layer, local):
            return (pY, pO)[local % Y_BANKS[layer]]

        def y_before(layer, turn, m):
            at = [local for kind, k, local in turn.steps if kind == "Y" and k == m]
            return turn.use("Y") + at[0] + 1

        def split_exp(eng, turn, h):
            who = split_by(h)[0]
            l = turn.layer
            at = [loc for kd, kk, loc in turn.steps if kd == "T" and kk == h][0]
            n = 3 * P if l == 3 else 2 * T
            eng.wait_ge(sem(f"L{l}_T_free"), PRIMED + turn.use("T") + at + 1)
            eng.tensor_tensor(pe16[:, 1, h % 4, 0:n], pe32[:, h % 4, 0:n], pe16[:, 0, h % 4, 0:n], ALU.subtract)\
               .then_inc(sem(f"L{l}_low_{who}"), 1)

        block = ctx.enter_context(nc.Block())

        @block.tensor
        def _(pe):
            pe.wait_ge(sem("ld_cst"), full["ld_cst"])

            def phase_a(l):
                s = lambda n: sem(f"L{l}_{n}")
                with pe.Fori(0, NT // 4 // 2) as turn:
                    i = turn * 2
                    for par in range(2):
                        pe.wait_ge(sem("xn_ready"), PRIMED + l * (NT // 4) + i + par + 1)
                        pe.wait_ge(sem("xts_ready"), PRIMED + l * (NT // 4) + i)
                        for u in range(4):
                            ins = pe.transpose(pS[:, par, u * P:(u + 1) * P], xn[:, par, u, :], ident[:, :])
                        ins.then_inc(sem("turned"), 1)
                    if l < 3:
                        for par in range(2):
                            pe.wait_ge(sem("xts_ready"), PRIMED + l * (NT // 4) + i + par + 1)
                            pe.wait_ge(sem("logits_copied"), PRIMED + l * (NT // 4) + i)
                            for u in range(4):
                                ins = pe.matmul(pT_[:, par, u * 16:u * 16 + EXPERTS[l]],
                                                xts[:, par, u * P:(u + 1) * P], wr[l][:, :], start=True, stop=True)
                            ins.then_inc(sem("logits"), 1)

            def search():
                with pe.Fori(0, SEARCH_BITS) as i:
                    pe.wait_ge(sem("counted"), PRIMED + i + 1)
                    pe.matmul(pT_[:, 0, 0:8], onesm[:, :], cnt[:, :], start=True, stop=True).then_inc(sem("summed"), 1)
                pe.wait_ge(sem("counted"), PRIMED + SEARCH_BITS + 1)
                pe.matmul(pT_[:, 0, 0:8], onesm[:, :], cnt[:, :], start=True, stop=True).then_inc(sem("summed"), 1)
                pe.wait_ge(sem("counted"), PRIMED + SEARCH_BITS + 2)
                pe.matmul(pS[:, 0, 0:8 * NT], tri[:, :], cmp_[:, :, :].rearrange("p e t -> p (e t)"),
                          start=True, stop=True)
                pe.matmul(pS[:, 1, 0:8 * NT], onesm[:, :], cmp_[:, :, :].rearrange("p e t -> p (e t)"),
                          start=True, stop=True).then_inc(sem("summed"), 1)

            def hidden(l, turn, k, use, s):
                pe.wait_ge(s("H_free"), PRIMED + use - (0 if l == 3 and k == 0 else 1))
                bank = pH[:, k % 2, :]
                for half in range(2):
                    if l == 3:
                        w = wf3[:, half, k * P:(k + 1) * P]
                    elif l == 1:
                        w = w1[1][:, 2 * k + half, :]
                    else:
                        f = 2 * (k % 2) + half
                        w = w1[l][:, k // 2, f * P:(f + 1) * P]
                    ins = pe.matmul(bank[:, half * T:(half + 1) * T], w, XT[:, bass.ts(turn.row(), T)],
                                    start=True, stop=True)
                ins.then_inc(s("H_full"), 1)

            def project(l, turn, m, use, local, s):
                need = plans[l][3]
                pe.wait_ge(s("H_free"), PRIMED + turn.use("H") + need[m] + 1)
                pe.wait_ge(s("Y_free"), PRIMED + use + 1 - Y_BANKS[l])
                yb = y_bank(l, local)
                if l == 1:
                    for half in range(2):
                        for c in range(2):
                            ins = pe.matmul(yb[:, half * T + c * P:half * T + (c + 1) * P],
                                            hb[:, m % 4, half * T + c * P:half * T + (c + 1) * P],
                                            w2[1][:, 2 * m + half, :], start=True, stop=True)
                else:
                    for c in range(2):
                        if l == 3:
                            parts = [(hb[:, f, c * P:(c + 1) * P], wf3[:, 2, f * P:(f + 1) * P]) for f in range(NHC)]
                        else:
                            parts = [(hb[:, (2 * m + f // 2) % 4, (f % 2) * T + c * P:(f % 2) * T + (c + 1) * P],
                                      w2[l][:, m, f, :]) for f in range(NF)]
                        for n, (lhs, rhs) in enumerate(parts):
                            ins = pe.matmul(yb[:, c * P:(c + 1) * P], lhs, rhs, start=(n == 0),
                                            stop=(n == len(parts) - 1))
                ins.then_inc(s("Y_full"), 1)

            def take_turn(turn):
                l, par, nxt = turn.layer, turn.par, 1 - turn.par
                s = lambda n: sem(f"L{l}_{n}")
                use_s, use_t, use_h, use_y, use_o = (turn.use(r) for r in "STHYO")
                for kind, k, local in turn.steps:
                    if RING.get(kind) == "S":
                        bank = pS[:, local % 2, :]
                        pe.wait_ge(s("S_free"), PRIMED + use_s + local - 1)
                    elif RING.get(kind) == "T":
                        bank = pT_[:, local % 2, :]
                        pe.wait_ge(s("T_free"), PRIMED + use_t + local - 1)
                    elif kind in "GBW":
                        yb = y_bank(l, local)
                        pe.wait_ge(s("Y_free"), PRIMED + use_y + local + (0 if kind == "B" else 1 - Y_BANKS[l]))

                    if kind == "H":
                        hidden(l, turn, k, use_h + local, s)
                    elif kind == "Y":
                        project(l, turn, k, use_y + local, local, s)
                    elif kind == "G":
                        pe.wait_ge(s("row_staged"), PRIMED + turn.row(1))
                        for c in range(2):
                            ins = pe.transpose(yb[0:16, c * P:(c + 1) * P], gst[:, par, c, :], ident[:, :])
                        ins.then_inc(s("Y_full"), 1)
                    elif kind == "B":
                        n = 16 if l == 1 else 8
                        for c in range(2):
                            ins = pe.matmul(yb[:, c * P:(c + 1) * P], gt[0:n, c * P:(c + 1) * P], b2[l][0:n, :],
                                            start=True, stop=True)
                        ins.then_inc(s("Y_full"), 1)
                    elif kind == "R":
                        pe.matmul(bank[:, 0:T], wb1[:, :], XT[:, bass.ts(turn.row(1), T)], start=True, stop=True)\
                          .then_inc(s("S_full"), 1)
                    elif kind == "Z":
                        pe.wait_ge(s("scanned"), PRIMED + turn.row(1))
                        pe.wait_ge(s("row_staged"), PRIMED + turn.row(1))
                        for c in range(2):
                            o = bank[:, c * P:(c + 1) * P]
                            pe.matmul(o, hT[:, c * P:(c + 1) * P], wc1[:, :], start=True, stop=False)
                            pe.matmul(o, xtb[:, par, c * P:(c + 1) * P], ident[:, :], start=False, stop=False)
                            ins = pe.matmul(o, onesr[:, :], bc1[:, :], start=False, stop=True)
                        ins.then_inc(s("S_full"), 1)
                    elif kind == "P":
                        w = {0: wq0, 2: wq2, 3: wq3}[l]
                        for n, which in enumerate({0: [2 * k, 2 * k + 1]}.get(l, [k])):
                            ins = pe.matmul(bank[:, n * T:(n + 1) * T], w[:, which, :],
                                            XT[:, bass.ts(turn.row(2), T)], start=True, stop=True)
                        ins.then_inc(s("S_full"), 1)
                    elif kind == "V":
                        pe.wait_ge(s("row_staged"), PRIMED + turn.row(2))
                        w = {0: wq0[:, 4, :], 2: wq2[:, 2, :], 3: wq3[:, 2, :]}[l]
                        pe.matmul(bank[:, 0:P], xtb[:, nxt, k * P:(k + 1) * P], w, start=True, stop=True)\
                          .then_inc(s("S_full"), 1)
                    elif kind == "K":
                        pe.wait_ge(s("qk_split"), PRIMED + turn.row(2))
                        for side in range(2):
                            o = bank[:, side * T:(side + 1) * T]
                            pe.matmul(o, selq[:, 2 * side, k, :], qk16[:, 0, side * T:(side + 1) * T],
                                      start=True, stop=False)
                            ins = pe.matmul(o, selq[:, 2 * side + 1, k, :], qk16[:, 1, side * T:(side + 1) * T],
                                            start=False, stop=(l != 3 and side == 0))
                            if l == 3:
                                ins = pe.matmul(o, alcol[:, side, k, :], alrow[:, :], start=False, stop=True)
                            elif side == 1:
                                ins = pe.matmul(o, onecol[:, :], alrow[:, :], start=False, stop=True)
                        ins.then_inc(s("T_full"), 1)
                    elif kind == "S":
                        g, j = k % NG, k // NG
                        rows = slice(32 * g, 32 * g + 32)
                        pe.wait_ge(s("T_free"), PRIMED + use_t + j + 1)
                        if l == 3:
                            pe.matmul(bank.rearrange("p (c n) -> p c n", c=2)[:, :, 0:P], identb[:, :],
                                      maskb[:, 0, None, :].to_broadcast([P, 2, P]), start=True, stop=True)
                            pe.matmul(bank[:, 0:P], stk[rows, nxt, j, 0:P], stk[rows, nxt, j, T:T + P],
                                      start=False, stop=True, skip_group_check=True)
                            ins = pe.matmul(bank[:, P:P + T], stk[rows, nxt, j, P:T], stk[rows, nxt, j, T:2 * T],
                                            start=False, stop=True, skip_group_check=True)
                        else:
                            for c in range(2):
                                ins = pe.matmul(bank[:, c * T:(c + 1) * T], stk[rows, nxt, j, c * P:(c + 1) * P],
                                                stk[rows, nxt, j, T:2 * T], start=True, stop=True)
                        ins.then_inc(s("S_full"), 1)
                    elif kind == "M":
                        pe.wait_ge(s("S_free"), PRIMED + use_s + local - k)
                        for j in range(NJ):
                            ins = pe.transpose(bank[:, j * P:(j + 1) * P], mx[:, k, j, :], ident[:, :])
                        ins.then_inc(s("S_full"), 1)
                    elif kind == "T":
                        g, j = k % NG, k // NG
                        rows = slice(32 * g, 32 * g + 32)
                        pe.wait_ge(s("S_free"), PRIMED + use_s)
                        if l == 3:
                            pe.matmul(bank.rearrange("p (c n) -> p c n", c=2)[:, :, 0:P], identb[:, :],
                                      maskb[:, 1, None, :].to_broadcast([P, 2, P]), start=True, stop=True)
                            for o, q0, q1 in ((0, 0, T), (T, P, T)):
                                kc = q0 // P
                                ins = pe.matmul(bank[:, o:o + q1 - q0], stk[rows, par, j, T + kc * P:T + (kc + 1) * P],
                                                stk[rows, par, j, q0:q1], start=False, stop=True,
                                                skip_group_check=True)
                        else:
                            for c in range(2):
                                ins = pe.matmul(bank[:, c * T:(c + 1) * T],
                                                stk[rows, par, j, T + c * P:T + (c + 1) * P],
                                                stk[rows, par, j, 0:T], start=True, stop=True)
                        ins.then_inc(s("T_full"), 1)
                    elif kind == "O":
                        who, nth = split_by(k)
                        pe.wait_ge(s(f"low_{who}"), PRIMED + turn.count(len(SPLITTERS[who]), nth + 1))
                        pe.wait_ge(s("v_split"), PRIMED + turn.row(1))
                        pe.wait_ge(s("out_read"), PRIMED + turn.row())
                        for c in range(2):
                            kcs = [0] if (l == 3 and c == 0) else [0, 1]
                            parts = [(kc, e, v) for kc in kcs for e, v in ((0, 0), (0, 1), (1, 0))]
                            for n, (kc, e, v) in enumerate(parts):
                                col = kc * T + (0 if (l == 3 and kc == 1) else c * P)
                                ins = pe.matmul(po[:, c, k, :], pe16[:, e, k % 4, col:col + P],
                                                va[:, par, v, kc, k, :], start=(n == 0), stop=(n == len(parts) - 1))
                        ins.then_inc(s("O_full"), 1)
                    elif kind == "Q":
                        pe.wait_ge(s("out_read"), PRIMED + turn.row())
                        pe.transpose(bank[:, 0:P], ob[:, k, :], ident[:, :]).then_inc(s("T_full"), 1)
                    elif kind == "W":
                        at = [loc for kd, kk, loc in turn.steps if kd == "Q" and kk == 1][0]
                        pe.wait_ge(s("T_free"), PRIMED + use_t + at + 1)
                        for c in range(2):
                            ins = pe.matmul(yb[:, c * P:(c + 1) * P], oT[:, c * P:(c + 1) * P], wp3[:, :],
                                            start=True, stop=True)
                        ins.then_inc(s("Y_full"), 1)

            for l in range(4):
                pe.wait_ge(sem(f"ld_{l}"), full[f"ld_{l}"])
                phase_a(l)
                if l == 0:
                    search()
                if l == 3:
                    pe.wait_ge(sem("w3_ready"), 3)
                pe.wait_ge(sem("xt_copied"), PRIMED + (l + 1) * (NT // 4))
                if l < 3:
                    pe.wait_ge(sem("gates"), PRIMED + l + 1)
                run_turns(pe, l, take_turn)

        @block.scalar
        def _(act):
            def phase_a(l):
                s = lambda n: sem(f"L{l}_{n}")
                with act.Fori(0, NT // 4 // 2) as turn:
                    i = turn * 2
                    for par in range(2):
                        act.wait_ge(sem("turned"), PRIMED + l * (NT // 4) + i + par + 1)
                        act.wait_ge(sem("xt_copied"), PRIMED + l * (NT // 4) + i)
                        if l < 3:
                            act.wait_ge(sem("logits"), PRIMED + l * (NT // 4) + i)
                        act.activation(xts[:, par, :], pS[:, par, :], ACT.Copy).then_inc(sem("xts_ready"), 1)
                    if l < 3:
                        for par in range(2):
                            act.wait_ge(sem("logits"), PRIMED + l * (NT // 4) + i + par + 1)
                            act.activation(LG[:, bass.ds((i + par) * 4, 4), 0:EXPERTS[l]],
                                           pT_[:, par, 0:64].rearrange("p (u e) -> p u e", e=16)[:, :, 0:EXPERTS[l]],
                                           ACT.Copy).then_inc(sem("logits_copied"), 1)

            def take_turn(turn):
                l, par, nxt = turn.layer, turn.par, 1 - turn.par
                s = lambda n: sem(f"L{l}_{n}")
                use_t, use_h, use_o = (turn.use(r) for r in "THO")
                for kind, k, local in turn.steps:
                    if RING.get(kind) == "T":
                        bank = pT_[:, local % 2, :]
                        act.wait_ge(s("T_full"), PRIMED + use_t + local + 1)
                    if kind == "H":
                        act.wait_ge(s("H_full"), PRIMED + use_h + local + 1)
                        bank = pH[:, k % 2, :]
                        if l == 3:
                            act.wait_ge(s("H_free"), PRIMED + use_h + local - (0 if k == 0 else 1))
                            act.activation(th[:, k % 2, :], bank[:, 0:T], ACT.Tanh, scale=0.5)\
                               .then_inc(s("tanh_done"), 1)
                            continue
                        done = k // 2 - 2 if l != 1 else k - 4
                        if done >= 0:
                            act.wait_ge(s("Y_full"), PRIMED + y_before(l, turn, done))
                        else:
                            act.wait_ge(s("Y_full"), PRIMED + turn.use("Y"))
                        if l == 0:
                            act.activation(hb[:, k % 4, :], bank, ACT.Relu).then_inc(s("H_free"), 1)
                        else:
                            for half in range(2):
                                bias = b1[1][:, 2 * k + half:2 * k + half + 1] if l == 1 else \
                                    b1[2][:, k // 2, 2 * (k % 2) + half:2 * (k % 2) + half + 1]
                                ins = act.activation(hb[:, k % 4, half * T:(half + 1) * T],
                                                     bank[:, half * T:(half + 1) * T], ACT.Relu, bias=bias)
                            ins.then_inc(s("H_free"), 1)
                    elif kind == "K":
                        act.activation(stk[:, nxt, k, :], bank, ACT.Copy).then_inc(s("T_free"), 1)
                    elif kind == "T":
                        act.wait_ge(s("O_full"), PRIMED + use_o + k - 2)
                        n = 3 * P if l == 3 else 2 * T
                        act.activation(pe32[:, k % 4, 0:n], bank[:, 0:n], ACT.Exp)
                        act.activation(pe16[:, 0, k % 4, 0:n], bank[:, 0:n], ACT.Exp).then_inc(s("T_free"), 1)
                    elif kind == "Q":
                        act.wait_ge(s("Y_full"), PRIMED + turn.use("Y"))
                        act.activation(oT[:, k * P:(k + 1) * P], bank[:, 0:P], ACT.Copy).then_inc(s("T_free"), 1)

            for l in range(4):
                if l < 3:
                    phase_a(l)
                    act.wait_ge(sem("shifted"), PRIMED + l + 1)
                    act.activation(pr[:, :, 0:EXPERTS[l]], ra[:, :, 0:EXPERTS[l]], ACT.Exp)\
                       .then_inc(sem("exp_logits"), 1)
                else:
                    phase_a(l)
                if l == 1:
                    act.wait_ge(sem("ld_1"), full["ld_1"])
                    act.activation(lamt[:, :], llr1[:, :], ACT.Tanh, scale=0.5).then_inc(sem("lam_tanh"), 1)
                run_turns(act, l, take_turn)

        @block.gpsimd
        def _(pool):
            chain = Chain(pool, sem("pool_chain"))
            pool.wait_ge(sem("ld_cst"), full["ld_cst"])
            for l in range(4):
                s = lambda n: sem(f"L{l}_{n}")
                if l == 3:
                    pool.wait_ge(sem("ld_3"), full["ld_3"])
                    for n in range(3):
                        pool.tensor_scalar(wf3[:, n, :], wi3[:, n, :], 1.0 / 127.0, None, ALU.mult)\
                            .then_inc(sem("w3_ready"), 1)
                pool.wait_ge(sem("stats"), PRIMED + l + 1)
                chain.link(pool.tensor_scalar(vare[:, :], MV[:, :, 1], EPS, None, ALU.add))
                pool.tensor_tensor(rstd[:, :], vare[:, :], neghalf[:, :], ALU.pow).then_inc(sem("rstd"), 1)
                with pool.Fori(0, NT // 4 // 2) as turn:
                    i = turn * 2
                    for par in range(2):
                        pool.wait_ge(sem("xts_ready"), PRIMED + l * (NT // 4) + i + par + 1)
                        settle(pool, sem("pool_settled"))
                        pool.tensor_copy(XT[:, bass.ts(i + par, 4 * P)], xts[:, par, :]).then_inc(sem("xt_copied"), 1)
                pool.wait_ge(sem("xt_copied"), PRIMED + (l + 1) * (NT // 4))
                if l < 3:
                    pool.wait_ge(sem("gates"), PRIMED + l + 1)
                split = TurnChain(pool, sem(f"L{l}_pool_chain"))

                def stage(turn, par):
                    pool.wait_ge(s("x_final"), PRIMED + turn.row())
                    settle(pool, sem("pool_settled"))
                    if l < 3:
                        split.link(pool.tensor_copy(gst[:, par, :, :], GA[:, bass.ds(turn.count(2, 2), 2), :]))
                        settle(pool, sem("pool_settled"))
                    pool.tensor_copy(xtb[:, par, :], XT[:, bass.ts(turn.row(1), T)]).then_inc(s("row_staged"), 1)

                def take_turn(turn):
                    split.enter(turn)
                    if 0 <= turn.n + 1 < B:
                        stage(turn, 1 - turn.par)
                    for kind, k, local in turn.steps:
                        if kind == "P" and k == 1:
                            pool.wait_ge(s("S_free"), PRIMED + turn.use("S") + local + 1)
                            settle(pool, sem("pool_settled"))
                            if l == 0:
                                split.link(pool.tensor_tensor(qkf[:, 0, :], qkf[:, 0, :], qkf[:, 1, :], ALU.add))
                                settle(pool, sem("pool_settled"))
                            split.link(pool.tensor_copy(qk16[:, 0, :], qkf[:, 0, :]))
                            pool.tensor_tensor(qk16[:, 1, :], qkf[:, 0, :], qk16[:, 0, :], ALU.subtract)\
                                .then_inc(s("qk_split"), 1)
                        elif kind == "V" and k == 1:
                            pool.wait_ge(s("S_free"), PRIMED + turn.use("S") + local + 1)
                            settle(pool, sem("pool_settled"))
                            src = v32[:, :, :].rearrange("p c (h e) -> p c h e", h=H)
                            hi, lo = (va[:, 1 - turn.par, v, :, :, 0:DH] for v in range(2))
                            split.link(pool.tensor_copy(hi, src))
                            pool.tensor_tensor(lo, src, hi, ALU.subtract).then_inc(s("v_split"), 1)
                        elif kind == "D" and k in POOL_HEADS:
                            split_exp(pool, turn, k)
                        elif kind == "Z":
                            pool.wait_ge(s("z_stats"), PRIMED + turn.row(1))
                            settle(pool, sem("pool_settled"))
                            split.link(pool.tensor_scalar(zve[:, :], zmv[:, :, 1], EPS, None, ALU.add))
                            pool.tensor_tensor(zr[:, :], zve[:, :], neghalf[:, 0:2], ALU.pow).then_inc(s("z_rstd"), 1)
                    split.leave()

                run_turns(pool, l, take_turn)

        @block.vector
        def _(dve):
            chain = Chain(dve, sem("dve_chain"))
            dve.wait_ge(sem("ld_cst"), full["ld_cst"])
            dve.wait_ge(sem("ld_x"), full["ld_x"])
            chain.link(dve.memset(va[:, :, 0, :, :, DH:DH + 1], 1.0))
            chain.link(dve.memset(va[:, :, 1, :, :, DH:DH + 1], 0.0))
            chain.link(dve.memset(mx[:, :, :, :], 0.0))
            chain.link(dve.memset(GA[:, :, :], 0.0))
            chain.link(dve.memset(gst[:, :, :, :], 0.0))

            def statistics(l):
                s = lambda n: sem(f"L{l}_{n}")
                with dve.Fori(0, NT // 4) as turn:
                    i = turn * 4
                    for u in range(4):
                        dve.bn_stats(st6[:, u, :], X[:, i + u, :]).then_inc(sem("bn"), 1)
                    dve.wait_ge(sem("bn"), PRIMED + l * (NT) + i + 4)
                    settle(dve, sem("dve_settled"))
                    for u in range(4):
                        ins = dve.bn_aggr(mv4[:, u, :], st6[:, u, :])
                    ins.then_inc(sem("aggr"), 1)
                    dve.wait_ge(sem("aggr"), PRIMED + l * (NT // 4) + turn + 1)
                    settle(dve, sem("dve_settled"))
                    dve.tensor_copy(MV[:, bass.ds(i, 4), :], mv4[:, :, :]).then_inc(sem("stats_kept"), 1)
                dve.wait_ge(sem("stats_kept"), PRIMED + l * (NT // 4) + NT // 4)
                dve.sem_inc(sem("stats"), 1)

            def phase_a(l):
                s = lambda n: sem(f"L{l}_{n}")
                statistics(l)
                dve.wait_ge(sem("rstd"), PRIMED + l + 1)
                with dve.Fori(0, NT // 4 // 2) as turn:
                    i = turn * 2
                    for par in range(2):
                        dve.wait_ge(sem("turned"), PRIMED + l * (NT // 4) + i)
                        for u in range(4):
                            t = (i + par) * 4 + u
                            ins = dve.tensor_scalar(xn[:, par, u, :], X[:, t, :], MV[:, t, 0:1],
                                                    rstd[:, bass.ds(t, 1)], ALU.subtract, ALU.mult)
                        ins.then_inc(sem("xn_ready"), 1)

            def routing(l):
                s = lambda n: sem(f"L{l}_{n}")
                n = EXPERTS[l]
                full_e = lambda a: a[:, :, None].to_broadcast([P, NT, n])
                lg, p_, a_, b_, c_, g_, k_ = (x[:, :, 0:n] for x in (LG, pr, ra, rb, rc, GA, rank))
                dve.wait_ge(sem(f"ld_{l}"), full[f"ld_{l}"])
                dve.wait_ge(sem("logits_copied"), PRIMED + l * (NT // 4) + NT // 4)
                if l > 0:
                    chain.link(dve.tensor_tensor(lg, lg, br[l][:, None, :].to_broadcast([P, NT, n]), ALU.add))
                chain.link(dve.tensor_reduce(r1[:, :], lg, AX.X, ALU.max))
                dve.tensor_tensor(a_, lg, full_e(r1), ALU.subtract).then_inc(sem("shifted"), 1)
                dve.wait_ge(sem("exp_logits"), PRIMED + l + 1)
                chain.link(dve.tensor_reduce(r1[:, :], p_, AX.X, ALU.add))
                chain.link(dve.reciprocal(r2[:, :], r1[:, :]))
                chain.link(dve.tensor_tensor(p_, p_, full_e(r2), ALU.mult))
                for k in range(TOPK[l]):
                    chain.link(dve.tensor_reduce(r1[:, :], p_, AX.X, ALU.max))
                    chain.link(dve.tensor_tensor(a_, p_, full_e(r1), ALU.is_ge))
                    chain.link(dve.tensor_tensor(a_, a_, k_, ALU.mult))
                    chain.link(dve.tensor_reduce(r2[:, :], a_, AX.X, ALU.max))
                    chain.link(dve.tensor_tensor(b_, k_, full_e(r2), ALU.is_equal))
                    if k == 0:
                        chain.link(dve.tensor_tensor(g_, p_, b_, ALU.mult))
                    else:
                        chain.link(dve.tensor_tensor(c_, p_, b_, ALU.mult))
                        chain.link(dve.tensor_tensor(g_, g_, c_, ALU.add))
                    if k < TOPK[l] - 1 or l == 0:
                        chain.link(dve.scalar_tensor_tensor(p_, b_, -2.0, p_, ALU.mult, ALU.add))
                if l == 1:
                    chain.link(dve.memset(GA[:, :, 15:16], 1.0))
                if l == 0:
                    capacity()
                dve.sem_inc(sem("gates"), 1)

            def capacity():
                e_t = lambda a: a[:, :, None].to_broadcast([P, 8, NT])
                flat = lambda a: a.rearrange("p e t -> p (e t)")
                g_ = GA[:, :, 0:8].rearrange("p t e -> p e t")
                p_ = pr[:, :, 0:8].rearrange("p t e -> p e t")
                chain.link(dve.tensor_scalar(key[:, :, :], p_, 0.0, None, ALU.is_ge))
                chain.link(dve.tensor_tensor(key[:, :, :], g_, key[:, :, :], ALU.subtract))
                chain.link(dve.memset(thr[:, :], 0))
                chain.link(dve.tensor_copy(biti[:, :], bitf[:, :]))
                with dve.Fori(0, SEARCH_BITS) as i:
                    rc_ = LoopChain(dve, sem("search_chain"), 7)
                    rc_.enter(i)
                    rc_.link(dve.tensor_tensor(cand[:, :], thr[:, :], biti[:, :], ALU.bitwise_or))
                    rc_.link(dve.tensor_tensor(cmp_[:, :, :], key[:, :, :], e_t(cand[:, :].bitcast(F32)), ALU.is_ge))
                    dve.tensor_reduce(cnt[:, :], cmp_[:, :, :], AX.X, ALU.add).then_inc(sem("counted"), 1)
                    dve.wait_ge(sem("summed"), PRIMED + i + 1)
                    rc_.link(dve.tensor_scalar(left[:, :], pT_[:, 0, 0:8], float(CAP), None, ALU.is_ge))
                    rc_.link(dve.tensor_tensor(addb[:, :], left[:, :], bitf[:, :], ALU.mult))
                    rc_.link(dve.tensor_tensor(thr[:, :], thr[:, :], addb[:, :], ALU.bitwise_or))
                    rc_.link(dve.tensor_scalar(bitf[:, :], bitf[:, :], 0.5, None, ALU.mult))
                    rc_.link(dve.tensor_copy(biti[:, :], bitf[:, :]))
                    rc_.leave()
                thf = e_t(thr[:, :].bitcast(F32))
                chain.link(dve.tensor_tensor(cmp_[:, :, :], key[:, :, :], thf, ALU.is_gt))
                dve.tensor_reduce(cnt[:, :], cmp_[:, :, :], AX.X, ALU.add).then_inc(sem("counted"), 1)
                dve.wait_ge(sem("summed"), PRIMED + SEARCH_BITS + 1)
                chain.link(dve.tensor_scalar(left[:, :], pT_[:, 0, 0:8], -1.0, float(CAP), ALU.mult, ALU.add))
                chain.link(dve.tensor_copy(scan[:, :, :], cmp_[:, :, :]))
                dve.tensor_tensor(cmp_[:, :, :], key[:, :, :], thf, ALU.is_equal).then_inc(sem("counted"), 1)
                dve.wait_ge(sem("counted"), PRIMED + SEARCH_BITS + 2)
                dve.wait_ge(sem("summed"), PRIMED + SEARCH_BITS + 2)
                before = rb[:, :, :].rearrange("p t e -> p (t e)")[:, 0:8 * NT].rearrange("p (e t) -> p e t", e=8)
                tot = rc[:, :, :].rearrange("p t e -> p (t e)")[:, 0:8 * NT].rearrange("p (e t) -> p e t", e=8)
                chain.link(dve.tensor_copy(flat(tot), pS[:, 1, 0:8 * NT]))
                for e in range(8):
                    ins = dve.tensor_tensor_scan(before[:, e, :], onesm[:, 0:NT], tot[:, e, :], 0.0, ALU.mult, ALU.add)
                    m = chain.mark(ins)
                chain.wait(m)
                chain.link(dve.tensor_tensor(flat(before), flat(before), flat(tot), ALU.subtract))
                chain.link(dve.tensor_tensor(flat(before), flat(before), pS[:, 0, 0:8 * NT], ALU.add))
                chain.link(dve.tensor_tensor(before, before, e_t(left[:, :]), ALU.is_lt))
                chain.link(dve.tensor_tensor(before, before, cmp_[:, :, :], ALU.mult))
                chain.link(dve.tensor_tensor(before, before, scan[:, :, :], ALU.add))
                chain.link(dve.tensor_tensor(g_, g_, before, ALU.mult))

            def take_turn(turn, tc):
                l, par, nxt = turn.layer, turn.par, 1 - turn.par
                s = lambda n: sem(f"L{l}_{n}")
                use_s, use_h, use_y, use_o = (turn.use(r) for r in "SHYO")
                tc.enter(turn)
                xt = lambda c: X[:, turn.count(2, c), :]
                x2 = X[:, bass.ds(turn.count(2, 0), 2), :] if 0 <= turn.n < B else None
                both = lambda a: a.rearrange("p (c e) -> p c e", c=2)
                last_x = [None, None, None]

                def before_x(c=None):
                    m = last_x[2 if c is None else c]
                    if m is not None:
                        tc.wait(m)

                def wrote_x(ins):
                    last_x[:] = [tc.mark(ins)] * 3

                for kind, k, local in turn.steps:
                    if RING.get(kind) == "S":
                        bank = pS[:, local % 2, :]
                        dve.wait_ge(s("S_full"), PRIMED + use_s + local + 1)
                    elif RING.get(kind) == "Y":
                        yb = y_bank(l, local)
                        dve.wait_ge(s("Y_full"), PRIMED + use_y + local + 1)

                    if kind == "P":
                        dve.wait_ge(s("qk_split"), PRIMED + turn.row(2))
                        side = slice(k * T, (k + 1) * T)
                        if l == 0:
                            for half in range(2):
                                ins = dve.scalar_tensor_tensor(
                                    qkf[:, half, side], bank[:, half * T:(half + 1) * T],
                                    bq0[:, 2 * k + half:2 * k + half + 1], rope0[:, 2 * k + half, :],
                                    ALU.add, ALU.mult)
                        elif l == 2:
                            ins = dve.tensor_scalar(qkf[:, 0, side], bank[:, 0:T],
                                                    rope2[:, k, bass.ds(turn.row(2), 1)], None, ALU.mult)
                        else:
                            ins = dve.tensor_scalar(qkf[:, 0, side], bank[:, 0:T], bq3[:, k:k + 1],
                                                    QSCALE if k == 0 else 1.0, ALU.add, ALU.mult)
                        ins.then_inc(s("S_free"), 1)
                    elif kind == "V":
                        dve.wait_ge(s("v_split"), PRIMED + turn.row(1))
                        if l == 2:
                            ins = dve.tensor_copy(v32[:, k, :], bank[:, 0:P])
                        else:
                            ins = dve.tensor_tensor(v32[:, k, :], bank[:, 0:P], (bv0 if l == 0 else bv3)[:, :], ALU.add)
                        ins.then_inc(s("S_free"), 1)
                    elif kind == "D" and k not in POOL_HEADS:
                        split_exp(dve, turn, k)
                    elif kind == "S":
                        j, col = k // NG, 32 * (k % NG) + MAXROW
                        if l == 3:
                            dve.tensor_reduce(mx[:, 0, j, col:col + 1], bank[:, 0:P], AX.X, ALU.max)
                            ins = dve.tensor_reduce(mx[:, 1, j, col:col + 1], bank[:, P:P + T], AX.X, ALU.max)
                        else:
                            ins = dve.tensor_reduce(mx[:, :, j, col], bank.rearrange("p (c n) -> p c n", c=2),
                                                    AX.X, ALU.max)
                        ins.then_inc(s("S_free"), 1)
                    elif kind == "M":
                        q = stk[:, nxt, :, k * P:(k + 1) * P]
                        dve.scalar_tensor_tensor(q, bank.rearrange("p (j n) -> p j n", j=NJ), -1.0, q,
                                                 ALU.mult, ALU.add).then_inc(s("S_free"), 1)
                    elif kind == "G":
                        dve.tensor_copy(gt[:, :], yb[0:16, 0:T]).then_inc(s("Y_free"), 1)
                    elif kind == "B":
                        wrote_x(dve.tensor_tensor(x2, x2, both(yb[:, 0:2 * P]), ALU.add))
                        before_x()
                        dve.sem_inc(s("Y_free"), 1)
                    elif kind == "Y":
                        if l == 3:
                            before_x()
                            wrote_x(dve.tensor_tensor(x2, x2, both(yb[:, 0:2 * P]), ALU.add))
                        else:
                            if k == 0:
                                dve.wait_ge(s("row_staged"), PRIMED + turn.row(1))
                            for half in range(2 if l == 1 else 1):
                                e = 2 * k + half if l == 1 else k
                                for c in range(2):
                                    o = half * T + c * P
                                    before_x(c)
                                    last_x[c] = last_x[2] = tc.mark(dve.scalar_tensor_tensor(
                                        xt(c), yb[:, o:o + P], gst[:, par, c, e:e + 1], xt(c), ALU.mult, ALU.add))
                        before_x()
                        dve.sem_inc(s("Y_free"), 1)
                    elif kind == "H" and l == 3:
                        dve.wait_ge(s("tanh_done"), PRIMED + use_h + local + 1)
                        dve.wait_ge(s("Y_full"), PRIMED + use_y)
                        tc.link(dve.scalar_tensor_tensor(hg[:, k % 2, :], th[:, k % 2, :], 1.0, pH[:, k % 2, 0:T],
                                                         ALU.add, ALU.mult))
                        dve.scalar_tensor_tensor(hb[:, k, 0:T], hg[:, k % 2, :], 0.5, pH[:, k % 2, T:2 * T],
                                                 ALU.mult, ALU.mult).then_inc(s("H_free"), 1)
                    elif kind == "R":
                        tc.link(dve.tensor_scalar(vals[:, :], bank[:, 0:T], bb1[:, 0:1], oml[:, 0:1],
                                                  ALU.add, ALU.mult))
                        dve.sem_inc(s("S_free"), 1)
                        dve.tensor_tensor_scan(hT[:, :], lamrow[:, :], vals[:, :], 0.0, ALU.mult, ALU.add)\
                           .then_inc(s("scanned"), 1)
                    elif kind == "Z":
                        z_bank = bank
                        for c in range(2):
                            m = tc.mark(dve.bn_stats(zs[:, c, :], z_bank[:, c * P:(c + 1) * P]))
                        tc.wait(m)
                        settle(dve, sem("dve_settled"))
                        for c in range(2):
                            m = tc.mark(dve.bn_aggr(zmv[:, c, :], zs[:, c, :]))
                        tc.wait(m)
                        dve.sem_inc(s("z_stats"), 1)
                    elif kind == "N" and l == 1:
                        dve.wait_ge(s("z_rstd"), PRIMED + turn.row(1))
                        for c in range(2):
                            m = tc.mark(dve.tensor_scalar(zn[:, c, :], z_bank[:, c * P:(c + 1) * P],
                                                          zmv[:, c, 0:1], zr[:, c:c + 1], ALU.subtract, ALU.mult))
                        tc.wait(m)
                        dve.sem_inc(s("S_free"), 1)
                        wide = lambda a: a[:, None, :].to_broadcast([P, 2, P])
                        tc.link(dve.tensor_tensor(zg[:, :, :], zn[:, :, :], wide(gam1), ALU.mult))
                        tc.link(dve.tensor_tensor(zn[:, :, :], zg[:, :, :], wide(bet1), ALU.add))
                        before_x()
                        wrote_x(dve.tensor_tensor(x2, x2, zn[:, :, :], ALU.add))
                    elif kind == "N":
                        dve.wait_ge(s("O_full"), PRIMED + use_o + H)
                        tc.link(dve.reciprocal(rden[:, :, :], po[:, :, :, DH]))
                        for c in range(2):
                            m = tc.mark(dve.tensor_tensor(ob[:, c, :].rearrange("p (h e) -> p h e", h=H),
                                                          po[:, c, :, 0:DH],
                                                          rden[:, c, :, None].to_broadcast([P, H, DH]), ALU.mult))
                        tc.wait(m)
                        dve.sem_inc(s("out_read"), 1)
                        before_x()
                        add = bp3[:, None, :].to_broadcast([P, 2, P]) if l == 3 else ob[:, :, :]
                        wrote_x(dve.tensor_tensor(x2, x2, add, ALU.add))
                    elif kind == "W":
                        xb = X[:, bass.ds(turn.count(2, -2), 2), :]
                        tc.link(dve.tensor_tensor(xb, xb, both(yb[:, 0:2 * P]), ALU.add))
                        dve.sem_inc(s("Y_free"), 1)
                        dve.sem_inc(s("x_final"), 1)
                    elif kind == "E":
                        before_x()
                        if l != 3:
                            dve.sem_inc(s("x_final"), 1)
                tc.leave()

            for l in range(4):
                phase_a(l)
                if l < 3:
                    routing(l)
                if l == 1:
                    dve.wait_ge(sem("lam_tanh"), 1)
                    chain.link(dve.tensor_scalar(lam1[:, :], lamt[:, :], 0.5, 0.5, ALU.mult, ALU.add))
                    chain.link(dve.tensor_scalar(oml[:, :], lamt[:, :], -0.5, 0.5, ALU.mult, ALU.add))
                    chain.link(dve.tensor_copy(lamrow[:, :], lam1[:, :].to_broadcast([P, T])))
                tc = TurnChain(dve, sem(f"L{l}_dve_chain"))
                run_turns(dve, l, lambda turn: take_turn(turn, tc))
                dve.wait_ge(sem(f"L{l}_x_final"), PRIMED + B)

        primed = [n for n in sems if n in SHARED_SIGNALS or (n.startswith("L") and not n.endswith("_chain"))]

        @block.sync
        def _(sp):
            for name in primed:
                sp.sem_inc(sem(name), PRIMED)
            for group, moves in loads.items():
                for n, (dst, src) in enumerate(moves):
                    if group == "ld_2" and n == 0:
                        sp.wait_ge(sem("L0_x_final"), PRIMED + B)
                    sp.dma_start(dst, src).then_inc(sem(group), 16)
            for c in range(4):
                sp.wait_ge(sem("L3_x_final"), PRIMED + 4 * c + 4)
                sp.dma_start(xout[:, 8 * c:8 * c + 8, :], X[:, 8 * c:8 * c + 8, :]).then_inc(sem("stored"), 16)
            sp.wait_ge(sem("stored"), 64)


def shape_constants():
    c = {}
    f = np.float32
    c["c_ident"] = np.eye(P, dtype=f)
    c["c_ones"] = np.ones((P, P), f)
    c["c_neghalf"] = np.full((P, NT), -0.5, f)
    c["c_tri"] = np.triu(np.ones((P, P), f), 1)
    c["c_rank"] = np.broadcast_to(16.0 - np.arange(16, dtype=f), (P, NT, 16)).copy()
    c["c_bitf"] = np.full((P, 8), 2.0 ** (SEARCH_BITS - 1), f)
    sel = np.zeros((P, 4, NJ, P), np.float16)
    for j in range(NJ):
        for g in range(NG):
            for e in range(DH):
                src = (NG * j + g) * DH + e
                for which, rs in ((0, (0, 1)), (1, (2,)), (2, (0, 2)), (3, (1,))):
                    for r in rs:
                        sel[src, which, j, 32 * g + DH * r + e] = 1
    c["c_selq"] = sel
    one = np.zeros((2, P), np.float16)
    one[0, MAXROW::32] = 1
    c["c_onecol"] = one
    al = np.zeros((2, 2, NJ, P), np.float16)
    for j in range(NJ):
        for g in range(NG):
            slope = 2.0 ** -(NG * j + g + 1)
            al[0, 0, j, 32 * g + 24] = slope * 256
            al[1, 1, j, 32 * g + 24] = 1
            al[1, 0, j, 32 * g + 25] = 1
            al[0, 1, j, 32 * g + 25] = -slope * 256
    al[0, 1, :, MAXROW::32] = 1
    c["c_alcol"] = al
    c["c_alrow"] = np.stack([np.ones(T), np.arange(T) / 256.0]).astype(np.float16)
    m = np.where(np.arange(P)[None, :] > np.arange(P)[:, None], -1e30, 0.0).astype(f)
    c["c_mask"] = np.stack([m, m.T], axis=1)
    c["c_identb"] = np.eye(P, dtype=f)
    freqs = (f(1.0) / np.power(f(10000.0), np.arange(0, DH, 2, dtype=f) / f(DH))).astype(f)
    ang = np.arange(T, dtype=f)[:, None] * freqs[None, :]
    cos, sin = np.cos(ang).astype(f), np.sin(ang).astype(f)
    e = np.arange(P) % DH
    cs = cos[:, e // 2].T
    sn = (sin[:, e // 2] * np.where(e % 2 == 0, -1.0, 1.0).astype(f)).T
    c["c_rope0"] = np.stack([cs * f(QSCALE), sn * f(QSCALE), cs, sn], axis=1).astype(f)
    ang2 = np.arange(B, dtype=f)[:, None] * freqs[None, :]
    ang2 = np.concatenate([ang2, ang2], axis=-1)
    r2 = np.cos(ang2) + np.sin(ang2) * np.where(np.arange(DH) < DH // 2, 1.0, -1.0)
    r2 = r2[:, e].T.astype(f)
    c["c_rope2"] = np.stack([r2 * f(QSCALE), r2], axis=1).astype(f)
    return {k: np.ascontiguousarray(v) for k, v in c.items()}


def lay_out(i):
    a = {k: np.asarray(v) for k, v in i.items()}
    o = {}
    swap = np.arange(P) ^ 1
    o["x"] = a["L0_attn_x"].reshape(B * T, P)
    wt = a["L0_attn_W_qkv"].T
    q, k, v = wt[:, 0:P], wt[:, P:2 * P], wt[:, 2 * P:]
    o["wq0"] = np.stack([q, q[:, swap], k, k[:, swap], v], axis=1)
    bq, bk = a["L0_attn_b_qkv"][0:P], a["L0_attn_b_qkv"][P:2 * P]
    o["bq0"] = np.stack([bq, bq[swap], bk, bk[swap]], axis=1)
    o["bv0"] = a["L0_attn_b_qkv"][2 * P:]
    o["wr0"] = a["L0_ffn_Wr"]
    o["w1_0"] = a["L0_ffn_W1"].transpose(1, 0, 2)
    o["w2_0"] = a["L0_ffn_W2"].reshape(8, NF, P, P).transpose(2, 0, 1, 3)
    o["wr1"], o["br1"] = a["L1_ffn_router_W"], a["L1_ffn_router_b"]
    o["w1_1"] = np.concatenate([a["L1_ffn_eW1"], a["L1_ffn_sW1"][None]]).transpose(1, 0, 2)
    o["w2_1"] = np.concatenate([a["L1_ffn_eW2"], a["L1_ffn_sW2"][None]]).transpose(1, 0, 2)
    o["b1_1"] = np.concatenate([a["L1_ffn_eb1"], a["L1_ffn_sb1"][None]]).T
    o["b2_1"] = np.concatenate([a["L1_ffn_eb2"], a["L1_ffn_sb2"][None]])
    o["wb1"], o["wc1"] = a["L1_attn_Wb"].T, a["L1_attn_Wc"].T
    o["bb1"], o["bc1"] = a["L1_attn_bb"].reshape(P, 1), a["L1_attn_bc"].reshape(1, P)
    o["gam1"], o["bet1"] = a["L1_attn_gamma"], a["L1_attn_beta"]
    o["llr1"] = a["L1_attn_log_lambda_raw"].reshape(P, 1)
    o["wq2"] = np.stack([a["L2_attn_Wq"].T, a["L2_attn_Wk"].T, a["L2_attn_Wv"].T], axis=1)
    o["wr2"], o["br2"] = a["L2_ffn_Wr"], a["L2_ffn_br"]
    o["w1_2"] = a["L2_ffn_W1"].transpose(1, 0, 2)
    o["w2_2"] = a["L2_ffn_W2"].reshape(8, NF, P, P).transpose(2, 0, 1, 3)
    o["b1_2"] = a["L2_ffn_b1"].reshape(8, NF, P).transpose(2, 0, 1)
    o["b2_2"] = a["L2_ffn_b2"]
    o["wq3"] = a["L3_attn_W_attn"].reshape(P, 3, P)
    o["bq3"] = a["L3_attn_b_attn"][0:2 * P].reshape(2, P).T
    o["bv3"] = a["L3_attn_b_attn"][2 * P:]
    o["wp3"], o["bp3"] = a["L3_attn_W_proj"], a["L3_attn_b_proj"]
    down = a["L3_ffn_w_down"].T.reshape(NHC, P, P).transpose(1, 0, 2).reshape(P, HID)
    o["wi3"] = np.stack([a["L3_ffn_w_gate"].T, a["L3_ffn_w_up"].T, down], axis=1)
    return {k: np.ascontiguousarray(v) for k, v in o.items()}


def kernel(**inputs):
    import ml_dtypes as _ml
    import concourse.bacc as _bacc
    from concourse.bass_utils import run_bass_kernel_spmd as _run

    nc = _bacc.Bacc("TRN2", target_bir_lowering=False, num_devices=1)
    consts = shape_constants()
    for name in ("c_mask", "c_identb"):
        consts[name] = consts[name].astype(_ml.bfloat16)
    arrays = {**lay_out(inputs), **consts}
    d = {name: nc.dram_tensor("in_" + name, list(v.shape), mybir.dt.from_np(v.dtype), kind="ExternalInput").ap()
         for name, v in arrays.items()}
    out = nc.dram_tensor("out", [B, T, P], F32, kind="ExternalOutput").ap()
    build(nc, d, out)
    r = _run(nc, [{"in_" + name: v for name, v in arrays.items()}], core_ids=[0])
    return r.results[0]["out"]
```

```python
from contextlib import ExitStack

import numpy as np

import concourse.bass as bass
from concourse import mybir

F32 = mybir.dt.float32
F16 = mybir.dt.float16
BF16 = mybir.dt.bfloat16
I32 = mybir.dt.int32
U32 = mybir.dt.uint32
ALU = mybir.AluOpType
ACT = mybir.ActivationFunctionType
AX = mybir.AxisListType

P = 128
B = 16
T = 256
NT = B * T // P
H = 16
DH = P // H
MAXROW = 26
NG = 4
NJ = H // NG
NPAIR = H // 2
CAP = 1280
EPS = 1e-5
PRIMED = 3
QSCALE = float(DH) ** -0.5
SEARCH_BITS = 30

SHARED_SIGNALS = ("ys_out0", "ys_out1", "ys_out2", "ys_out3", "stats", "rstd", "xn_ready", "turned", "xts_ready", 
                  "logits", "logits_copied", "shifted", "exp_logits", "gates", "counted", "summed")

EXPERTS = {0: 8, 1: 15, 2: 8}
TOPK = {0: 2, 1: 3, 2: 1}
FF = 512
NF = FF // P
HID = 384
NHC = HID // P


SORTED = (0, 2)
RING3 = 3
IN_FLIGHT = {0: 4, 2: 3}
RING_IN = max(IN_FLIGHT.values())
BLOCKS = {l: -(-((B * T * TOPK[l] + EXPERTS[l] * (P - 1)) // P) // IN_FLIGHT[l]) * IN_FLIGHT[l]
          for l in SORTED}
MAXBLOCKS = max(BLOCKS.values())
BLOCKS_A_TURN = {0: 6, 2: 3}
BLOCK_TURNS = {0: range(2, 14), 2: range(1, 14)}
SORT_TURNS = {0: range(-2, 2), 2: range(-2, 0)}
SEARCH_STEPS = 6
CAPACITY_TURN = 14
GATHERS_A_HEAD = {14: 3, 15: 4}
TILES_A_HEAD = {0: 1, 2: 2}
GATHERS = 8
WROW = 2 * FF + NF
SEARCH_TURNS = range(-1, 14)


def blocks_of(layer, n):
    if layer not in SORTED or n not in BLOCK_TURNS[layer]:
        return 0, 0
    first = BLOCKS_A_TURN[layer] * (n - BLOCK_TURNS[layer][0])
    return first, max(0, min(BLOCKS_A_TURN[layer], BLOCKS[layer] - first))


def feed_forward_plan(layer):
    if layer == 1:
        nh = ny = 8
        need = list(range(ny))
    else:
        nh, ny = NHC, 1
        need = [NHC - 1]
    pieces, m = [], 0
    for k in range(nh):
        pieces.append(("H", k))
        if m < ny and k >= need[m] + 1:
            pieces.append(("Y", m))
            m += 1
    pieces += [("Y", mm) for mm in range(m, ny)]
    return pieces, nh, ny, need


RING = {"S": "S", "M": "S", "V": "S", "P": "S", "R": "S", "Z": "S", "K": "T", "T": "T", "Q": "T",
        "H": "H", "Y": "Y", "X": "H", "C": "S", "U": "S", "G": "Y", "B": "Y", "W": "Y", "O": "O"}
LAG = 3
POOL_HEADS = set(range(H)) - {0, 4, 8, 12}
HIGH_BY_VECTOR = {0: [1, 4, 7, 10, 13], 2: [0, 2, 4, 6, 8, 10, 12, 14], 3: [1, 4, 7, 10, 13]}
Y_BANKS = {0: 1, 1: 2, 2: 1, 3: 1}
LOOP_FROM, LOOP_TO = 2, 14


def turn_steps(layer, n):
    here, ahead, far, behind = (0 <= m < B for m in (n, n + 1, n + 2, n - 1))
    if layer in SORTED:
        nb, pieces = blocks_of(layer, n)[1], []
        for i in range(nb + 2 if nb else 0):
            pieces += [(kind, i - lag) for lag, kind in enumerate("XHY") if 0 <= i - lag < nb]
    else:
        pieces = feed_forward_plan(layer)[0] if here else []
    if layer == 1:
        when = lambda cond, *steps: list(steps) if cond else []
        frame = ["F"] + when(here, ("G", 0)) + ["F"] + when(here, ("B", 0), ("Z", 0)) + ["F"] * 3
        frame += when(here, ("N", 0)) + ["F"] * 4 + when(ahead, ("R", 0)) + ["F"] * 2 + when(here, ("A", 0))
    else:
        frame = []
        for j in range(NJ):
            frame += ([("K", j)] if ahead else []) + ["F"]
            if layer == 3 and behind:
                frame += {0: [("Q", 0)], 1: [("Q", 1)], 3: [("W", 0)]}.get(j, [])
        for h in range(H):
            frame += ([("T", h)] if here else []) + ([("S", h)] if ahead else []) + ["F"]
            frame += [("D", h)] if here else []
            frame += [("O", h - LAG)] if here and h >= LAG else []
            if layer == 0 and n in SEARCH_TURNS and h % 8 < SEARCH_STEPS:
                k, part = divmod(h, 8)
                frame += [("c", 10 * k + part) if part else ("C", k)]
            if layer == 0 and n == CAPACITY_TURN:
                frame += {2: [("u", 0)], 5: [("U", 0)], 8: [("U", 1), ("U", 2)]}.get(h, [])
            if h == 9 and far:
                frame += [("P", 0), ("P", 1)]
        for h in range(H - LAG, H):
            frame += ["F"] + ([("O", h)] if here else []) + ([("M", h - H + LAG)] if ahead and h < H - LAG + 2 else [])
        frame += ([("V", 0), ("V", 1)] if ahead else []) + ["F"] + ([("N", 0)] if here else [])
    slots, done, placed, steps = frame.count("F"), 0, 0, []
    for step in frame:
        if step == "F":
            done += 1
            upto = -(-len(pieces) * done // slots) if layer != 1 else min(len(pieces), done)
            steps += pieces[placed:upto]
            placed = max(placed, upto)
        else:
            steps.append(step)
    steps += pieces[placed:] + ([("E", 0)] if here else [])
    used, out = {}, []
    for kind, k in steps:
        ring = RING.get(kind)
        out.append((kind, k, used.get(ring, 0)))
        used[ring] = used.get(ring, 0) + 1
    return out


def ring_uses(layer, ring, n):
    return sum(RING.get(kind) == ring for kind, _, _ in turn_steps(layer, n))


class Turn:

    def __init__(self, layer, n, loop=None):
        self.layer, self.n, self.loop = layer, n, loop
        self.steps = turn_steps(layer, n)
        self.par = n % 2

    def count(self, per, plus=0):
        if self.loop is None:
            return self.n * per + plus
        return self.loop * (2 * per) + (self.n * per + plus)

    def row(self, ahead=0):
        return self.count(1, ahead)

    def use(self, ring):
        before = sum(ring_uses(self.layer, ring, m) for m in range(-2, self.n))
        if self.loop is None:
            return before
        return self.loop * (2 * ring_uses(self.layer, ring, self.n)) + before


def run_turns(eng, layer, body):
    last = B + 1 if layer == 3 else B
    for n in range(-2, LOOP_FROM):
        body(Turn(layer, n))
    with eng.Fori(0, (LOOP_TO - LOOP_FROM) // 2) as loop:
        for par in range(2):
            body(Turn(layer, LOOP_FROM + par, loop))
    for n in range(LOOP_TO, last):
        body(Turn(layer, n))


def settle(eng, sem):
    eng.sem_inc(sem, 1)


class Chain:

    def __init__(self, eng, sem):
        self.eng, self.sem, self.base, self.n = eng, sem, 0, 0

    def mark(self, ins):
        ins.then_inc(self.sem, 1)
        self.n += 1
        return self.base + self.n

    def wait(self, mark):
        self.eng.wait_ge(self.sem, mark)

    def link(self, ins):
        self.wait(self.mark(ins))


class TurnChain(Chain):

    def __init__(self, eng, sem):
        super().__init__(eng, sem)
        self.total, self.counts = 0, {}

    def enter(self, turn):
        self.turn = turn
        if turn.loop is None:
            self.base = self.total
        else:
            per = self.counts[LOOP_FROM - 1]
            self.base = turn.loop * (2 * per) + self.total
        self.n = 0

    def leave(self):
        self.counts[self.turn.n] = self.n
        if self.turn.loop is not None:
            assert self.n == self.counts[LOOP_FROM - 1], (self.n, self.counts)
            if self.turn.n == LOOP_FROM + 1:
                self.total += self.n * (LOOP_TO - LOOP_FROM) - self.n
                return
        self.total += self.n


def build(nc, d, out):
    ctx = ExitStack()
    with ctx:
        def sb(name, shape, dt=F32):
            return ctx.enter_context(nc.sbuf_tensor(name, shape, dt))

        def psum(name, shape):
            return ctx.enter_context(nc.psum_tensor(name, shape, F32))

        sems = {}

        def sem(name):
            if name not in sems:
                sems[name] = ctx.enter_context(nc.semaphore(name))
            return sems[name]

        X = sb("X", [P, NT, P])
        XT = sb("XT", [P, B * T])
        XN = sb("XN", [P, NT, P])
        wb = sb("wb", [P, RING_IN, WROW])
        wb2 = sb("wb2", [1, RING_IN, P])
        xsb = sb("xsb", [P, RING_IN, P])
        xsT = sb("xsT", [P, RING3, P])
        hbs = sb("hbs", [P, RING3, FF])
        ysb = sb("ysb", [P, RING_IN, P])
        w1, w2 = {1: sb("w1_1", [P, 16, P])}, {1: sb("w2_1", [P, 16, P])}
        b1, b2 = {1: sb("b1_1", [P, 16])}, {1: sb("b2_1", [16, P])}
        oh = sb("oh", [P, 2, 8, NT])
        place = sb("place", [P, 8, NT])
        slotf = sb("slotf", [P, 2, NT])
        slot = sb("slot", [P, 2, NT], U32)
        gk = sb("gk", [P, 2, NT])
        keep = sb("keep", [P, 8, NT])
        nblk = sb("nblk", [P, 8])
        nblki = sb("nblki", [P, 8], I32)
        nend = sb("nend", [P, 8])
        ebf = sb("ebf", [P, MAXBLOCKS])
        eb = sb("eb", [P, MAXBLOCKS], I32)
        cmpb = sb("cmpb", [P, MAXBLOCKS, 8])
        blockno = sb("blockno", [P, MAXBLOCKS])
        XS = nc.dram_tensor("sorted_x", [MAXBLOCKS * P, P], F32, kind="Internal").ap()
        YS = nc.dram_tensor("sorted_y", [MAXBLOCKS * P, P], F32, kind="Internal").ap()
        wr = {l: sb(f"wr_{l}", [P, EXPERTS[l]]) for l in EXPERTS}
        br = {1: sb("br_1", [P, 15]), 2: sb("br_2", [P, 8])}
        wq0 = sb("wq0", [P, 5, P])
        bq0 = sb("bq0", [P, 4])
        bv0 = sb("bv0", [P, P])
        rope0 = sb("rope0", [P, 4, T])
        wq2 = sb("wq2", [P, 3, P])
        rope2 = sb("rope2", [P, 2, B])
        wq3 = sb("wq3", [P, 3, P])
        bq3 = sb("bq3", [P, 2])
        bv3 = sb("bv3", [P, P])
        wp3 = sb("wp3", [P, P])
        bp3 = sb("bp3", [P, P])
        wi3 = sb("wi3", [P, 3, HID], I32)
        wf3 = sb("wf3", [P, 3, HID])
        wb1, wc1 = sb("wb1", [P, P]), sb("wc1", [P, P])
        bb1 = sb("bb1", [P, 1])
        bc1 = sb("bc1", [1, P])
        gam1, bet1 = sb("gam1", [P, P]), sb("bet1", [P, P])
        llr1 = sb("llr1", [P, 1])
        lamt = sb("lamt", [P, 1])
        oml = sb("oml", [P, 1])
        lam1 = sb("lam1", [P, 1])
        lamrow = sb("lamrow", [P, T])
        ident = sb("ident", [P, P])
        onesr = sb("onesr", [1, P])
        onesm = sb("onesm", [P, P])
        selq = sb("selq", [P, 4, NJ, P], F16)
        onecol = sb("onecol", [2, P], F16)
        alcol = sb("alcol", [2, 2, NJ, P], F16)
        alrow = sb("alrow", [2, T], F16)
        maskb = sb("maskb", [P, 2, P], BF16)
        identb = sb("identb", [P, P], BF16)
        rank = sb("rank", [P, NT, 16])
        neghalf = sb("neghalf", [P, NT])
        tri = sb("tri", [P, P])

        st6 = sb("st6", [P, 4, 6])
        mv4 = sb("mv4", [P, 4, 2])
        MV = sb("MV", [P, NT, 2])
        vare = sb("vare", [P, NT])
        rstd = sb("rstd", [P, NT])
        xn = sb("xn", [P, 2, 4, P])
        xts = sb("xts", [P, 2, 4 * P])
        LG = sb("LG", [P, NT, 16])
        pr = sb("pr", [P, NT, 16])
        GA = sb("GA", [P, NT, 16])
        ra, rb, rc = (sb(n, [P, NT, 16]) for n in ("ra", "rb", "rc"))
        r1, r2 = sb("r1", [P, NT]), sb("r2", [P, NT])
        thr = sb("thr", [P, 8], I32)
        cand = sb("cand", [P, 8], I32)
        bitf = sb("bitf", [P, 8])
        biti = sb("biti", [P, 8], I32)
        addb = sb("addb", [P, 8], I32)
        cmp_ = sb("cmp_", [P, 8, NT])
        key = sb("key", [P, 8, NT])
        cnt = sb("cnt", [P, 8])
        left = sb("left", [P, 8])
        scan = sb("scan", [P, 8, NT])

        xtb = sb("xtb", [P, 2, T])
        gst = sb("gst", [P, 2, 2, 16])
        qkf = sb("qkf", [P, 2, 2 * T])
        qk16 = sb("qk16", [P, 2, 2 * T], F16)
        stk = sb("stk", [P, 2, NJ, 2 * T], F16)
        mx = sb("mx", [P, 2, NJ, P])
        pe32 = sb("pe32", [P, 4, 2 * T])
        pe16 = sb("pe16", [P, 2, 4, 2 * T], F16)
        v32 = sb("v32", [P, 2, P])
        va = sb("va", [P, 2, 2, 2, H, DH + 1], F16)
        hb = wb[:, :, :].rearrange("p r n -> p (r n)")[:, 0:8 * T].rearrange("p (k n) -> p k n", k=4)
        gt = sb("gt", [16, T])
        rden = sb("rden", [P, 2, H])
        ob = sb("ob", [P, 2, P])
        oT = sb("oT", [P, T])
        spare = hbs[:, :, :].rearrange("p r n -> p (r n)")
        th, hg = (spare[:, 2 * T * i:2 * T * (i + 1)].rearrange("p (k n) -> p k n", k=2) for i in range(2))
        vals, hT = (spare[:, T * i:T * (i + 1)] for i in range(2))
        zs = sb("zs", [P, 2, 6])
        zmv = sb("zmv", [P, 2, 2])
        zve, zr = sb("zve", [P, 2]), sb("zr", [P, 2])
        zn = spare[:, 2 * T:3 * T].rearrange("p (c n) -> p c n", c=2)
        zg = spare[:, 3 * T:5 * T].rearrange("p (k c n) -> p k c n", k=2, c=2)

        pS = psum("pS", [P, 2, 512])
        pT_ = psum("pT_", [P, 2, 512])
        pH = psum("pH", [P, 2, 512])
        pY = psum("pY", [P, 512])
        pO = psum("pO", [P, 512])
        po = pO[:, 0:2 * H * (DH + 1)].rearrange("p (c h e) -> p c h e", c=2, h=H)

        xin = d["x"].rearrange("(t p) e -> p t e", p=P)
        xout = out.rearrange("b (c p) e -> p (b c) e", p=P)

        loads = {
            "ld_x": [(X[:, 0:16, :], xin[:, 0:16, :]), (X[:, 16:32, :], xin[:, 16:32, :])],
            "ld_id": [(ident[:, :], d["c_ident"])],
            "ld_0": [(wr[0][:, :], d["wr0"]), (wq0[:, :, :], d["wq0"]), (bq0[:, :], d["bq0"]),
                     (bv0[:, :], d["bv0"].partition_broadcast(P))],
            "ld_cst": [(onesr[:, :], d["c_ones"][0:1, :]), (onesm[:, :], d["c_ones"]),
                       (selq[:, :, :, :], d["c_selq"]), (onecol[:, :], d["c_onecol"]),
                       (alcol[:, :, :, :], d["c_alcol"]), (alrow[:, :], d["c_alrow"]),
                       (maskb[:, :, :], d["c_mask"]), (identb[:, :], d["c_identb"]), (rank[:, :, :], d["c_rank"]),
                       (tri[:, :], d["c_tri"]), (rope0[:, :, :], d["c_rope0"]),
                       (rope2[:, :, :], d["c_rope2"]), (bitf[:, :], d["c_bitf"]), (blockno[:, :], d["c_blockno"])],
            "ld_1": [(wr[1][:, :], d["wr1"]), (br[1][:, :], d["br1"].partition_broadcast(P)),
                     (w1[1][:, :, :], d["w1_1"]), (w2[1][:, :, :], d["w2_1"]), (b1[1][:, :], d["b1_1"]),
                     (b2[1][:, :], d["b2_1"]), (wb1[:, :], d["wb1"]), (wc1[:, :], d["wc1"]), (bb1[:, :], d["bb1"]),
                     (bc1[:, :], d["bc1"]), (gam1[:, :], d["gam1"].partition_broadcast(P)),
                     (bet1[:, :], d["bet1"].partition_broadcast(P)), (llr1[:, :], d["llr1"])],
            "ld_3": [(wq3[:, :, :], d["wq3"]), (bq3[:, :], d["bq3"]), (bv3[:, :], d["bv3"].partition_broadcast(P)),
                     (wp3[:, :], d["wp3"]), (bp3[:, :], d["bp3"].partition_broadcast(P)), (wi3[:, :, :], d["wi3"])],
            "ld_2": [(wr[2][:, :], d["wr2"]), (br[2][:, :], d["br2"].partition_broadcast(P)),
                     (wq2[:, :, :], d["wq2"])],
        }
        full = {k: 16 * len(v) for k, v in loads.items()}

        plans = {l: feed_forward_plan(l) for l in range(4)}

        SPLITTERS = {"pool": sorted(POOL_HEADS), "dve": sorted(set(range(H)) - POOL_HEADS)}

        def split_by(turn, h):
            if turn.layer in SORTED and turn.n in GATHERS_A_HEAD:
                first = min(GATHERS_A_HEAD)
                return "dve", first * len(SPLITTERS["dve"]) + (turn.n - first) * H + h + 1
            who = "pool" if h in POOL_HEADS else "dve"
            return who, turn.count(len(SPLITTERS[who]), SPLITTERS[who].index(h) + 1)

        def y_bank(layer, local):
            return (pY, pO)[local % Y_BANKS[layer]]

        def y_before(layer, turn, m):
            at = [local for kind, k, local in turn.steps if kind == "Y" and k == m]
            return turn.use("Y") + at[0] + 1

        def place_in(turn, i):
            l, per = turn.layer, BLOCKS_A_TURN[turn.layer]
            ring = IN_FLIGHT[l]
            first = per * (turn.n - BLOCK_TURNS[l][0]) + i
            rounds = first // ring + 1
            return first % ring, rounds if turn.loop is None else turn.loop * (2 * per // ring) + rounds

        before_in = BLOCKS[0] // IN_FLIGHT[0]

        def tokens_in(turn, rounds):
            return rounds * 16 + (0 if turn.layer == 0 else 16 * before_in)

        def expert_in(turn, rounds):
            return rounds * 16 if turn.layer == 0 else rounds * 32 + 16 * before_in

        def fetched(l, t):
            return 16 * TOPK[l] * (t // GATHERS + 1) + (0 if l == 0 else 16 * TOPK[0] * NT // GATHERS)

        def used_at(turn, kind, k):
            return [loc for kd, kk, loc in turn.steps if kd == kind and kk == k][0]

        def high_made(turn, h):
            heads = HIGH_BY_VECTOR[turn.layer]
            return turn.count(len(heads), heads.index(h) + 1)

        def split_exp(eng, turn, h):
            who = split_by(turn, h)[0]
            l = turn.layer
            at = [loc for kd, kk, loc in turn.steps if kd == "T" and kk == h][0]
            n = 3 * P if l == 3 else 2 * T
            eng.wait_ge(sem(f"L{l}_T_free"), PRIMED + turn.use("T") + at + 1)
            if h in HIGH_BY_VECTOR[l] and who == "pool":
                eng.wait_ge(sem(f"L{l}_high"), PRIMED + high_made(turn, h))
            eng.tensor_tensor(pe16[:, 1, h % 4, 0:n], pe32[:, h % 4, 0:n], pe16[:, 0, h % 4, 0:n], ALU.subtract)\
               .then_inc(sem(f"L{l}_low_{who}"), 1)

        block = ctx.enter_context(nc.Block())

        @block.tensor
        def _(pe):
            pe.wait_ge(sem("ld_id"), full["ld_id"])

            def phase_a(l):
                s = lambda n: sem(f"L{l}_{n}")
                with pe.Fori(0, NT // 4 // 2) as turn:
                    i = turn * 2
                    for par in range(2):
                        pe.wait_ge(sem("xn_ready"), PRIMED + l * (NT // 4) + i + par + 1)
                        pe.wait_ge(sem("xts_ready"), PRIMED + l * (NT // 4) + i)
                        for u in range(4):
                            ins = pe.transpose(pS[:, par, u * P:(u + 1) * P], xn[:, par, u, :], ident[:, :])
                        ins.then_inc(sem("turned"), 1)
                    if l < 3:
                        for par in range(2):
                            pe.wait_ge(sem("xts_ready"), PRIMED + l * (NT // 4) + i + par + 1)
                            pe.wait_ge(sem("logits_copied"), PRIMED + l * (NT // 4) + i)
                            for u in range(4):
                                ins = pe.matmul(pT_[:, par, u * 16:u * 16 + EXPERTS[l]],
                                                xts[:, par, u * P:(u + 1) * P], wr[l][:, :], start=True, stop=True)
                            ins.then_inc(sem("logits"), 1)

            def hidden(l, turn, k, use, s):
                pe.wait_ge(s("H_free"), PRIMED + use - (0 if l == 3 and k == 0 else 1))
                bank = pH[:, k % 2, :]
                for half in range(2):
                    w = wf3[:, half, k * P:(k + 1) * P] if l == 3 else w1[1][:, 2 * k + half, :]
                    ins = pe.matmul(bank[:, half * T:(half + 1) * T], w, XT[:, bass.ts(turn.row(), T)],
                                    start=True, stop=True)
                ins.then_inc(s("H_full"), 1)

            def project(l, turn, m, use, local, s):
                need = plans[l][3]
                pe.wait_ge(s("H_free"), PRIMED + turn.use("H") + need[m] + 1)
                pe.wait_ge(s("Y_free"), PRIMED + use + 1 - Y_BANKS[l])
                yb = y_bank(l, local)
                if l == 1:
                    for half in range(2):
                        for c in range(2):
                            ins = pe.matmul(yb[:, half * T + c * P:half * T + (c + 1) * P],
                                            hb[:, m % 4, half * T + c * P:half * T + (c + 1) * P],
                                            w2[1][:, 2 * m + half, :], start=True, stop=True)
                else:
                    for c in range(2):
                        for f in range(NHC):
                            ins = pe.matmul(yb[:, c * P:(c + 1) * P], hb[:, f, c * P:(c + 1) * P],
                                            wf3[:, 2, f * P:(f + 1) * P], start=(f == 0), stop=(f == NHC - 1))
                ins.then_inc(s("Y_full"), 1)

            def take_turn(turn):
                l, par, nxt = turn.layer, turn.par, 1 - turn.par
                s = lambda n: sem(f"L{l}_{n}")
                use_s, use_t, use_h, use_y, use_o = (turn.use(r) for r in "STHYO")
                for kind, k, local in turn.steps:
                    if RING.get(kind) == "S":
                        bank = pS[:, local % 2, :]
                        pe.wait_ge(s("S_free"), PRIMED + use_s + local - 1)
                    elif RING.get(kind) == "T":
                        bank = pT_[:, local % 2, :]
                        pe.wait_ge(s("T_free"), PRIMED + use_t + local - 1)
                    elif kind in "GBW":
                        yb = y_bank(l, local)
                        pe.wait_ge(s("Y_free"), PRIMED + use_y + local + (0 if kind == "B" else 1 - Y_BANKS[l]))

                    if kind == "H" and l in SORTED:
                        ring = k % RING3
                        place_, nth = place_in(turn, k)
                        pe.wait_ge(s("H_free"), PRIMED + use_h + max(local - 1, used_at(turn, "X", k) + 1))
                        pe.wait_ge(sem(f"w_in{place_}"), expert_in(turn, nth))
                        for f in range(NF):
                            ins = pe.matmul(pH[:, local % 2, f * P:(f + 1) * P], wb[:, place_, f * P:(f + 1) * P],
                                            xsT[:, ring, :], start=True, stop=True)
                        ins.then_inc(s("H_full"), 1)
                    elif kind == "Y" and l in SORTED:
                        ring, place_ = k % RING3, place_in(turn, k)[0]
                        pe.wait_ge(s("H_free"), PRIMED + use_h + used_at(turn, "H", k) + 1)
                        pe.wait_ge(s("Y_free"), PRIMED + use_y + local)
                        for f in range(NF):
                            ins = pe.matmul(pY[:, 0:P], hbs[:, ring, f * P:(f + 1) * P],
                                            wb[:, place_, FF + f * P:FF + (f + 1) * P], start=(f == 0),
                                            stop=(f == NF - 1 and l == 0))
                        if l == 2:
                            ins = pe.matmul(pY[:, 0:P], onesr[:, :], wb2[:, place_, :], start=False, stop=True)
                        ins.then_inc(s("Y_full"), 1)
                    elif kind == "C":
                        pe.wait_ge(sem("counted"), PRIMED + turn.count(2, k + 3))
                        pe.matmul(bank[:, 0:8], onesm[:, :], cnt[:, :], start=True, stop=True)\
                          .then_inc(s("S_full"), 1)
                    elif kind == "U":
                        pe.wait_ge(sem("counted"), PRIMED + SEARCH_BITS + (2 if k == 0 else 3))
                        equal = cmp_[:, :, :].rearrange("p e t -> p (e t)")
                        what, by = ((cnt[:, :], onesm), (equal, tri), (equal, onesm))[k]
                        pe.matmul(bank[:, 0:8 if k == 0 else 8 * NT], by[:, :], what, start=True, stop=True)\
                          .then_inc(s("S_full"), 1)
                    elif kind == "H":
                        hidden(l, turn, k, use_h + local, s)
                    elif kind == "Y":
                        project(l, turn, k, use_y + local, local, s)
                    elif kind == "X":
                        place_, nth = place_in(turn, k)
                        pe.wait_ge(s("H_free"), PRIMED + use_h + local - 1)
                        pe.wait_ge(sem(f"xs_in{place_}"), tokens_in(turn, nth))
                        pe.transpose(pH[:, local % 2, 0:P], xsb[:, place_, :], ident[:, :]).then_inc(s("H_full"), 1)
                    elif kind == "G":
                        pe.wait_ge(s("row_staged"), PRIMED + turn.row(1))
                        for c in range(2):
                            ins = pe.transpose(yb[0:16, c * P:(c + 1) * P], gst[:, par, c, :], ident[:, :])
                        ins.then_inc(s("Y_full"), 1)
                    elif kind == "B":
                        for c in range(2):
                            ins = pe.matmul(yb[:, c * P:(c + 1) * P], gt[:, c * P:(c + 1) * P], b2[1][:, :],
                                            start=True, stop=True)
                        ins.then_inc(s("Y_full"), 1)
                    elif kind == "R":
                        pe.matmul(bank[:, 0:T], wb1[:, :], XT[:, bass.ts(turn.row(1), T)], start=True, stop=True)\
                          .then_inc(s("S_full"), 1)
                    elif kind == "Z":
                        pe.wait_ge(s("scanned"), PRIMED + turn.row(1))
                        pe.wait_ge(s("row_staged"), PRIMED + turn.row(1))
                        for c in range(2):
                            o = bank[:, c * P:(c + 1) * P]
                            pe.matmul(o, hT[:, c * P:(c + 1) * P], wc1[:, :], start=True, stop=False)
                            pe.matmul(o, xtb[:, par, c * P:(c + 1) * P], ident[:, :], start=False, stop=False)
                            ins = pe.matmul(o, onesr[:, :], bc1[:, :], start=False, stop=True)
                        ins.then_inc(s("S_full"), 1)
                    elif kind == "P":
                        w = {0: wq0, 2: wq2, 3: wq3}[l]
                        for n, which in enumerate({0: [2 * k, 2 * k + 1]}.get(l, [k])):
                            ins = pe.matmul(bank[:, n * T:(n + 1) * T], w[:, which, :],
                                            XT[:, bass.ts(turn.row(2), T)], start=True, stop=True)
                        ins.then_inc(s("S_full"), 1)
                    elif kind == "V":
                        pe.wait_ge(s("row_staged"), PRIMED + turn.row(2))
                        w = {0: wq0[:, 4, :], 2: wq2[:, 2, :], 3: wq3[:, 2, :]}[l]
                        pe.matmul(bank[:, 0:P], xtb[:, nxt, k * P:(k + 1) * P], w, start=True, stop=True)\
                          .then_inc(s("S_full"), 1)
                    elif kind == "K":
                        pe.wait_ge(s("qk_split"), PRIMED + turn.row(2))
                        for side in range(2):
                            o = bank[:, side * T:(side + 1) * T]
                            pe.matmul(o, selq[:, 2 * side, k, :], qk16[:, 0, side * T:(side + 1) * T],
                                      start=True, stop=False)
                            ins = pe.matmul(o, selq[:, 2 * side + 1, k, :], qk16[:, 1, side * T:(side + 1) * T],
                                            start=False, stop=(l != 3 and side == 0))
                            if l == 3:
                                ins = pe.matmul(o, alcol[:, side, k, :], alrow[:, :], start=False, stop=True)
                            elif side == 1:
                                ins = pe.matmul(o, onecol[:, :], alrow[:, :], start=False, stop=True)
                        ins.then_inc(s("T_full"), 1)
                    elif kind == "S":
                        g, j = k % NG, k // NG
                        rows = slice(32 * g, 32 * g + 32)
                        pe.wait_ge(s("T_free"), PRIMED + use_t + j + 1)
                        if l == 3:
                            pe.matmul(bank.rearrange("p (c n) -> p c n", c=2)[:, :, 0:P], identb[:, :],
                                      maskb[:, 0, None, :].to_broadcast([P, 2, P]), start=True, stop=True)
                            pe.matmul(bank[:, 0:P], stk[rows, nxt, j, 0:P], stk[rows, nxt, j, T:T + P],
                                      start=False, stop=True, skip_group_check=True)
                            ins = pe.matmul(bank[:, P:P + T], stk[rows, nxt, j, P:T], stk[rows, nxt, j, T:2 * T],
                                            start=False, stop=True, skip_group_check=True)
                        else:
                            for c in range(2):
                                ins = pe.matmul(bank[:, c * T:(c + 1) * T], stk[rows, nxt, j, c * P:(c + 1) * P],
                                                stk[rows, nxt, j, T:2 * T], start=True, stop=True)
                        ins.then_inc(s("S_full"), 1)
                    elif kind == "M":
                        pe.wait_ge(s("S_free"), PRIMED + use_s + local - k)
                        for j in range(NJ):
                            ins = pe.transpose(bank[:, j * P:(j + 1) * P], mx[:, k, j, :], ident[:, :])
                        ins.then_inc(s("S_full"), 1)
                    elif kind == "T":
                        g, j = k % NG, k // NG
                        rows = slice(32 * g, 32 * g + 32)
                        pe.wait_ge(s("S_free"), PRIMED + use_s)
                        if l == 3:
                            pe.matmul(bank.rearrange("p (c n) -> p c n", c=2)[:, :, 0:P], identb[:, :],
                                      maskb[:, 1, None, :].to_broadcast([P, 2, P]), start=True, stop=True)
                            for o, q0, q1 in ((0, 0, T), (T, P, T)):
                                kc = q0 // P
                                ins = pe.matmul(bank[:, o:o + q1 - q0], stk[rows, par, j, T + kc * P:T + (kc + 1) * P],
                                                stk[rows, par, j, q0:q1], start=False, stop=True,
                                                skip_group_check=True)
                        else:
                            for c in range(2):
                                ins = pe.matmul(bank[:, c * T:(c + 1) * T],
                                                stk[rows, par, j, T + c * P:T + (c + 1) * P],
                                                stk[rows, par, j, 0:T], start=True, stop=True)
                        ins.then_inc(s("T_full"), 1)
                    elif kind == "O":
                        who, nth = split_by(turn, k)
                        pe.wait_ge(s(f"low_{who}"), PRIMED + nth)
                        pe.wait_ge(s("v_split"), PRIMED + turn.row(1))
                        pe.wait_ge(s("out_read"), PRIMED + turn.row())
                        for c in range(2):
                            kcs = [0] if (l == 3 and c == 0) else [0, 1]
                            parts = [(kc, e, v) for kc in kcs for e, v in ((0, 0), (0, 1), (1, 0))]
                            for n, (kc, e, v) in enumerate(parts):
                                col = kc * T + (0 if (l == 3 and kc == 1) else c * P)
                                ins = pe.matmul(po[:, c, k, :], pe16[:, e, k % 4, col:col + P],
                                                va[:, par, v, kc, k, :], start=(n == 0), stop=(n == len(parts) - 1))
                        ins.then_inc(s("O_full"), 1)
                    elif kind == "Q":
                        pe.wait_ge(s("out_read"), PRIMED + turn.row())
                        pe.transpose(bank[:, 0:P], ob[:, k, :], ident[:, :]).then_inc(s("T_full"), 1)
                    elif kind == "W":
                        at = [loc for kd, kk, loc in turn.steps if kd == "Q" and kk == 1][0]
                        pe.wait_ge(s("T_free"), PRIMED + use_t + at + 1)
                        for c in range(2):
                            ins = pe.matmul(yb[:, c * P:(c + 1) * P], oT[:, c * P:(c + 1) * P], wp3[:, :],
                                            start=True, stop=True)
                        ins.then_inc(s("Y_full"), 1)

            for l in range(4):
                pe.wait_ge(sem(f"ld_{l}"), full[f"ld_{l}"])
                phase_a(l)
                if l == 0:
                    pe.wait_ge(sem("ld_cst"), full["ld_cst"])
                if l in SORTED:
                    pe.wait_ge(sem("chosen"), 1 + SORTED.index(l))
                    every = rb[:, :, :].rearrange("p t e -> p (t e)")[:, 0:8 * NT]
                    pe.matmul(pS[:, 0, 0:8 * NT], tri[:, :], every, start=True, stop=True)
                    pe.matmul(pS[:, 1, 0:8 * NT], onesm[:, :], every, start=True, stop=True)\
                      .then_inc(sem("ranked"), 1)
                if l == 3:
                    pe.wait_ge(sem("w3_ready"), 3)
                pe.wait_ge(sem("xts_ready"), PRIMED + (l + 1) * (NT // 4))
                if l < 3:
                    pe.wait_ge(sem("gates"), PRIMED + l + 1)
                run_turns(pe, l, take_turn)

        @block.scalar
        def _(act):
            def phase_a(l):
                s = lambda n: sem(f"L{l}_{n}")
                with act.Fori(0, NT // 4 // 2) as turn:
                    i = turn * 2
                    for par in range(2):
                        act.wait_ge(sem("turned"), PRIMED + l * (NT // 4) + i + par + 1)
                        if l < 3:
                            act.wait_ge(sem("logits"), PRIMED + l * (NT // 4) + i)
                        if l < 3:
                            act.activation(xts[:, par, :], pS[:, par, :], ACT.Copy)
                        act.activation(XT[:, bass.ts(i + par, 4 * P)], pS[:, par, :], ACT.Copy)\
                           .then_inc(sem("xts_ready"), 1)
                    if l < 3:
                        for par in range(2):
                            act.wait_ge(sem("logits"), PRIMED + l * (NT // 4) + i + par + 1)
                            act.activation(LG[:, bass.ds((i + par) * 4, 4), 0:EXPERTS[l]],
                                           pT_[:, par, 0:64].rearrange("p (u e) -> p u e", e=16)[:, :, 0:EXPERTS[l]],
                                           ACT.Copy).then_inc(sem("logits_copied"), 1)

            def take_turn(turn):
                l, par, nxt = turn.layer, turn.par, 1 - turn.par
                s = lambda n: sem(f"L{l}_{n}")
                use_t, use_h, use_o = (turn.use(r) for r in "THO")
                for kind, k, local in turn.steps:
                    if RING.get(kind) == "T":
                        bank = pT_[:, local % 2, :]
                        act.wait_ge(s("T_full"), PRIMED + use_t + local + 1)
                    if kind in "XH" and l in SORTED:
                        act.wait_ge(s("H_full"), PRIMED + use_h + local + 1)
                        bank = pH[:, local % 2, :]
                        ring, place_ = k % RING3, place_in(turn, k)[0]
                        if kind == "X":
                            ins = act.activation(xsT[:, ring, :], bank[:, 0:P], ACT.Copy)
                        elif l == 0:
                            ins = act.activation(hbs[:, ring, :], bank, ACT.Relu)
                        else:
                            for f in range(NF):
                                ins = act.activation(hbs[:, ring, f * P:(f + 1) * P], bank[:, f * P:(f + 1) * P],
                                                     ACT.Relu, bias=wb[:, place_, 2 * FF + f:2 * FF + f + 1])
                        ins.then_inc(s("H_free"), 1)
                    elif kind == "H":
                        act.wait_ge(s("H_full"), PRIMED + use_h + local + 1)
                        bank = pH[:, k % 2, :]
                        if l == 3:
                            act.wait_ge(s("H_free"), PRIMED + use_h + local - (0 if k == 0 else 1))
                            act.activation(th[:, k % 2, :], bank[:, 0:T], ACT.Tanh, scale=0.5)\
                               .then_inc(s("tanh_done"), 1)
                            continue
                        done = k - 4
                        if done >= 0:
                            act.wait_ge(s("Y_full"), PRIMED + y_before(l, turn, done))
                        else:
                            act.wait_ge(s("Y_full"), PRIMED + turn.use("Y"))
                        for half in range(2):
                            ins = act.activation(hb[:, k % 4, half * T:(half + 1) * T],
                                                 bank[:, half * T:(half + 1) * T], ACT.Relu,
                                                 bias=b1[1][:, 2 * k + half:2 * k + half + 1])
                        ins.then_inc(s("H_free"), 1)
                    elif kind == "K":
                        act.activation(stk[:, nxt, k, :], bank, ACT.Copy).then_inc(s("T_free"), 1)
                    elif kind == "T":
                        act.wait_ge(s("O_full"), PRIMED + use_o + k - 2)
                        n = 3 * P if l == 3 else 2 * T
                        ins = act.activation(pe32[:, k % 4, 0:n], bank[:, 0:n], ACT.Exp)
                        if k not in HIGH_BY_VECTOR[l]:
                            ins = act.activation(pe16[:, 0, k % 4, 0:n], bank[:, 0:n], ACT.Exp)
                        ins.then_inc(s("T_free"), 1)
                    elif kind == "Q":
                        act.wait_ge(s("Y_full"), PRIMED + turn.use("Y"))
                        act.activation(oT[:, k * P:(k + 1) * P], bank[:, 0:P], ACT.Copy).then_inc(s("T_free"), 1)

            for l in range(4):
                if l < 3:
                    phase_a(l)
                    act.wait_ge(sem("shifted"), PRIMED + l + 1)
                    act.activation(pr[:, :, 0:EXPERTS[l]], ra[:, :, 0:EXPERTS[l]], ACT.Exp)\
                       .then_inc(sem("exp_logits"), 1)
                else:
                    phase_a(l)
                if l == 1:
                    act.wait_ge(sem("ld_1"), full["ld_1"])
                    act.activation(lamt[:, :], llr1[:, :], ACT.Tanh, scale=0.5).then_inc(sem("lam_tanh"), 1)
                run_turns(act, l, take_turn)

        @block.gpsimd
        def _(pool):
            chain = Chain(pool, sem("pool_chain"))
            chain.link(pool.memset(neghalf[:, :], -0.5))
            for l in range(4):
                s = lambda n: sem(f"L{l}_{n}")
                if l == 3:
                    pool.wait_ge(sem("ld_3"), full["ld_3"])
                    for n in range(3):
                        pool.tensor_scalar(wf3[:, n, :], wi3[:, n, :], 1.0 / 127.0, None, ALU.mult)\
                            .then_inc(sem("w3_ready"), 1)
                for g in range(NT // 4):
                    four = slice(4 * g, 4 * g + 4)
                    pool.wait_ge(sem("stats"), PRIMED + l * (NT // 4) + g + 1)
                    chain.link(pool.tensor_scalar(vare[:, four], MV[:, four, 1], EPS, None, ALU.add))
                    pool.tensor_tensor(rstd[:, four], vare[:, four], neghalf[:, four], ALU.pow).then_inc(sem("rstd"), 1)
                pool.wait_ge(sem("xts_ready"), PRIMED + (l + 1) * (NT // 4))
                if l < 3:
                    pool.wait_ge(sem("gates"), PRIMED + l + 1)
                split = TurnChain(pool, sem(f"L{l}_pool_chain"))

                def stage(turn, par):
                    pool.wait_ge(s("x_final"), PRIMED + turn.row())
                    settle(pool, sem("pool_settled"))
                    if l == 1:
                        split.link(pool.tensor_copy(gst[:, par, :, :], GA[:, bass.ds(turn.count(2, 2), 2), :]))
                        settle(pool, sem("pool_settled"))
                    pool.tensor_copy(xtb[:, par, :], XT[:, bass.ts(turn.row(1), T)]).then_inc(s("row_staged"), 1)

                def take_turn(turn):
                    split.enter(turn)
                    if 0 <= turn.n + 1 < B:
                        stage(turn, 1 - turn.par)
                    halves = []
                    sorting = l in SORTED and turn.loop is None and turn.n in SORT_TURNS[l]
                    for kind, k, local in turn.steps:
                        if sorting and turn.n > -2 and kind == "S":
                            scatter(1)
                        if kind == "P" and k == 1:
                            pool.wait_ge(s("S_free"), PRIMED + turn.use("S") + local + 1)
                            settle(pool, sem("pool_settled"))
                            if l == 0:
                                split.link(pool.tensor_tensor(qkf[:, 0, :], qkf[:, 0, :], qkf[:, 1, :], ALU.add))
                                halves = [0, 1]
                            else:
                                halves = [1]
                        if halves and (turn.n < 0 or kind == "V" or (kind == "D" and k > 9 and k % 2 == 1)):
                            for half in (list(halves) if turn.n < 0 or kind == "V" else halves[:1]):
                                if half == 0:
                                    settle(pool, sem("pool_settled"))
                                    split.link(pool.tensor_copy(qk16[:, 0, :], qkf[:, 0, :]))
                                else:
                                    pool.tensor_tensor(qk16[:, 1, :], qkf[:, 0, :], qk16[:, 0, :], ALU.subtract)\
                                        .then_inc(s("qk_split"), 1)
                                halves = halves[1:]
                        if kind == "V" and k == 1:
                            pool.wait_ge(s("S_free"), PRIMED + turn.use("S") + local + 1)
                            settle(pool, sem("pool_settled"))
                            src = v32[:, :, :].rearrange("p c (h e) -> p c h e", h=H)
                            hi, lo = (va[:, 1 - turn.par, v, :, :, 0:DH] for v in range(2))
                            split.link(pool.tensor_copy(hi, src))
                            pool.tensor_tensor(lo, src, hi, ALU.subtract).then_inc(s("v_split"), 1)
                        elif kind == "D":
                            if split_by(turn, k)[0] == "pool":
                                split_exp(pool, turn, k)
                            if l in SORTED and turn.loop is None and turn.n in GATHERS_A_HEAD and (turn.n, k) >= (14, 2):
                                gather(GATHERS_A_HEAD[turn.n])
                        elif kind == "Z":
                            pool.wait_ge(s("z_stats"), PRIMED + turn.row(1))
                            settle(pool, sem("pool_settled"))
                            split.link(pool.tensor_scalar(zve[:, :], zmv[:, :, 1], EPS, None, ALU.add))
                            pool.tensor_tensor(zr[:, :], zve[:, :], neghalf[:, 0:2], ALU.pow).then_inc(s("z_rstd"), 1)
                        elif kind == "N" and l == 1:
                            wide = lambda a: a[:, None, :].to_broadcast([P, 2, P])
                            pool.wait_ge(s("z_normal"), PRIMED + turn.row(1))
                            split.link(pool.tensor_tensor(zg[:, 0, :, :], zn[:, :, :], wide(gam1), ALU.mult))
                            pool.tensor_tensor(zg[:, 1, :, :], zg[:, 0, :, :], wide(bet1), ALU.add)\
                                .then_inc(s("z_done"), 1)
                    if sorting and turn.n == -2:
                        scatter(NT // 2)
                    split.leave()

                scatters = [(t, choice) for t in range(NT) for choice in range(TOPK.get(l, 0))]

                def scatter(n):
                    for t, choice in scatters[:n]:
                        pool.indirect_dma_start(XS, bass.IndirectOffsetOnAxis(ap=slot[:, choice, t:t + 1], axis=0),
                                                XN[:, t, :], None).then_inc(sem("sorted_out"), 16)
                    del scatters[:n]

                gathers = [(t, choice) for t in range(NT) for choice in range(TOPK.get(l, 0))]

                def gather(n):
                    if len(gathers) == NT * TOPK[l]:
                        for ring in range(RING_IN):
                            n_out = sum(len(range(ring, BLOCKS[m], IN_FLIGHT[m])) for m in SORTED
                                        if m <= l and ring < IN_FLIGHT[m])
                            pool.wait_ge(sem(f"ys_out{ring}"), PRIMED + 16 * n_out)
                        pool.wait_ge(s("S_free"), PRIMED + Turn(l, 14).use("S"))
                    for t, choice in gathers[:n]:
                        if t >= GATHERS and choice == 0:
                            pool.wait_ge(sem(f"fetched{t % GATHERS}"), fetched(l, t - GATHERS))
                        dst = XN[:, t, :] if choice == 0 else XT[:, t * P:(t + 1) * P]
                        pool.indirect_dma_start(
                            dst, None, YS, bass.IndirectOffsetOnAxis(ap=slot[:, choice, t:t + 1], axis=0))\
                            .then_inc(sem(f"fetched{t % GATHERS}"), 16)
                    del gathers[:n]

                if l in SORTED:
                    if l == 0:
                        pool.wait_ge(sem("places_zeroed"), 16 * -(-MAXBLOCKS // NT))
                    pool.wait_ge(sem("places_ready"), 1 + SORTED.index(l))
                run_turns(pool, l, take_turn)
                if l in SORTED:
                    gather(NT * TOPK[l])

        @block.vector
        def _(dve):
            chain = Chain(dve, sem("dve_chain"))
            dve.memset(wb[:, :, :], 0.0).then_inc(sem("zeroed"), 1)
            chain.link(dve.memset(va[:, :, 0, :, :, DH:DH + 1], 1.0))
            chain.link(dve.memset(va[:, :, 1, :, :, DH:DH + 1], 0.0))
            chain.link(dve.memset(mx[:, :, :, :], 0.0))
            chain.link(dve.memset(GA[:, :, :], 0.0))
            chain.link(dve.memset(gst[:, :, :, :], 0.0))
            dve.wait_ge(sem("ld_x"), full["ld_x"])

            def phase_a(l):
                s = lambda n: sem(f"L{l}_{n}")
                if l == 0:
                    combine(l, {}, {}, range(NT + 2), gathered=False)
                with dve.Fori(0, NT // 4 // 2) as turn:
                    i = turn * 2
                    for par in range(2):
                        dve.wait_ge(sem("turned"), PRIMED + l * (NT // 4) + i)
                        dve.wait_ge(sem("rstd"), PRIMED + l * (NT // 4) + i + par + 1)
                        for u in range(4):
                            t = (i + par) * 4 + u
                            ins = dve.tensor_scalar(xn[:, par, u, :], X[:, t, :], MV[:, t, 0:1],
                                                    rstd[:, bass.ds(t, 1)], ALU.subtract, ALU.mult)
                        ins.then_inc(sem("xn_ready"), 1)
                        if l in SORTED:
                            for u in range(4):
                                t = (i + par) * 4 + u
                                dve.tensor_scalar(XN[:, t, :], X[:, t, :], MV[:, t, 0:1],
                                                  rstd[:, bass.ds(t, 1)], ALU.subtract, ALU.mult)\
                                   .then_inc(sem("xn_kept"), 1)

            def routing(l):
                s = lambda n: sem(f"L{l}_{n}")
                n = EXPERTS[l]
                full_e = lambda a: a[:, :, None].to_broadcast([P, NT, n])
                lg, p_, a_, b_, c_, g_, k_ = (x[:, :, 0:n] for x in (LG, pr, ra, rb, rc, GA, rank))
                dve.wait_ge(sem(f"ld_{l}"), full[f"ld_{l}"])
                dve.wait_ge(sem("logits_copied"), PRIMED + l * (NT // 4) + NT // 4)
                if l > 0:
                    chain.link(dve.tensor_tensor(lg, lg, br[l][:, None, :].to_broadcast([P, NT, n]), ALU.add))
                chain.link(dve.tensor_reduce(r1[:, :], lg, AX.X, ALU.max))
                dve.tensor_tensor(a_, lg, full_e(r1), ALU.subtract).then_inc(sem("shifted"), 1)
                dve.wait_ge(sem("exp_logits"), PRIMED + l + 1)
                chain.link(dve.tensor_reduce(r1[:, :], p_, AX.X, ALU.add))
                chain.link(dve.reciprocal(r2[:, :], r1[:, :]))
                chain.link(dve.tensor_tensor(p_, p_, full_e(r2), ALU.mult))
                for k in range(TOPK[l]):
                    chain.link(dve.tensor_reduce(r1[:, :], p_, AX.X, ALU.max))
                    chain.link(dve.tensor_tensor(a_, p_, full_e(r1), ALU.is_ge))
                    chain.link(dve.tensor_tensor(a_, a_, k_, ALU.mult))
                    chain.link(dve.tensor_reduce(r2[:, :], a_, AX.X, ALU.max))
                    chain.link(dve.tensor_tensor(b_, k_, full_e(r2), ALU.is_equal))
                    if l in SORTED:
                        chain.link(dve.tensor_copy(oh[:, k, :, :], b_.rearrange("p t e -> p e t")))
                        chain.link(dve.tensor_copy(gk[:, k, :], r1[:, :]))
                    if k == 0:
                        chain.link(dve.tensor_tensor(g_, p_, b_, ALU.mult))
                    else:
                        chain.link(dve.tensor_tensor(c_, p_, b_, ALU.mult))
                        chain.link(dve.tensor_tensor(g_, g_, c_, ALU.add))
                    if k < TOPK[l] - 1 or l == 0:
                        chain.link(dve.scalar_tensor_tensor(p_, b_, -2.0, p_, ALU.mult, ALU.add))
                if l == 1:
                    chain.link(dve.memset(GA[:, :, 15:16], 1.0))
                if l == 0:
                    start_search()
                if l in SORTED:
                    places(l)
                dve.sem_inc(sem("gates"), 1)

            e_t = lambda a: a[:, :, None].to_broadcast([P, 8, NT])
            flat = lambda a: a.rearrange("p e t -> p (e t)")
            wide_rb = rb[:, :, :].rearrange("p t e -> p (t e)")[:, 0:8 * NT].rearrange("p (e t) -> p e t", e=8)
            wide_rc = rc[:, :, :].rearrange("p t e -> p (t e)")[:, 0:8 * NT].rearrange("p (e t) -> p e t", e=8)

            def places(l):
                if TOPK[l] == 2:
                    ins = dve.tensor_tensor(wide_rb, oh[:, 0, :, :], oh[:, 1, :, :], ALU.add)
                else:
                    ins = dve.tensor_copy(wide_rb, oh[:, 0, :, :])
                ins.then_inc(sem("chosen"), 1)
                dve.wait_ge(sem("ranked"), 1 + SORTED.index(l))
                before_and_total(pS[:, 1, :])
                chain.link(dve.tensor_tensor(nblk[:, :], scan[:, :, NT - 1], wide_rc[:, :, NT - 1], ALU.add))
                chain.link(dve.tensor_scalar(nblk[:, :], nblk[:, :], float(P - 1), None, ALU.add))
                chain.link(dve.tensor_copy(nblki[:, :], nblk[:, :]))
                chain.link(dve.tensor_scalar(nblki[:, :], nblki[:, :], 7, None, ALU.arith_shift_right))
                chain.link(dve.tensor_copy(nblk[:, :], nblki[:, :]))
                chain.link(dve.tensor_tensor_scan(nend[:, :], onesm[:, 0:8], nblk[:, :], 0.0, ALU.mult, ALU.add))
                chain.link(dve.tensor_tensor(cmpb[:, :, :], nend[:, None, :].to_broadcast([P, MAXBLOCKS, 8]),
                                             blockno[:, :, None].to_broadcast([P, MAXBLOCKS, 8]), ALU.is_le))
                chain.link(dve.tensor_reduce(ebf[:, :], cmpb[:, :, :], AX.X, ALU.add))
                chain.link(dve.tensor_scalar(ebf[:, :], ebf[:, :], float(EXPERTS[l] - 1), None, ALU.min))
                chain.link(dve.tensor_copy(eb[:, :], ebf[:, :]))
                chain.link(dve.tensor_tensor(nblk[:, :], nend[:, :], nblk[:, :], ALU.subtract))
                chain.link(dve.tensor_scalar(nblk[:, :], nblk[:, :], float(P), None, ALU.mult))
                chain.link(dve.tensor_tensor(place[:, :, :], scan[:, :, :], e_t(nblk[:, :]), ALU.add))
                chain.link(dve.tensor_tensor(flat(place), flat(place), pS[:, 0, 0:8 * NT], ALU.add))
                for k in range(TOPK[l]):
                    chain.link(dve.tensor_tensor(key_tmp, oh[:, k, :, :], place[:, :, :], ALU.mult))
                    chain.link(dve.tensor_reduce(slotf[:, k, :], key_tmp.rearrange("p e t -> p t e"), AX.X, ALU.add))
                    chain.link(dve.tensor_copy(slot[:, k, :], slotf[:, k, :]))
                dve.wait_ge(sem("xn_kept"), NT * (1 + SORTED.index(l)))
                dve.sem_inc(sem("places_ready"), 1)

            key_tmp = wide_rb

            def before_and_total(bank):
                chain.link(dve.tensor_copy(flat(wide_rc), bank[:, 0:8 * NT]))
                for e in range(8):
                    m = chain.mark(dve.tensor_tensor_scan(scan[:, e, :], onesm[:, 0:NT], wide_rc[:, e, :], 0.0,
                                                          ALU.mult, ALU.add))
                chain.wait(m)
                chain.link(dve.tensor_tensor(flat(scan), flat(scan), flat(wide_rc), ALU.subtract))

            def start_search():
                g_ = GA[:, :, 0:8].rearrange("p t e -> p e t")
                p_ = pr[:, :, 0:8].rearrange("p t e -> p e t")
                chain.link(dve.tensor_scalar(key[:, :, :], p_, 0.0, None, ALU.is_ge))
                chain.link(dve.tensor_tensor(key[:, :, :], g_, key[:, :, :], ALU.subtract))
                chain.link(dve.memset(thr[:, :], 0))
                chain.link(dve.tensor_copy(biti[:, :], bitf[:, :]))
                for part in count_parts(chain):
                    m = part()
                    if isinstance(m, int):
                        chain.wait(m)

            def search_parts(c):
                return [
                    lambda bank: c.mark(dve.scalar_tensor_tensor(addb[:, :], bank[:, 0:8], float(CAP), bitf[:, :],
                                                                 ALU.is_ge, ALU.mult)),
                    lambda: c.mark(dve.tensor_tensor(thr[:, :], thr[:, :], addb[:, :], ALU.bitwise_or)),
                    lambda: c.mark(dve.tensor_scalar(bitf[:, :], bitf[:, :], 0.5, None, ALU.mult)),
                    lambda: c.mark(dve.tensor_copy(biti[:, :], bitf[:, :])),
                ] + count_parts(c)

            def count_parts(c):
                return [
                    lambda: c.mark(dve.tensor_tensor(cand[:, :], thr[:, :], biti[:, :], ALU.bitwise_or)),
                    lambda: c.mark(dve.tensor_tensor(cmp_[:, :, :], key[:, :, :], e_t(cand[:, :].bitcast(F32)), ALU.is_ge)),
                    lambda: dve.tensor_reduce(cnt[:, :], cmp_[:, :, :], AX.X, ALU.add).then_inc(sem("counted"), 1),
                ]

            def search(turn, tc, k, bank, s):
                parts = search_parts(tc)
                if bank is not None:
                    searched[:] = [parts[0](bank)]
                    tc.wait(searched[0])
                    dve.sem_inc(s("S_free"), 1)
                    return
                for part in {1: (1, 2), 2: (3,), 3: (4,), 4: (5,), 5: (6,)}[k]:
                    if part != 2:
                        tc.wait(searched[-1])
                    searched.append(parts[part]())

            searched = []

            def above_capacity():
                dve.wait_ge(sem("counted"), PRIMED + SEARCH_BITS + 1)
                chain.link(dve.tensor_tensor(keep[:, :, :], key[:, :, :], e_t(thr[:, :].bitcast(F32)), ALU.is_gt))
                dve.tensor_reduce(cnt[:, :], keep[:, :, :], AX.X, ALU.add).then_inc(sem("counted"), 1)

            def cut_to_capacity(k, bank, s):
                before = wide_rb
                if k == 0:
                    chain.link(dve.tensor_scalar(left[:, :], bank[:, 0:8], -1.0, float(CAP), ALU.mult, ALU.add))
                    dve.sem_inc(s("S_free"), 1)
                    dve.tensor_tensor(cmp_[:, :, :], key[:, :, :], e_t(thr[:, :].bitcast(F32)), ALU.is_equal)\
                       .then_inc(sem("counted"), 1)
                elif k == 1:
                    dve.tensor_copy(flat(before), bank[:, 0:8 * NT]).then_inc(s("S_free"), 1)
                else:
                    before_and_total(bank)
                    dve.sem_inc(s("S_free"), 1)
                    chain.link(dve.tensor_tensor(before, before, scan[:, :, :], ALU.add))
                    chain.link(dve.tensor_tensor(before, before, e_t(left[:, :]), ALU.is_lt))
                    chain.link(dve.tensor_tensor(before, before, cmp_[:, :, :], ALU.mult))
                    chain.link(dve.tensor_tensor(keep[:, :, :], keep[:, :, :], before, ALU.add))
                    for choice in range(TOPK[0]):
                        chain.link(dve.tensor_tensor(before, oh[:, choice, :, :], keep[:, :, :], ALU.mult))
                        chain.link(dve.tensor_reduce(slotf[:, choice, :], before.rearrange("p e t -> p t e"), AX.X,
                                                     ALU.add))
                        chain.link(dve.tensor_tensor(gk[:, choice, :], gk[:, choice, :], slotf[:, choice, :],
                                                     ALU.mult))

            def combine(l, final, stats, tiles, gathered=True):
                for t in tiles:
                    if t < NT and gathered:
                        dve.wait_ge(sem(f"fetched{t % GATHERS}"), fetched(l, t))
                        for choice in range(TOPK[l]):
                            if choice:
                                chain.wait(final[t])
                            src = XN[:, t, :] if choice == 0 else XT[:, t * P:(t + 1) * P]
                            final[t] = chain.mark(dve.scalar_tensor_tensor(
                                X[:, t, :], src, gk[:, choice, t:t + 1], X[:, t, :], ALU.mult, ALU.add))
                    if 1 <= t <= NT:
                        if gathered:
                            chain.wait(final[t - 1])
                        stats[t - 1] = chain.mark(dve.bn_stats(st6[:, (t - 1) % 4, :], X[:, t - 1, :]))
                    if t >= 2:
                        chain.wait(stats[t - 2])
                        last = chain.mark(dve.bn_aggr(MV[:, t - 2, :], st6[:, (t - 2) % 4, :]))
                        if (t - 2) % 4 == 3:
                            chain.wait(last)
                            dve.sem_inc(sem("stats"), 1)

            def take_turn(turn, tc):
                l, par, nxt = turn.layer, turn.par, 1 - turn.par
                s = lambda n: sem(f"L{l}_{n}")
                use_s, use_h, use_y, use_o = (turn.use(r) for r in "SHYO")
                tc.enter(turn)
                xt = lambda c: X[:, turn.count(2, c), :]
                x2 = X[:, bass.ds(turn.count(2, 0), 2), :] if 0 <= turn.n < B else None
                both = lambda a: a.rearrange("p (c e) -> p c e", c=2)
                last_x = [None, None, None]

                def before_x(c=None):
                    m = last_x[2 if c is None else c]
                    if m is not None:
                        tc.wait(m)

                def wrote_x(ins):
                    last_x[:] = [tc.mark(ins)] * 3

                for kind, k, local in turn.steps:
                    if RING.get(kind) == "S":
                        bank = pS[:, local % 2, :]
                        dve.wait_ge(s("S_full"), PRIMED + use_s + local + 1)
                    elif RING.get(kind) == "Y":
                        yb = y_bank(l, local)
                        dve.wait_ge(s("Y_full"), PRIMED + use_y + local + 1)

                    if kind == "P":
                        dve.wait_ge(s("qk_split"), PRIMED + turn.row(2))
                        side = slice(k * T, (k + 1) * T)
                        if l == 0:
                            for half in range(2):
                                ins = dve.scalar_tensor_tensor(
                                    qkf[:, half, side], bank[:, half * T:(half + 1) * T],
                                    bq0[:, 2 * k + half:2 * k + half + 1], rope0[:, 2 * k + half, :],
                                    ALU.add, ALU.mult)
                        else:
                            for to in (qkf[:, 0, side], qk16[:, 0, side]):
                                if l == 2:
                                    ins = dve.tensor_scalar(to, bank[:, 0:T],
                                                            rope2[:, k, bass.ds(turn.row(2), 1)], None, ALU.mult)
                                else:
                                    ins = dve.tensor_scalar(to, bank[:, 0:T], bq3[:, k:k + 1],
                                                            QSCALE if k == 0 else 1.0, ALU.add, ALU.mult)
                        ins.then_inc(s("S_free"), 1)
                    elif kind == "V":
                        dve.wait_ge(s("v_split"), PRIMED + turn.row(1))
                        if l == 2:
                            ins = dve.tensor_copy(v32[:, k, :], bank[:, 0:P])
                        else:
                            ins = dve.tensor_tensor(v32[:, k, :], bank[:, 0:P], (bv0 if l == 0 else bv3)[:, :], ALU.add)
                        ins.then_inc(s("S_free"), 1)
                    elif kind == "D":
                        if k in HIGH_BY_VECTOR[l]:
                            n = 3 * P if l == 3 else 2 * T
                            dve.wait_ge(s("T_free"), PRIMED + turn.use("T") + used_at(turn, "T", k) + 1)
                            ins = dve.tensor_copy(pe16[:, 0, k % 4, 0:n], pe32[:, k % 4, 0:n]).then_inc(s("high"), 1)
                            if split_by(turn, k)[0] == "dve":
                                dve.wait_ge(s("high"), PRIMED + high_made(turn, k))
                        if split_by(turn, k)[0] == "dve":
                            split_exp(dve, turn, k)
                        if l in SORTED and turn.n == B - 1:
                            n_add = TILES_A_HEAD[l]
                            combine(l, final, stats, [t for t in range(n_add * k, n_add * (k + 1)) if t < 2 * (B - 2)])
                    elif kind == "S":
                        j, col = k // NG, 32 * (k % NG) + MAXROW
                        if l == 3:
                            dve.tensor_reduce(mx[:, 0, j, col:col + 1], bank[:, 0:P], AX.X, ALU.max)
                            ins = dve.tensor_reduce(mx[:, 1, j, col:col + 1], bank[:, P:P + T], AX.X, ALU.max)
                        else:
                            ins = dve.tensor_reduce(mx[:, :, j, col], bank.rearrange("p (c n) -> p c n", c=2),
                                                    AX.X, ALU.max)
                        ins.then_inc(s("S_free"), 1)
                    elif kind == "M":
                        q = stk[:, nxt, :, k * P:(k + 1) * P]
                        dve.scalar_tensor_tensor(q, bank.rearrange("p (j n) -> p j n", j=NJ), -1.0, q,
                                                 ALU.mult, ALU.add).then_inc(s("S_free"), 1)
                    elif kind == "u":
                        above_capacity()
                    elif kind == "U":
                        cut_to_capacity(k, bank, s)
                    elif kind == "C":
                        search(turn, tc, 0, bank, s)
                    elif kind == "c":
                        search(turn, tc, k % 10, None, s)
                    elif kind == "Y" and l in SORTED:
                        place_, nth = place_in(turn, k)
                        dve.wait_ge(sem(f"ys_out{place_}"), PRIMED - 16 + tokens_in(turn, nth))
                        dve.tensor_copy(ysb[:, place_, :], yb[:, 0:P]).then_inc(s("Y_free"), 1)
                    elif kind == "G":
                        dve.tensor_copy(gt[:, :], yb[0:16, 0:T]).then_inc(s("Y_free"), 1)
                    elif kind == "B":
                        wrote_x(dve.tensor_tensor(x2, x2, both(yb[:, 0:2 * P]), ALU.add))
                        before_x()
                        dve.sem_inc(s("Y_free"), 1)
                    elif kind == "Y":
                        if l == 3:
                            before_x()
                            wrote_x(dve.tensor_tensor(x2, x2, both(yb[:, 0:2 * P]), ALU.add))
                        else:
                            if k == 0:
                                dve.wait_ge(s("row_staged"), PRIMED + turn.row(1))
                            for half in range(2):
                                e = 2 * k + half
                                for c in range(2):
                                    o = half * T + c * P
                                    before_x(c)
                                    last_x[c] = last_x[2] = tc.mark(dve.scalar_tensor_tensor(
                                        xt(c), yb[:, o:o + P], gst[:, par, c, e:e + 1], xt(c), ALU.mult, ALU.add))
                        before_x()
                        dve.sem_inc(s("Y_free"), 1)
                    elif kind == "H" and l == 3:
                        dve.wait_ge(s("tanh_done"), PRIMED + use_h + local + 1)
                        dve.wait_ge(s("Y_full"), PRIMED + use_y)
                        tc.link(dve.scalar_tensor_tensor(hg[:, k % 2, :], th[:, k % 2, :], 1.0, pH[:, k % 2, 0:T],
                                                         ALU.add, ALU.mult))
                        dve.scalar_tensor_tensor(hb[:, k, 0:T], hg[:, k % 2, :], 0.5, pH[:, k % 2, T:2 * T],
                                                 ALU.mult, ALU.mult).then_inc(s("H_free"), 1)
                    elif kind == "R":
                        tc.link(dve.tensor_scalar(vals[:, :], bank[:, 0:T], bb1[:, 0:1], oml[:, 0:1],
                                                  ALU.add, ALU.mult))
                        dve.sem_inc(s("S_free"), 1)
                        dve.tensor_tensor_scan(hT[:, :], lamrow[:, :], vals[:, :], 0.0, ALU.mult, ALU.add)\
                           .then_inc(s("scanned"), 1)
                    elif kind == "Z":
                        z_bank = bank
                        for c in range(2):
                            m = tc.mark(dve.bn_stats(zs[:, c, :], z_bank[:, c * P:(c + 1) * P]))
                        tc.wait(m)
                        settle(dve, sem("dve_settled"))
                        for c in range(2):
                            m = tc.mark(dve.bn_aggr(zmv[:, c, :], zs[:, c, :]))
                        tc.wait(m)
                        dve.sem_inc(s("z_stats"), 1)
                    elif kind == "N" and l == 1:
                        dve.wait_ge(s("z_rstd"), PRIMED + turn.row(1))
                        for c in range(2):
                            m = tc.mark(dve.tensor_scalar(zn[:, c, :], z_bank[:, c * P:(c + 1) * P],
                                                          zmv[:, c, 0:1], zr[:, c:c + 1], ALU.subtract, ALU.mult))
                        tc.wait(m)
                        dve.sem_inc(s("S_free"), 1)
                        dve.sem_inc(s("z_normal"), 1)
                    elif kind == "A":
                        dve.wait_ge(s("z_done"), PRIMED + turn.row(1))
                        before_x()
                        wrote_x(dve.tensor_tensor(x2, x2, zg[:, 1, :, :], ALU.add))
                    elif kind == "N":
                        dve.wait_ge(s("O_full"), PRIMED + use_o + H)
                        tc.link(dve.reciprocal(rden[:, :, :], po[:, :, :, DH]))
                        for c in range(2):
                            m = tc.mark(dve.tensor_tensor(ob[:, c, :].rearrange("p (h e) -> p h e", h=H),
                                                          po[:, c, :, 0:DH],
                                                          rden[:, c, :, None].to_broadcast([P, H, DH]), ALU.mult))
                        tc.wait(m)
                        dve.sem_inc(s("out_read"), 1)
                        before_x()
                        add = bp3[:, None, :].to_broadcast([P, 2, P]) if l == 3 else ob[:, :, :]
                        wrote_x(dve.tensor_tensor(x2, x2, add, ALU.add))
                    elif kind == "W":
                        xb = X[:, bass.ds(turn.count(2, -2), 2), :]
                        tc.link(dve.tensor_tensor(xb, xb, both(yb[:, 0:2 * P]), ALU.add))
                        dve.sem_inc(s("Y_free"), 1)
                        dve.sem_inc(s("x_final"), 1)
                    elif kind == "E":
                        before_x()
                        if l != 3:
                            dve.sem_inc(s("x_final"), 1)
                        if l == 1:
                            settle(dve, sem("dve_settled"))
                            for c in range(2):
                                m = tc.mark(dve.bn_stats(st6[:, c, :], xt(c)))
                            tc.wait(m)
                            settle(dve, sem("dve_settled"))
                            for c in range(2):
                                m = tc.mark(dve.bn_aggr(mv4[:, c, :], st6[:, c, :]))
                            tc.wait(m)
                            settle(dve, sem("dve_settled"))
                            m = tc.mark(dve.tensor_copy(MV[:, bass.ds(turn.count(2, 0), 2), :], mv4[:, 0:2, :]))
                            if turn.n == B - 1:
                                tc.wait(m)
                                dve.sem_inc(sem("stats"), NT // 4)
                tc.leave()

            for l in range(4):
                phase_a(l)
                if l == 0:
                    dve.wait_ge(sem("ld_cst"), full["ld_cst"])
                if l < 3:
                    routing(l)
                if l == 1:
                    dve.wait_ge(sem("lam_tanh"), 1)
                    chain.link(dve.tensor_scalar(lam1[:, :], lamt[:, :], 0.5, 0.5, ALU.mult, ALU.add))
                    chain.link(dve.tensor_scalar(oml[:, :], lamt[:, :], -0.5, 0.5, ALU.mult, ALU.add))
                    chain.link(dve.tensor_copy(lamrow[:, :], lam1[:, :].to_broadcast([P, T])))
                final, stats = {}, {}
                tc = TurnChain(dve, sem(f"L{l}_dve_chain"))
                run_turns(dve, l, lambda turn: take_turn(turn, tc))
                dve.wait_ge(sem(f"L{l}_x_final"), PRIMED + B)
                if l in SORTED:
                    combine(l, final, stats, range(min(TILES_A_HEAD[l] * H, 2 * (B - 2)), NT + 2))

        primed = [n for n in sems if n in SHARED_SIGNALS or (n.startswith("L") and not n.endswith("_chain"))]

        @block.sync
        def _(sp):
            def load(l, ring, k):
                e = sp.value_load(eb[0:1, bass.ds(k, 1)], min_val=0, max_val=EXPERTS[l] - 1)
                sp.dma_start(wb[:, ring, :], d[f"w_{l}"][bass.ds(e, 1), :, :].rearrange("e p n -> (e p) n"))\
                  .then_inc(sem(f"w_in{ring}"), 16)
                if l == 2:
                    sp.dma_start(wb2[:, ring, :], d["b2_2"][bass.ds(e, 1), :]).then_inc(sem(f"w_in{ring}"), 16)
                sp.dma_start(xsb[:, ring, :], XS[bass.ts(k, P), :]).then_inc(sem(f"xs_in{ring}"), 16)

            def store(l, ring, k):
                sp.wait_ge(sem(f"L{l}_Y_free"), PRIMED + k + 1)
                sp.dma_start(YS[bass.ts(k, P), :], ysb[:, ring, :]).then_inc(sem(f"ys_out{ring}"), 16)

            def blocks_in_and_out(sp, l):
                nb, ring = BLOCKS[l], IN_FLIGHT[l]
                sp.wait_ge(sem("sorted_out"), 16 * NT * sum(TOPK[m] for m in SORTED if m <= l))
                for k in range(ring):
                    load(l, k, k)
                with sp.Fori(0, nb // ring - 1) as g:
                    for k in range(ring):
                        sp.wait_ge(sem(f"L{l}_Y_full"), PRIMED + (g * ring + (k + 1)))
                        load(l, k, g * ring + (k + ring))
                        store(l, k, g * ring + k)
                for k in range(nb - ring, nb):
                    store(l, k % ring, k)

            for name in primed:
                sp.sem_inc(sem(name), PRIMED)
            for group, moves in loads.items():
                for dst, src in moves:
                    sp.dma_start(dst, src).then_inc(sem(group), 16)
            sp.wait_ge(sem("zeroed"), 1)
            for c in range(0, MAXBLOCKS, NT):
                n = min(NT, MAXBLOCKS - c)
                sp.dma_start(XS[c * P:(c + n) * P, :].rearrange("(t p) e -> p t e", p=P),
                             wb[:, :, :].rearrange("p r n -> p (r n)")[:, 0:n * P].rearrange("p (t e) -> p t e", e=P))\
                  .then_inc(sem("places_zeroed"), 16)
            for l in SORTED:
                blocks_in_and_out(sp, l)
            for c in range(4):
                sp.wait_ge(sem("L3_x_final"), PRIMED + 4 * c + 4)
                sp.dma_start(xout[:, 8 * c:8 * c + 8, :], X[:, 8 * c:8 * c + 8, :]).then_inc(sem("stored"), 16)
            sp.wait_ge(sem("stored"), 64)


def shape_constants():
    c = {}
    f = np.float32
    c["c_ident"] = np.eye(P, dtype=f)
    c["c_ones"] = np.ones((P, P), f)
    c["c_tri"] = np.triu(np.ones((P, P), f), 1)
    c["c_rank"] = np.broadcast_to(16.0 - np.arange(16, dtype=f), (P, NT, 16)).copy()
    c["c_blockno"] = np.broadcast_to(np.arange(MAXBLOCKS, dtype=f), (P, MAXBLOCKS)).copy()
    c["c_bitf"] = np.full((P, 8), 2.0 ** (SEARCH_BITS - 1), f)
    sel = np.zeros((P, 4, NJ, P), np.float16)
    for j in range(NJ):
        for g in range(NG):
            for e in range(DH):
                src = (NG * j + g) * DH + e
                for which, rs in ((0, (0, 1)), (1, (2,)), (2, (0, 2)), (3, (1,))):
                    for r in rs:
                        sel[src, which, j, 32 * g + DH * r + e] = 1
    c["c_selq"] = sel
    one = np.zeros((2, P), np.float16)
    one[0, MAXROW::32] = 1
    c["c_onecol"] = one
    al = np.zeros((2, 2, NJ, P), np.float16)
    for j in range(NJ):
        for g in range(NG):
            slope = 2.0 ** -(NG * j + g + 1)
            al[0, 0, j, 32 * g + 24] = slope * 256
            al[1, 1, j, 32 * g + 24] = 1
            al[1, 0, j, 32 * g + 25] = 1
            al[0, 1, j, 32 * g + 25] = -slope * 256
    al[0, 1, :, MAXROW::32] = 1
    c["c_alcol"] = al
    c["c_alrow"] = np.stack([np.ones(T), np.arange(T) / 256.0]).astype(np.float16)
    m = np.where(np.arange(P)[None, :] > np.arange(P)[:, None], -1e30, 0.0).astype(f)
    c["c_mask"] = np.stack([m, m.T], axis=1)
    c["c_identb"] = np.eye(P, dtype=f)
    freqs = (f(1.0) / np.power(f(10000.0), np.arange(0, DH, 2, dtype=f) / f(DH))).astype(f)
    ang = np.arange(T, dtype=f)[:, None] * freqs[None, :]
    cos, sin = np.cos(ang).astype(f), np.sin(ang).astype(f)
    e = np.arange(P) % DH
    cs = cos[:, e // 2].T
    sn = (sin[:, e // 2] * np.where(e % 2 == 0, -1.0, 1.0).astype(f)).T
    c["c_rope0"] = np.stack([cs * f(QSCALE), sn * f(QSCALE), cs, sn], axis=1).astype(f)
    ang2 = np.arange(B, dtype=f)[:, None] * freqs[None, :]
    ang2 = np.concatenate([ang2, ang2], axis=-1)
    r2 = np.cos(ang2) + np.sin(ang2) * np.where(np.arange(DH) < DH // 2, 1.0, -1.0)
    r2 = r2[:, e].T.astype(f)
    c["c_rope2"] = np.stack([r2 * f(QSCALE), r2], axis=1).astype(f)
    return {k: np.ascontiguousarray(v) for k, v in c.items()}


def lay_out(i):
    a = {k: np.asarray(v) for k, v in i.items()}
    o = {}
    swap = np.arange(P) ^ 1
    o["x"] = a["L0_attn_x"].reshape(B * T, P)
    wt = a["L0_attn_W_qkv"].T
    q, k, v = wt[:, 0:P], wt[:, P:2 * P], wt[:, 2 * P:]
    o["wq0"] = np.stack([q, q[:, swap], k, k[:, swap], v], axis=1)
    bq, bk = a["L0_attn_b_qkv"][0:P], a["L0_attn_b_qkv"][P:2 * P]
    o["bq0"] = np.stack([bq, bq[swap], bk, bk[swap]], axis=1)
    o["bv0"] = a["L0_attn_b_qkv"][2 * P:]
    o["wr0"] = a["L0_ffn_Wr"]
    w2 = lambda w: w.reshape(8, NF, P, P).transpose(0, 2, 1, 3).reshape(8, P, FF)
    unused = np.zeros((8, P, NF), np.float32)
    o["w_0"] = np.concatenate([a["L0_ffn_W1"], w2(a["L0_ffn_W2"]), unused], axis=2)
    o["wr1"], o["br1"] = a["L1_ffn_router_W"], a["L1_ffn_router_b"]
    o["w1_1"] = np.concatenate([a["L1_ffn_eW1"], a["L1_ffn_sW1"][None]]).transpose(1, 0, 2)
    o["w2_1"] = np.concatenate([a["L1_ffn_eW2"], a["L1_ffn_sW2"][None]]).transpose(1, 0, 2)
    o["b1_1"] = np.concatenate([a["L1_ffn_eb1"], a["L1_ffn_sb1"][None]]).T
    o["b2_1"] = np.concatenate([a["L1_ffn_eb2"], a["L1_ffn_sb2"][None]])
    o["wb1"], o["wc1"] = a["L1_attn_Wb"].T, a["L1_attn_Wc"].T
    o["bb1"], o["bc1"] = a["L1_attn_bb"].reshape(P, 1), a["L1_attn_bc"].reshape(1, P)
    o["gam1"], o["bet1"] = a["L1_attn_gamma"], a["L1_attn_beta"]
    o["llr1"] = a["L1_attn_log_lambda_raw"].reshape(P, 1)
    o["wq2"] = np.stack([a["L2_attn_Wq"].T, a["L2_attn_Wk"].T, a["L2_attn_Wv"].T], axis=1)
    o["wr2"], o["br2"] = a["L2_ffn_Wr"], a["L2_ffn_br"]
    b1 = a["L2_ffn_b1"].reshape(8, NF, P).transpose(0, 2, 1)
    o["w_2"] = np.concatenate([a["L2_ffn_W1"], w2(a["L2_ffn_W2"]), b1], axis=2)
    o["b2_2"] = a["L2_ffn_b2"]
    o["wq3"] = a["L3_attn_W_attn"].reshape(P, 3, P)
    o["bq3"] = a["L3_attn_b_attn"][0:2 * P].reshape(2, P).T
    o["bv3"] = a["L3_attn_b_attn"][2 * P:]
    o["wp3"], o["bp3"] = a["L3_attn_W_proj"], a["L3_attn_b_proj"]
    down = a["L3_ffn_w_down"].T.reshape(NHC, P, P).transpose(1, 0, 2).reshape(P, HID)
    o["wi3"] = np.stack([a["L3_ffn_w_gate"].T, a["L3_ffn_w_up"].T, down], axis=1)
    return {k: np.ascontiguousarray(v) for k, v in o.items()}


def kernel(**inputs):
    import ml_dtypes as _ml
    import concourse.bacc as _bacc
    from concourse.bass_utils import run_bass_kernel_spmd as _run

    nc = _bacc.Bacc("TRN2", target_bir_lowering=False, num_devices=1)
    consts = shape_constants()
    for name in ("c_mask", "c_identb"):
        consts[name] = consts[name].astype(_ml.bfloat16)
    arrays = {**lay_out(inputs), **consts}
    d = {name: nc.dram_tensor("in_" + name, list(v.shape), mybir.dt.from_np(v.dtype), kind="ExternalInput").ap()
         for name, v in arrays.items()}
    out = nc.dram_tensor("out", [B, T, P], F32, kind="ExternalOutput").ap()
    build(nc, d, out)
    r = _run(nc, [{"in_" + name: v for name, v in arrays.items()}], core_ids=[0])
    return r.results[0]["out"]
```
